# Optimizing a Trainium2 kernel written in Bass

```python
import numpy as np
import jax
import jax.numpy as jnp

def _softmax(x, axis=-1):
    return jax.nn.softmax(x, axis=axis)

def _gelu(x):
    return jax.nn.gelu(x, approximate=True)

def _silu(x):
    return jax.nn.silu(x)

def _sigmoid(x):
    return jax.nn.sigmoid(x)

def _layernorm(x, axis=-1, eps=1e-05):
    m = jnp.mean(x, axis=axis, keepdims=True)
    v = jnp.var(x, axis=axis, keepdims=True)
    return (x - m) / jnp.sqrt(v + eps)

def _scatter_add(tgt, idx, src, axis=0):
    return tgt.at[idx].add(src)

def _segment_sum(src, seg, n):
    return jax.ops.segment_sum(src, seg, n)
kernel_name = 'mk_flamingo_gated_d2_seqx_r4_ceb8f5'

def setup_inputs(seed: int=0):
    np.random.seed(seed)
    _w = jnp.asarray

    def _rec_inputs():
        import jax
        import jax.numpy as jnp
        _rk = jax.random.key(seed)
        x = -0.0002928 + 1 * jax.random.normal(jax.random.fold_in(_rk, 1), (32, 256, 256), jnp.float32)
        _lenS = 256 - jax.random.randint(jax.random.fold_in(_rk, 7), (32,), 0, max(1, 256 // 4) + 1, jnp.int32)
        _lenS2 = 77 - jax.random.randint(jax.random.fold_in(_rk, 8), (32,), 0, max(1, 77 // 4) + 1, jnp.int32)
        _ctx_1024P = jax.random.normal(jax.random.fold_in(_rk, 11), (32, 16, 256), jnp.float32)
        _ctx_1024c = jax.random.dirichlet(jax.random.fold_in(_rk, 511), 0.3 * jnp.ones((16,), jnp.float32), (32, 77))
        _ctx_1024t = jnp.einsum('bsk,bkd->bsd', _ctx_1024c, _ctx_1024P)
        _ctx_1024t = _ctx_1024t * jax.lax.rsqrt(jnp.mean(jnp.square(_ctx_1024t)) + 1e-12) * 0.953939
        ctx_1024 = -1.39393e-06 + 0.999914 * (_ctx_1024t + 0.3 * jax.random.normal(jax.random.fold_in(_rk, 611), (32, 77, 256), jnp.float32))
        _validS = jnp.arange(256)[None, :] < _lenS[:, None]
        _validS2 = jnp.arange(77)[None, :] < _lenS2[:, None]
        _causal = jnp.tril(jnp.ones((256, 256), dtype=bool))
        mask_Bx1x1xS2_if1 = jnp.where(jnp.ones((32, 1, 1, 77), dtype=bool), 1, 0).astype(jnp.int32)
        _g = jax.random.normal(jax.random.fold_in(_rk, 9001), (2, 2), jnp.float32)
        _g = jnp.sign(_g) * jnp.maximum(jnp.abs(_g), 1.0) + (_g == 0) * 1.0
        g_xattn = _g[0]
        g_ffn = _g[1]
        return (x, ctx_1024, mask_Bx1x1xS2_if1, g_xattn, g_ffn)
    x, ctx_1024, mask_Bx1x1xS2_if1, g_xattn, g_ffn = _rec_inputs()

    def _L0_xattn_setup():
        import jax, jax.numpy as jnp
        import numpy as np
        D_MODEL = 256
        N_HEADS = 16
        D_K = D_MODEL // N_HEADS
        NEG = -1000000000.0

        def _split_heads(x):
            B, S, _ = x.shape
            return x.reshape(B, S, N_HEADS, D_K).transpose(0, 2, 1, 3)
        key = jax.random.key(seed)
        ks = jax.random.split(key, 12)
        B, S, D = (2, 512, D_MODEL)
        s = 1.0 / np.sqrt(D)
        inp = {'query': jax.random.normal(ks[0], (B, S, D), jnp.float32), 'key': jax.random.normal(ks[1], (B, S, D), jnp.float32), 'value': jax.random.normal(ks[2], (B, S, D), jnp.float32), 'mask': jnp.ones((B, 1, 1, S), jnp.int32), 'Wq': jax.random.normal(ks[3], (D, D), jnp.float32) * s, 'bq': jax.random.normal(ks[4], (D,), jnp.float32) * s, 'Wk': jax.random.normal(ks[5], (D, D), jnp.float32) * s, 'bk': jax.random.normal(ks[6], (D,), jnp.float32) * s, 'Wv': jax.random.normal(ks[7], (D, D), jnp.float32) * s, 'bv': jax.random.normal(ks[8], (D,), jnp.float32) * s, 'Wo': jax.random.normal(ks[9], (D, D), jnp.float32) * s, 'bo': jax.random.normal(ks[10], (D,), jnp.float32) * s}
        return inp
    _L0_xattn_all = _L0_xattn_setup()
    _L0_xattn_in = {k: v for k, v in _L0_xattn_all.items() if k in ('Wq', 'bq', 'Wk', 'bk', 'Wv', 'bv', 'Wo', 'bo')}
    del _L0_xattn_all

    def _L0_ffn_setup():
        import jax, jax.numpy as jnp
        import numpy as np

        def _bitlinear(x, w_latent):
            scale = jax.lax.stop_gradient(jnp.clip(jnp.mean(jnp.abs(w_latent), axis=1, keepdims=True), 1e-05, None))
            tern = jnp.clip(jnp.round(w_latent / scale), -1.0, 1.0)
            w = w_latent + jax.lax.stop_gradient(tern - w_latent)
            return x @ (w * scale).T
        key = jax.random.key(seed)
        ks = jax.random.split(key, 6)
        dim, hidden, rank = (256, 1024, 16)
        B, S = (4, 1024)
        x = jax.random.normal(ks[0], (B, S, dim), dtype=jnp.float32)
        w_fc = 0.02 * jax.random.normal(ks[1], (hidden, dim), dtype=jnp.float32)
        w_proj = 0.02 * jax.random.normal(ks[2], (dim, hidden), dtype=jnp.float32)
        u = 0.02 * jax.random.normal(ks[3], (hidden, rank), dtype=jnp.float32)
        v = 0.02 * jax.random.normal(ks[4], (rank, dim), dtype=jnp.float32)
        fast_b = jax.random.normal(ks[5], (rank, rank), dtype=jnp.float32)
        gate = jnp.float32(0.05)
        return {'x': x, 'fast_b': fast_b, 'w_fc': w_fc, 'w_proj': w_proj, 'u': u, 'v': v, 'gate': gate}
    _L0_ffn_all = _L0_ffn_setup()
    _L0_ffn_in = {k: v for k, v in _L0_ffn_all.items() if k in ('fast_b', 'w_fc', 'w_proj', 'u', 'v', 'gate')}
    del _L0_ffn_all

    def _L1_xattn_setup():
        import jax, jax.numpy as jnp
        import numpy as np
        DIM = 256
        NUM_HEADS = 16
        HEAD_DIM = DIM // NUM_HEADS
        key = jax.random.key(seed)
        ks = jax.random.split(key, 11)
        B, N, C = (2, 512, DIM)
        s = 1.0 / np.sqrt(C)
        inp = {'q': jax.random.normal(ks[0], (B, N, C), jnp.float32), 'k': jax.random.normal(ks[1], (B, N, C), jnp.float32), 'v': jax.random.normal(ks[2], (B, N, C), jnp.float32), 'Wq': jax.random.normal(ks[3], (C, C), jnp.float32) * s, 'bq': jnp.zeros((C,), jnp.float32), 'Wk': jax.random.normal(ks[4], (C, C), jnp.float32) * s, 'bk': jnp.zeros((C,), jnp.float32), 'Wv': jax.random.normal(ks[5], (C, C), jnp.float32) * s, 'bv': jnp.zeros((C,), jnp.float32), 'Wo': jax.random.normal(ks[6], (C, C), jnp.float32) * s, 'bo': jnp.zeros((C,), jnp.float32)}
        return inp
    _L1_xattn_all = _L1_xattn_setup()
    _L1_xattn_in = {k: v for k, v in _L1_xattn_all.items() if k in ('Wq', 'bq', 'Wk', 'bk', 'Wv', 'bv', 'Wo', 'bo')}
    del _L1_xattn_all

    def _L1_ffn_setup():
        import jax, jax.numpy as jnp
        import numpy as np
        TOPK = 2
        CAPACITY_FACTOR = 1.0
        EPS = 1e-06
        B, S, D = (4, 1024, 256)
        E = 8
        SUB_H = 512 // E
        key = jax.random.key(seed)
        ks = jax.random.split(key, 7)
        x = jax.random.normal(ks[0], (B, S, D), dtype=jnp.float32)
        w_gate_w = jax.random.normal(ks[1], (D, E), dtype=jnp.float32) * 0.02
        w_gate_b = jnp.zeros((E,), jnp.float32)
        W1 = jax.random.normal(ks[2], (E, D, SUB_H), dtype=jnp.float32) * 0.02
        b1 = jnp.zeros((E, SUB_H), jnp.float32)
        W2 = jax.random.normal(ks[3], (E, SUB_H, D), dtype=jnp.float32) * 0.02
        b2 = jnp.zeros((E, D), jnp.float32)
        return {'x': x, 'w_gate_w': w_gate_w, 'w_gate_b': w_gate_b, 'W1': W1, 'b1': b1, 'W2': W2, 'b2': b2}
    _L1_ffn_all = _L1_ffn_setup()
    _L1_ffn_in = {k: v for k, v in _L1_ffn_all.items() if k in ('w_gate_w', 'w_gate_b', 'W1', 'b1', 'W2', 'b2')}
    del _L1_ffn_all
    return {'x': x, 'ctx_1024': ctx_1024, 'mask_Bx1x1xS2_if1': mask_Bx1x1xS2_if1, 'g_xattn': g_xattn, 'g_ffn': g_ffn, 'L0_xattn_Wq': _L0_xattn_in['Wq'], 'L0_xattn_bq': _L0_xattn_in['bq'], 'L0_xattn_Wk': _L0_xattn_in['Wk'], 'L0_xattn_bk': _L0_xattn_in['bk'], 'L0_xattn_Wv': _L0_xattn_in['Wv'], 'L0_xattn_bv': _L0_xattn_in['bv'], 'L0_xattn_Wo': _L0_xattn_in['Wo'], 'L0_xattn_bo': _L0_xattn_in['bo'], 'L0_ffn_fast_b': _L0_ffn_in['fast_b'], 'L0_ffn_w_fc': _L0_ffn_in['w_fc'], 'L0_ffn_w_proj': _L0_ffn_in['w_proj'], 'L0_ffn_u': _L0_ffn_in['u'], 'L0_ffn_v': _L0_ffn_in['v'], 'L0_ffn_gate': _L0_ffn_in['gate'], 'L1_xattn_Wq': _L1_xattn_in['Wq'], 'L1_xattn_bq': _L1_xattn_in['bq'], 'L1_xattn_Wk': _L1_xattn_in['Wk'], 'L1_xattn_bk': _L1_xattn_in['bk'], 'L1_xattn_Wv': _L1_xattn_in['Wv'], 'L1_xattn_bv': _L1_xattn_in['bv'], 'L1_xattn_Wo': _L1_xattn_in['Wo'], 'L1_xattn_bo': _L1_xattn_in['bo'], 'L1_ffn_w_gate_w': _L1_ffn_in['w_gate_w'], 'L1_ffn_w_gate_b': _L1_ffn_in['w_gate_b'], 'L1_ffn_W1': _L1_ffn_in['W1'], 'L1_ffn_b1': _L1_ffn_in['b1'], 'L1_ffn_W2': _L1_ffn_in['W2'], 'L1_ffn_b2': _L1_ffn_in['b2']}

def reference(x, ctx_1024, mask_Bx1x1xS2_if1, g_xattn, g_ffn, L0_xattn_Wq, L0_xattn_bq, L0_xattn_Wk, L0_xattn_bk, L0_xattn_Wv, L0_xattn_bv, L0_xattn_Wo, L0_xattn_bo, L0_ffn_fast_b, L0_ffn_w_fc, L0_ffn_w_proj, L0_ffn_u, L0_ffn_v, L0_ffn_gate, L1_xattn_Wq, L1_xattn_bq, L1_xattn_Wk, L1_xattn_bk, L1_xattn_Wv, L1_xattn_bv, L1_xattn_Wo, L1_xattn_bo, L1_ffn_w_gate_w, L1_ffn_w_gate_b, L1_ffn_W1, L1_ffn_b1, L1_ffn_W2, L1_ffn_b2):
    import jax
    import jax.numpy as jnp

    def _L0_xattn_ref(query, key, value, mask, Wq, bq, Wk, bk, Wv, bv, Wo, bo):
        import jax, jax.numpy as jnp
        import numpy as np
        D_MODEL = 256
        N_HEADS = 16
        D_K = D_MODEL // N_HEADS
        NEG = -1000000000.0

        def _split_heads(x):
            B, S, _ = x.shape
            return x.reshape(B, S, N_HEADS, D_K).transpose(0, 2, 1, 3)
        Q = _split_heads(query @ Wq.T + bq)
        K = _split_heads(key @ Wk.T + bk)
        V = _split_heads(value @ Wv.T + bv)
        scores = jnp.einsum('bhqd,bhkd->bhqk', Q, K) / np.sqrt(D_K).astype(np.float32)
        scores = jnp.where(mask == 0, jnp.float32(NEG), scores)
        attn = jax.nn.softmax(scores, axis=-1)
        out = jnp.einsum('bhqk,bhkd->bhqd', attn, V)
        B, H, S, dk = out.shape
        out = out.transpose(0, 2, 1, 3).reshape(B, S, H * dk)
        return out @ Wo.T + bo

    def _L0_ffn_ref(x, fast_b, w_fc, w_proj, u, v, gate):
        import jax, jax.numpy as jnp
        import numpy as np

        def _bitlinear(x, w_latent):
            scale = jax.lax.stop_gradient(jnp.clip(jnp.mean(jnp.abs(w_latent), axis=1, keepdims=True), 1e-05, None))
            tern = jnp.clip(jnp.round(w_latent / scale), -1.0, 1.0)
            w = w_latent + jax.lax.stop_gradient(tern - w_latent)
            return x @ (w * scale).T
        h = _bitlinear(x, w_fc) + gate * (x @ v.T @ fast_b.T @ u.T)
        r = jnp.maximum(h, 0.0)
        return _bitlinear(r * r, w_proj)

    def _L1_xattn_ref(q, k, v, Wq, bq, Wk, bk, Wv, bv, Wo, bo):
        import jax, jax.numpy as jnp
        import numpy as np
        DIM = 256
        NUM_HEADS = 16
        HEAD_DIM = DIM // NUM_HEADS
        B, Nq, C = q.shape
        Nkv = k.shape[1]
        H, D = (NUM_HEADS, HEAD_DIM)
        qh = (q @ Wq.T + bq).reshape(B, Nq, H, D).transpose(0, 2, 1, 3)
        kh = (k @ Wk.T + bk).reshape(B, Nkv, H, D).transpose(0, 2, 1, 3)
        vh = (v @ Wv.T + bv).reshape(B, Nkv, H, D).transpose(0, 2, 1, 3)
        scale = D ** (-0.5)
        attn = jax.nn.softmax(jnp.einsum('bhqd,bhkd->bhqk', qh, kh) * scale, axis=-1)
        out = jnp.einsum('bhqk,bhkd->bhqd', attn, vh)
        out = out.transpose(0, 2, 1, 3).reshape(B, Nq, C)
        return out @ Wo.T + bo

    def _L1_ffn_ref(x, w_gate_w, w_gate_b, W1, b1, W2, b2):
        import jax, jax.numpy as jnp
        import numpy as np
        TOPK = 2
        CAPACITY_FACTOR = 1.0
        EPS = 1e-06
        B, S, D = (4, 1024, 256)
        E = 8
        SUB_H = 512 // E
        Bx, Sx, Dx = x.shape
        Ex = w_gate_b.shape[0]
        K = Sx // 2
        capacity = int(CAPACITY_FACTOR * Bx)
        gate_scores = jax.nn.softmax(x @ w_gate_w + w_gate_b, axis=-1)
        _, top_idx = jax.lax.top_k(gate_scores, TOPK)
        mask = jax.nn.one_hot(top_idx, Ex, dtype=gate_scores.dtype).sum(axis=-2)
        masked = gate_scores * mask
        denom = masked.sum(axis=0, keepdims=True) + EPS
        route = masked / denom * capacity
        route_eb = jnp.transpose(route, (2, 0, 1))
        _, seq_ids = jax.lax.top_k(route_eb, K)
        seq_ids = jnp.sort(seq_ids, axis=-1)
        xg = jax.vmap(lambda idx: jnp.take_along_axis(x, idx[..., None], axis=1))(seq_ids)
        h = jnp.einsum('ebkd,edh->ebkh', xg, W1) + b1[:, None, None, :]
        h = jax.nn.gelu(h, approximate=False)
        o = jnp.einsum('ebkh,ehd->ebkd', h, W2) + b2[:, None, None, :]
        flat_ids = (jnp.arange(Bx)[None, :, None] * Sx + seq_ids).reshape(-1)
        outs = jnp.zeros((Bx * Sx, Dx), x.dtype).at[flat_ids].add(o.reshape(-1, Dx))
        return outs.reshape(Bx, Sx, Dx)
    x = x + jnp.tanh(g_xattn[0]) * _L0_xattn_ref(_layernorm(x, axis=-1), ctx_1024, ctx_1024, mask_Bx1x1xS2_if1, L0_xattn_Wq, L0_xattn_bq, L0_xattn_Wk, L0_xattn_bk, L0_xattn_Wv, L0_xattn_bv, L0_xattn_Wo, L0_xattn_bo)
    x = x + jnp.tanh(g_ffn[0]) * _L0_ffn_ref(_layernorm(x, axis=-1), L0_ffn_fast_b, L0_ffn_w_fc, L0_ffn_w_proj, L0_ffn_u, L0_ffn_v, L0_ffn_gate)
    x = x + jnp.tanh(g_xattn[1]) * _L1_xattn_ref(_layernorm(x, axis=-1), ctx_1024, ctx_1024, L1_xattn_Wq, L1_xattn_bq, L1_xattn_Wk, L1_xattn_bk, L1_xattn_Wv, L1_xattn_bv, L1_xattn_Wo, L1_xattn_bo)
    x = x + jnp.tanh(g_ffn[1]) * _L1_ffn_ref(_layernorm(x, axis=-1), L1_ffn_w_gate_w, L1_ffn_w_gate_b, L1_ffn_W1, L1_ffn_b1, L1_ffn_W2, L1_ffn_b2)
    return x

_drawn_inputs = setup_inputs


def setup_inputs(seed=0):
    import zlib

    import numpy as np

    out = dict(_drawn_inputs(seed))
    spreads = {'g_ffn': (-1.0, 0.6),
     'L1_xattn_bq': (0.0, 1.219),
     'L1_xattn_bk': (0.0, 2.0),
     'L1_xattn_bv': (0.0, 0.311),
     'L1_xattn_bo': (0.0, 0.296),
     'L1_ffn_w_gate_b': (0.0, 0.305),
     'L1_ffn_b1': (0.0, 0.669),
     'L1_ffn_b2': (0.0, 0.1)}
    factors = {'L0_xattn_bq': 3.893,
     'L0_xattn_bk': 64.0,
     'L0_ffn_fast_b': 8.0,
     'L0_ffn_u': 8.0,
     'L0_ffn_v': 8.0,
     'L1_ffn_W1': 3.662}
    for name, (base, spread) in spreads.items():
        noise = np.random.default_rng([zlib.crc32(name.encode()), seed]).standard_normal(out[name].shape)
        drawn = base * np.exp(spread * noise) if base else spread * noise
        out[name] = jnp.asarray(drawn.astype(out[name].dtype))
    for name, factor in factors.items():
        out[name] = (out[name] * factor).astype(out[name].dtype)
    return out
```

```python
from contextlib import ExitStack

import concourse.bass as bass
from concourse import mybir

F32 = mybir.dt.float32
F32R = mybir.dt.float32r
BF16 = mybir.dt.bfloat16
I32 = mybir.dt.int32
ACT = mybir.ActivationFunctionType
ALU = mybir.AluOpType
AX = mybir.AxisListType

P = 128
B, S, D = 32, 256, 256
KEYS, MAIN, REST = 77, 64, 16
PAD = MAIN + REST
HEADS, HD = 16, 16
GH = P // HD
DT = D // P
HID0, HT0 = 1024, 8
RANK = 16
E, SUB = 8, 64
HT1 = E * SUB // P
CHOSEN = S // 2
CAPACITY = float(B)
BODIES = B // 2
LANES = 2
VC = HD + 1
NEG = 1000079360.0
LN_EPS = 1e-5


def at(i, per_body, k):
    return i * per_body + (per_body + k + 1)


def before(i, per_body, k):
    return i * per_body + (k + 1)


class Banks:

    def __init__(self, walk):
        self.use, self.count, self.users = {}, [0] * 8, [[] for _ in range(8)]
        turn = {"score": 0, "other": 0}
        for kind, key in walk:
            b = turn[kind] % 4 + (4 if kind == "other" else 0)
            turn[kind] += 1
            self.use[key] = (b, self.count[b])
            self.users[b].append(key)
            self.count[b] += 1

    def wait_filled(self, eng, filled, i, key):
        b, n = self.use[key]
        eng.wait_ge(filled[b], at(i, self.count[b], n))

    def wait_free(self, pe, read_out, i, key):
        b, n = self.use[key]
        sem, per_body, k = read_out(self.users[b][n - 1])
        pe.wait_ge(sem, at(i, per_body, k) if n else before(i, per_body, k))


def layer_walk():
    for layer in range(2):
        yield "other", ("K", layer)
        for c in range(LANES):
            yield "other", ("V", layer, c)
        for c in range(LANES):
            yield "other", ("xT", 2 * layer, c)
        for c in range(LANES):
            yield "other", ("Q", layer, c)
        for c in range(LANES):
            for u in range(5):
                yield "score", ("SA", layer, c, u)
        for c in range(LANES):
            yield "other", ("mT", layer, c)
        for c in range(LANES):
            for u in range(5):
                yield "score", ("SB", layer, c, u)
        for c in range(LANES):
            for q in range(2):
                yield "other", ("PV", layer, c, q)
        for c in range(LANES):
            yield "other", ("oT", layer, c)
        for c in range(LANES):
            yield "other", ("O", layer, c)
        for c in range(LANES):
            yield "other", ("xT", 2 * layer + 1, c)
        if layer == 0:
            for c in range(LANES):
                for u in range(4):
                    yield "score", ("up", c, u)
            for c in range(LANES):
                yield "other", ("down", c)
        else:
            for c in range(LANES):
                yield "other", ("gate", c)


def expert_walk():
    for c in range(LANES):
        yield "other", ("xT", c)
    for c in range(LANES):
        for u in range(2):
            yield "other", ("sel", c, u)
    for c in range(LANES):
        for u in range(2):
            yield "score", ("up", c, u)
    for c in range(LANES):
        yield "other", ("sel8", c)
    for c in range(LANES):
        yield "other", ("down", c)


def three_products(pe, out, lhs, rhs, parts=DT, first=True, last=True):
    n = 3 * parts
    for j in range(parts):
        for m, (a, b) in enumerate(((0, 0), (0, 1), (1, 0))):
            k = 3 * j + m
            ins = pe.matmul(out, lhs(a, j), rhs(b, j), start=first and k == 0, stop=last and k == n - 1)
    return ins


def prepare(nc, ten, ps, w, const, dram):
    with ExitStack() as ctx:
        def sb(name, shape, dt=F32):
            return ctx.enter_context(nc.sbuf_tensor(name, shape, dt))

        def sem(name):
            return ctx.enter_context(nc.semaphore(name))

        names = [f"{m}{layer}" for layer in range(2) for m in "qkvo"]
        raw = {n: sb(f"raw_{n}", [P, DT, D]) for n in names}
        fc, fc_abs = sb("raw_fc", [P, DT, HID0]), sb("fc_abs", [P, DT, HID0])
        pj, pj_abs = sb("raw_pj", [P, HT0, D]), sb("pj_abs", [P, HT0, D])
        fc_scale = sb("fc_scale", [P, HID0])
        fc_half, fc_neg = sb("fc_half", [P, HID0]), sb("fc_neg", [P, HID0])
        pj_half, pj_neg = sb("pj_half", [P, D]), sb("pj_neg", [P, D])
        fast, uT, vr, fu = sb("fast", [RANK, RANK]), sb("uT", [RANK, HID0]), sb("vr", [RANK, D]), sb("fu", [RANK, HID0])
        gate, gx = sb("gate", [P, 1]), sb("gx", [P, 4])
        wg = sb("wg_raw", [P, DT, E])
        bvc, bvb, bo = sb("bvc", [P, 2, DT]), sb("bvb", [P, 2, DT, P]), sb("bo_raw", [P, 2, D])
        ones, ohf, kb = sb("ones", [P, P]), sb("ohf", [HEADS, HEADS * MAIN + HEADS * REST]), sb("kb_raw", [P, 2, DT])
        loaded, made, dve, act, pe_s = sem("w_loaded"), sem("tables_made"), sem("prep_dve"), sem("prep_act"), sem("prep_pe")
        mark = {}

        loads = [(raw[n][:], dram[f"L{n[1]}_W{n[0]}T"].rearrange("(t p) n -> p t n", p=P)) for n in names]
        loads += [(fc[:], dram["fcT"].rearrange("(t p) n -> p t n", p=P)),
                  (pj[:], dram["pjT"].rearrange("(t p) n -> p t n", p=P)),
                  (fast[:], dram["fast_b"]), (uT[:], dram["uT"]), (vr[:], dram["v"]),
                  (gate[:], dram["gate"].partition_broadcast(P)), (gx[:, 0:2], dram["g_xattn"].partition_broadcast(P)),
                  (gx[:, 2:4], dram["g_ffn"].partition_broadcast(P)),
                  (wg[:], dram["w_gate"].rearrange("(t p) n -> p t n", p=P)),
                  (const["gate_b"][:], dram["gate_b"].partition_broadcast(P))]
        for layer in range(2):
            loads += [(const["bq"][:, layer, :], dram[f"L{layer}_bq"]), (kb[:, layer, :], dram[f"L{layer}_bk"]),
                      (bvc[:, layer, :], dram[f"L{layer}_bv"]),
                      (bo[:, layer, :], dram[f"L{layer}_bo"].partition_broadcast(P))]

        with nc.Block() as block:
            @block.sync
            def _(sp):
                for dst, src in loads:
                    sp.dma_start(dst, src).then_inc(loaded, 16)

            @block.gpsimd
            def _(pool):
                n = [0]

                def step(ins):
                    n[0] += 1
                    ins.then_inc(made, 1)
                    pool.wait_ge(made, n[0])

                def band(t, pattern, low, high, mult):
                    step(pool.affine_select(out=t, in_=t, compare_op=ALU.is_ge, fill=0.0, base=-low,
                                            pattern=pattern, channel_multiplier=mult))
                    step(pool.affine_select(out=t, in_=t, compare_op=ALU.is_ge, fill=0.0, base=high,
                                            pattern=[[-s, c] for s, c in pattern], channel_multiplier=-mult))

                for t in (ones, ohf, const["head"], const["rest"], const["ident"]):
                    step(pool.memset(t[:], 1.0))
                step(pool.memset(const["minus_half"][:], -0.5))
                band(const["ident"][:], [[-1, P]], 0, 0, 1)
                band(const["head"][:], [[-HD, GH]], 0, HD - 1, 1)
                band(const["rest"][:], [[-REST, GH]], 0, KEYS - MAIN - 1, 1)
                band(ohf[:, 0:HEADS * MAIN], [[1, HEADS * MAIN]], 0, MAIN - 1, -MAIN)
                band(ohf[:, HEADS * MAIN:], [[1, HEADS * REST]], 0, REST - 1, -REST)
                for c in range(LANES):
                    vb = ten["V_blocks"][c]
                    step(pool.memset(vb[:], 0.0))
                    pairs = vb[:].rearrange("p g (t s) -> p g t s", s=GH * VC + 2 * VC)
                    step(pool.memset(pairs[0:MAIN, :, :, HD:VC], 1.0))
                    step(pool.memset(pairs[MAIN:P, :, :, VC + HD:2 * VC], 1.0))
                    for g in range(2):
                        rest = vb[:, g, 4 * GH * VC:].rearrange("p (h v) -> p h v", v=VC)
                        step(pool.tensor_copy(rest[:, :, HD], const["rest"][:]))

            tables = 6 + 10 + LANES * 5

            @block.scalar
            def _(sc):
                sc.wait_ge(loaded, 16 * len(loads))
                sc.activation(const["gain"][:], gx[:], ACT.Tanh).then_inc(act, 1)
                for t in range(DT):
                    sc.activation(fc_abs[:, t, :], fc[:, t, :], ACT.Abs).then_inc(act, 1)
                sc.activation(pj_abs[:], pj[:], ACT.Abs).then_inc(act, 1)

            @block.vector
            def _(v):
                n = [0]

                def step(ins):
                    n[0] += 1
                    ins.then_inc(dve, 1)
                    v.wait_ge(dve, n[0])

                def split(hi, lo, src):
                    step(v.tensor_copy(hi, src))
                    step(v.tensor_tensor(lo, src, hi.bitcast(F32), ALU.subtract))

                v.wait_ge(loaded, 16 * len(loads))
                v.wait_ge(made, tables)
                step(v.tensor_copy(bvb[:], bvc[:].unsqueeze(3).to_broadcast([P, 2, DT, P])))
                mark["bv"] = n[0]
                v.wait_ge(pe_s, 2)
                v.tensor_copy(fu[:, 0:512], ps[3][0:RANK, :])
                step(v.tensor_copy(fu[:, 512:1024], ps[4][0:RANK, :]))
                mark["fu"] = n[0]
                for j in range(2):
                    v.tensor_scalar(fc_scale[:, j * 512:(j + 1) * 512], ps[j][:], 1.0 / D, 1e-5, ALU.mult, ALU.max)
                step(v.tensor_scalar(const["pj_scale"][:], ps[2][:, 0:D], 1.0 / HID0, 1e-5, ALU.mult, ALU.max))
                mark["scales"] = n[0]
                step(v.tensor_scalar(fc_half[:], fc_scale[:], 0.5, None, ALU.mult))
                step(v.tensor_scalar(fc_neg[:], fc_scale[:], -0.5, None, ALU.mult))
                step(v.tensor_scalar(pj_half[:], const["pj_scale"][:], 0.5, None, ALU.mult))
                step(v.tensor_scalar(pj_neg[:], const["pj_scale"][:], -0.5, None, ALU.mult))
                wide = [P, DT, HID0]
                step(v.tensor_tensor(fc_abs[:], fc[:], fc_half[:].unsqueeze(1).to_broadcast(wide), ALU.is_gt))
                step(v.tensor_tensor(fc[:], fc[:], fc_neg[:].unsqueeze(1).to_broadcast(wide), ALU.is_lt))
                step(v.tensor_tensor(fc[:], fc_abs[:], fc[:], ALU.subtract))
                step(v.tensor_tensor(fc[:], fc[:], fc_scale[:].unsqueeze(1).to_broadcast(wide), ALU.mult))
                for j in range(2):
                    v.wait_ge(pe_s, 4 + j)
                    for t in range(DT):
                        part = fc[:, t, j * 512:(j + 1) * 512]
                        step(v.scalar_tensor_tensor(part, ps[(6, 0)[j] + t][:], gate[:, 0:1], part, ALU.mult, ALU.add))
                split(w["fc"][:, 0], w["fc"][:, 1], fc[:])
                wide = [P, HT0, D]
                step(v.tensor_tensor(pj_abs[:], pj[:], pj_half[:].unsqueeze(1).to_broadcast(wide), ALU.is_gt))
                step(v.tensor_tensor(pj[:], pj[:], pj_neg[:].unsqueeze(1).to_broadcast(wide), ALU.is_lt))
                step(v.tensor_tensor(w["pj"][:], pj_abs[:], pj[:], ALU.subtract))
                v.wait_ge(act, 4)
                step(v.tensor_scalar(const["pj_scale"][:], const["pj_scale"][:], const["gain"][:, 2:3], None, ALU.mult))
                v.wait_ge(pe_s, 3)
                for layer in range(2):
                    step(v.tensor_tensor(const["bo"][:, layer, :], ps[5][:, layer * D:(layer + 1) * D], bo[:, layer, :], ALU.add))
                    step(v.tensor_scalar(const["bo"][:, layer, :], const["bo"][:, layer, :],
                                         const["gain"][:, layer:layer + 1], None, ALU.mult))
                    step(v.tensor_scalar(raw[f"o{layer}"][:], raw[f"o{layer}"][:],
                                         const["gain"][:, layer:layer + 1], None, ALU.mult))
                step(v.tensor_scalar(const["bk"][:], kb[:], HD ** -0.5, None, ALU.mult))
                step(v.tensor_copy(const["onehot"][:], ohf[:]))
                step(v.tensor_copy(const["ones_row"][:], ones[0:1, :]))
                for name in names:
                    split(w[name][:, 0], w[name][:, 1], raw[name][:])
                split(w["gate"][:, 0], w["gate"][:, 1], wg[:])

            @block.tensor
            def _(pe):
                pe.wait_ge(made, tables)
                pe.wait_ge(act, 4)
                pe.wait_ge(loaded, 16 * len(loads))
                for j in range(2):
                    for t in range(DT):
                        pe.matmul(ps[j][:], ones[:], fc_abs[:, t, j * 512:(j + 1) * 512], start=t == 0, stop=t == DT - 1)
                for t in range(HT0):
                    ins = pe.matmul(ps[2][:, 0:D], ones[:], pj_abs[:, t, :], start=t == 0, stop=t == HT0 - 1)
                ins.then_inc(pe_s, 1)
                for j in range(2):
                    ins = pe.matmul(ps[3 + j][0:RANK, :], fast[:], uT[:, j * 512:(j + 1) * 512], start=True, stop=True)
                ins.then_inc(pe_s, 1)
                pe.wait_ge(dve, mark["bv"])
                for layer in range(2):
                    for t in range(DT):
                        ins = pe.matmul(ps[5][:, layer * D:(layer + 1) * D], bvb[:, layer, t, :],
                                        raw[f"o{layer}"][:, t, :], start=t == 0, stop=t == DT - 1)
                ins.then_inc(pe_s, 1)
                for j in range(2):
                    pe.wait_ge(dve, mark["scales"] if j else mark["fu"])
                    for t in range(DT):
                        ins = pe.matmul(ps[(6, 0)[j] + t][:], vr[:, t * P:(t + 1) * P], fu[:, j * 512:(j + 1) * 512],
                                        start=True, stop=True)
                    ins.then_inc(pe_s, 1)


def layers(nc, ten, ps, w, const, dram):
    banks = Banks(layer_walk())
    with ExitStack() as ctx:
        def sb(name, shape, dt=F32):
            return ctx.enter_context(nc.sbuf_tensor(name, shape, dt))

        def sem(name):
            return ctx.enter_context(nc.semaphore(name))

        x_in, x_mid, x_out = (sb(n, [P, 2 * LANES, D]) for n in ("x_in", "x_mid", "x_out"))
        ctxt = sb("ctxt", [P, DT, LANES, PAD])
        ctx_hi, ctx_lo = (sb(n, [P, DT, LANES, 2 * P], F32R) for n in ("ctx_hi", "ctx_lo"))
        mrow_i, mrow, neg_row = sb("mrow_i", [P, LANES, PAD], I32), sb("mrow", [P, LANES, PAD]), sb("neg_row", [1, LANES, PAD], F32R)
        mcol_i, neg_col = sb("mcol_i", [P, LANES, 2], I32), sb("neg_col", [P, LANES, 2])
        stats = [sb(f"stats{c}", [P, 2, 6]) for c in range(LANES)]
        moments = [sb(f"moments{c}", [P, 2, 2]) for c in range(LANES)]
        var_eps = [sb(f"var_eps{c}", [P, 2]) for c in range(LANES)]
        rstd = [sb(f"rstd{c}", [P, 2]) for c in range(LANES)]
        xn = [sb(f"xn{c}", [P, 2, D]) for c in range(LANES)]
        xT_hi = [sb(f"xT_hi{c}", [P, DT, S], F32R) for c in range(LANES)]
        xT_lo = [sb(f"xT_lo{c}", [P, DT, S], F32R) for c in range(LANES)]
        q_hi = [sb(f"q_hi{c}", [P, 2, S], F32R) for c in range(LANES)]
        q_lo = [sb(f"q_lo{c}", [P, 2, S], F32R) for c in range(LANES)]
        kt = sb("kt", [P, 2, LANES, PAD])
        k_hi, k_lo = sb("k_hi", [P, 2, LANES, PAD], F32R), sb("k_lo", [P, 2, LANES, PAD], F32R)
        kb_hi = [sb(f"kb_hi{c}", [P, 2, GH * PAD], F32R) for c in range(LANES)]
        kb_lo = [sb(f"kb_lo{c}", [P, 2, GH * PAD], F32R) for c in range(LANES)]
        max_main = [sb(f"max_main{c}", [P, 2, HEADS]) for c in range(LANES)]
        max_rest = [sb(f"max_rest{c}", [P, 2, HEADS]) for c in range(LANES)]
        neg_max = [sb(f"neg_max{c}", [P, 2, HEADS]) for c in range(LANES)]
        neg_maxT = [sb(f"neg_maxT{c}", [HEADS, S], F32R) for c in range(LANES)]
        prob = [sb(f"prob{c}", [P, 10, S]) for c in range(LANES)]
        inv_sum = [sb(f"inv_sum{c}", [P, 2, HEADS]) for c in range(LANES)]
        relu, sq = (prob[c][:, 0:8, :].rearrange("p (u t) s -> p u (t s)", u=4) for c in (1, 0))
        sq_hi = [sb(f"sq_hi{c}", [P, HT0, S], F32R) for c in range(LANES)]
        sq_lo = [sb(f"sq_lo{c}", [P, HT0, S], F32R) for c in range(LANES)]
        y = sb("y", [P, 2, D])
        v_blocks = ten["V_blocks"]

        per_body = {}

        def loop_sem(name, n):
            per_body[name] = (sem(name), n)
            return per_body[name][0]

        filled = [loop_sem(f"bank_filled{b}", banks.count[b]) for b in range(8)]
        x_loaded, ctx_loaded, mrow_loaded, mcol_loaded = (loop_sem(n, 16) for n in (
            "x_loaded", "ctx_loaded", "mrow_loaded", "mcol_loaded"))
        x_stored = loop_sem("x_stored", 16)
        ctx_hi_made, ctx_split, mask_made, neg_made, neg_col_made = (loop_sem(n, 1) for n in (
            "ctx_hi_made", "ctx_split", "mask_made", "neg_made", "neg_col_made"))
        stats_made, moments_made, var_made, rstd_made, xn_made, xT_hi_made, xT_made = (loop_sem(n, 8) for n in (
            "stats_made", "moments_made", "var_made", "rstd_made", "xn_made", "xT_hi_made", "xT_made"))
        kt_made, k_hi_made, k_split = (loop_sem(n, 2) for n in ("kt_made", "k_hi_made", "k_split"))
        kt_masked = loop_sem("kt_masked", 1)
        q_hi_made, q_made, kb_hi_made, kb_lo_made, v_main_made, v_made = (loop_sem(n, 4) for n in (
            "q_hi_made", "q_made", "kb_hi_made", "kb_lo_made", "v_main_made", "v_made"))
        neg_max_made, neg_maxT_made, oT_hi_made, oT_made, bias_added, x_attended = (loop_sem(n, 4) for n in (
            "neg_max_made", "neg_maxT_made", "oT_hi_made", "oT_made", "bias_added", "x_attended"))
        maxima_made, prob_made = loop_sem("maxima_made", 20), loop_sem("prob_made", 20)
        inv_made, heads_made = loop_sem("inv_made", 8), loop_sem("heads_made", 8)
        relu_made, sq_made, sq_hi_made, sq_split = (loop_sem(n, 8) for n in ("relu_made", "sq_made", "sq_hi_made", "sq_split"))
        y_made, x_fed, logits_made = (loop_sem(n, 2) for n in ("y_made", "x_fed", "logits_made"))

        with nc.Block() as block:
            @block.sync
            def _(sp):
                for s, n in per_body.values():
                    sp.sem_inc(s, n)

        def bank(key):
            return ps[banks.use[key][0]]

        def wait_filled(eng, i, key):
            banks.wait_filled(eng, filled, i, key)

        def fill(key):
            return filled[banks.use[key][0]]

        def read_out(key):
            kind = key[0]
            a = LANES * key[1] + key[2] if len(key) > 2 else 0
            return {"K": lambda: (kt_made, 2, key[1]), "V": lambda: (v_made, 4, a), "xT": lambda: (xT_made, 8, a),
                    "Q": lambda: (q_made, 4, a), "SA": lambda: (maxima_made, 20, 5 * a + key[3]),
                    "mT": lambda: (neg_maxT_made, 4, a), "SB": lambda: (prob_made, 20, 5 * a + key[3]),
                    "PV": lambda: (heads_made, 8, 2 * a + key[3]), "oT": lambda: (oT_made, 4, a),
                    "O": lambda: (x_attended, 4, a), "up": lambda: (relu_made, 8, 4 * key[1] + key[2]),
                    "down": lambda: (y_made, 2, key[1]), "gate": lambda: (logits_made, 2, key[1])}[kind]()

        def wait_free(pe, i, key):
            banks.wait_free(pe, read_out, i, key)

        def repeated(t, rest):
            return t[:].rearrange("p t c k -> p (t c) k")[:, :, rest * P:(rest + 1) * P].rearrange("p n (r k) -> p n r k", r=(2, GH)[rest])

        def keys_of(t, rest):
            keys = t[:].rearrange("p t c k -> p (t c) k")[:, :, MAIN:PAD] if rest else t[:].rearrange("p t c k -> p (t c) k")[:, :, 0:MAIN]
            return keys.unsqueeze(2).to_broadcast([P, DT * LANES, (2, GH)[rest], (MAIN, REST)[rest]])

        def x_of(stage):
            return (x_in, x_mid, x_mid, x_out)[stage]

        with nc.Block() as block:
            @block.sync
            def _(sp):
                sp.dma_start(x_in[:], dram["x"][0]).then_inc(x_loaded, 16)
                sp.dma_start(ctxt[:], dram["ctxT"][0]).then_inc(ctx_loaded, 16)
                sp.dma_start(mrow_i[:], dram["mask_row"][0].partition_broadcast(P)).then_inc(mrow_loaded, 16)
                sp.dma_start(mcol_i[:], dram["mask_col"][0]).then_inc(mcol_loaded, 16)
                with sp.Fori(0, BODIES - 1) as i:
                    sp.wait_ge(bias_added, at(i, 4, 1))
                    sp.dma_start(x_in[:], dram["x"][bass.ds(i + 1, 1)].squeeze(0)).then_inc(x_loaded, 16)
                    sp.wait_ge(ctx_split, at(i, 1, 0))
                    sp.dma_start(ctxt[:], dram["ctxT"][bass.ds(i + 1, 1)].squeeze(0)).then_inc(ctx_loaded, 16)
                    sp.wait_ge(neg_col_made, at(i, 1, 0))
                    sp.dma_start(mrow_i[:], dram["mask_row"][bass.ds(i + 1, 1)].squeeze(0).partition_broadcast(P)).then_inc(mrow_loaded, 16)
                    sp.dma_start(mcol_i[:], dram["mask_col"][bass.ds(i + 1, 1)].squeeze(0)).then_inc(mcol_loaded, 16)
                    sp.wait_ge(x_attended, at(i, 4, 3))
                    sp.dma_start(dram["x3"][bass.ds(i, 1)].squeeze(0), x_out[:]).then_inc(x_stored, 16)
                last = BODIES - 1
                sp.wait_ge(x_attended, at(last, 4, 3))
                sp.dma_start(dram["x3"][last], x_out[:]).then_inc(x_stored, 16)
                sp.wait_ge(x_stored, 16 * (BODIES + 1))

            @block.gpsimd
            def _(pool):
                def inv_std(i, j, c):
                    pool.wait_ge(var_made, at(i, 8, 2 * j + c))
                    pool.tensor_tensor(rstd[c][:], var_eps[c][:], const["minus_half"][:], ALU.pow).then_inc(rstd_made, 1)

                def add_bias(i, layer, c):
                    pool.wait_ge(xn_made, at(i, 8, 4 * layer + c))
                    src = (x_in, x_mid)[layer][:, 2 * c:2 * c + 2, :]
                    pool.tensor_tensor(x_mid[:, 2 * c:2 * c + 2, :], src,
                                       const["bo"][:, layer, :].unsqueeze(1).to_broadcast([P, 2, D]), ALU.add).then_inc(bias_added, 1)

                def key_blocks_lo(i, layer, c):
                    pool.wait_ge(k_split, at(i, 2, layer))
                    kb, head = kb_lo[c], const["head"]
                    pool.tensor_tensor(
                        kb[:, :, 0:GH * MAIN].rearrange("p g (h k) -> p g h k", k=MAIN),
                        k_lo[:, :, c, 0:MAIN].bitcast(F32).unsqueeze(2).to_broadcast([P, 2, GH, MAIN]),
                        head[:].unsqueeze(1).unsqueeze(3).to_broadcast([P, 2, GH, MAIN]), ALU.mult)
                    pool.tensor_tensor(
                        kb[:, :, GH * MAIN:].rearrange("p g (h k) -> p g h k", k=REST),
                        k_lo[:, :, c, MAIN:PAD].bitcast(F32).unsqueeze(2).to_broadcast([P, 2, GH, REST]),
                        head[:].unsqueeze(1).unsqueeze(3).to_broadcast([P, 2, GH, REST]), ALU.mult).then_inc(kb_lo_made, 1)

                with pool.Fori(0, BODIES) as i:
                    for layer in range(2):
                        for c in range(LANES):
                            inv_std(i, 2 * layer, c)
                        for c in range(LANES):
                            key_blocks_lo(i, layer, c)
                        for c in range(LANES):
                            add_bias(i, layer, c)
                        for c in range(LANES):
                            inv_std(i, 2 * layer + 1, c)
                        if layer == 0:
                            for c in range(LANES):
                                for u in range(4):
                                    pool.wait_ge(sq_hi_made, at(i, 8, 4 * c + u))
                                    pool.wait_ge(sq_made, at(i, 8, 4 * c + u))
                                    pool.tensor_tensor(sq_lo[c][:, 2 * u:2 * u + 2, :].rearrange("p t s -> p (t s)"), sq[:, u, :],
                                                       sq_hi[c][:, 2 * u:2 * u + 2, :].bitcast(F32).rearrange("p t s -> p (t s)"),
                                                       ALU.subtract).then_inc(sq_split, 1)

            @block.scalar
            def _(sc):
                def transposed_hi(i, key, made, dst):
                    wait_filled(sc, i, key)
                    sc.copy(dst[:].rearrange("p t s -> p (t s)"), bank(key)[:]).then_inc(made, 1)

                def attention(i, layer):
                    wait_filled(sc, i, ("K", layer))
                    for g in range(2):
                        ins = sc.activation(kt[:, g].rearrange("p c k -> p (c k)"), bank(("K", layer))[:, g * LANES * PAD:(g + 1) * LANES * PAD],
                                            ACT.Identity, bias=const["bk"][:, layer, g:g + 1], scale=HD ** -0.5)
                    ins.then_inc(kt_made, 1)
                    for c in range(LANES):
                        key = ("V", layer, c)
                        wait_filled(sc, i, key)
                        blocks = v_blocks[c][:].rearrange("p g (t s) -> p g t s", s=GH * VC + 2 * VC)
                        rows = bank(key)[:, 0:D].rearrange("p (g t e d) -> p g t e d", g=2, t=4, e=2)
                        sc.copy(blocks[0:MAIN, :, :, 0:HD], rows[0:MAIN, :, :, 0])
                        sc.copy(blocks[MAIN:P, :, :, VC:VC + HD], rows[MAIN:P, :, :, 1]).then_inc(v_main_made, 1)
                    for c in range(LANES):
                        transposed_hi(i, ("xT", 2 * layer, c), xT_hi_made, xT_hi[c])
                    for c in range(LANES):
                        wait_filled(sc, i, ("Q", layer, c))
                        for g in range(2):
                            ins = sc.activation(q_hi[c][:, g, :], bank(("Q", layer, c))[:, g * S:(g + 1) * S], ACT.Identity,
                                                bias=const["bq"][:, layer, g:g + 1])
                        ins.then_inc(q_hi_made, 1)
                    for c in range(LANES):
                        key = ("mT", layer, c)
                        wait_filled(sc, i, key)
                        sc.copy(neg_maxT[c][:], bank(key)[0:HEADS, 0:S]).then_inc(neg_maxT_made, 1)
                    for c in range(LANES):
                        for u in range(5):
                            key = ("SB", layer, c, u)
                            wait_filled(sc, i, key)
                            if layer == 0 and u == 0:
                                sc.wait_ge(neg_col_made, at(i, 1, 0))
                            bias = neg_col[:, c, u // 4:u // 4 + 1] if layer == 0 else 0.0
                            sc.activation(prob[c][:, 2 * u:2 * u + 2, :].rearrange("p t s -> p (t s)"), bank(key)[:], ACT.Exp,
                                          bias=bias).then_inc(prob_made, 1)
                    for c in range(LANES):
                        transposed_hi(i, ("oT", layer, c), oT_hi_made, xT_hi[c])
                    for c in range(LANES):
                        transposed_hi(i, ("xT", 2 * layer + 1, c), xT_hi_made, xT_hi[c])

                sc.preload_act_table(ACT.Exp)
                with sc.Fori(0, BODIES) as i:
                    sc.wait_ge(ctx_loaded, at(i, 16, 15))
                    sc.copy(repeated(ctx_hi, 0), keys_of(ctxt, 0))
                    sc.copy(repeated(ctx_hi, 1), keys_of(ctxt, 1)).then_inc(ctx_hi_made, 1)
                    attention(i, 0)
                    for c in range(LANES):
                        for u in range(4):
                            key = ("up", c, u)
                            wait_filled(sc, i, key)
                            if c:
                                sc.wait_ge(sq_made, at(i, 8, u))
                            sc.activation(relu[:, u, :], bank(key)[:], ACT.Relu).then_inc(relu_made, 1)
                            sc.wait_ge(relu_made, at(i, 8, 4 * c + u))
                            sc.activation(sq_hi[c][:, 2 * u:2 * u + 2, :].rearrange("p t s -> p (t s)"), relu[:, u, :],
                                          ACT.Square).then_inc(sq_hi_made, 1)
                    attention(i, 1)

            @block.vector
            def _(v):
                def layer_norm(i, j, c):
                    n = 2 * j + c
                    src = x_of(j)
                    if j == 0:
                        v.wait_ge(x_loaded, at(i, 16, 15))
                    elif j == 2:
                        v.wait_ge(x_fed, at(i, 2, c))
                    else:
                        v.wait_ge(x_attended, at(i, 4, 2 * (j // 2) + c))
                    for q in range(2):
                        ins = v.bn_stats(stats[c][:, q, :], src[:, 2 * c + q, :])
                    ins.then_inc(stats_made, 1)
                    v.wait_ge(stats_made, at(i, 8, n))
                    v.sem_inc(const["passed"], 1)
                    for q in range(2):
                        ins = v.bn_aggr(moments[c][:, q, :], stats[c][:, q, :])
                    ins.then_inc(moments_made, 1)
                    v.wait_ge(moments_made, at(i, 8, n))
                    v.tensor_scalar(var_eps[c][:], moments[c][:, :, 1], LN_EPS, None, ALU.add).then_inc(var_made, 1)

                def normalise(i, j, c):
                    v.wait_ge(rstd_made, at(i, 8, 2 * j + c))
                    for q in range(2):
                        ins = v.tensor_scalar(xn[c][:, q, :], x_of(j)[:, 2 * c + q, :], moments[c][:, q, 0:1],
                                              rstd[c][:, q:q + 1], ALU.subtract, ALU.mult)
                    ins.then_inc(xn_made, 1)

                def transposed_lo(i, key, hi_made, count, made):
                    c = key[2]
                    v.wait_ge(hi_made, at(i, count, LANES * key[1] + c))
                    v.tensor_tensor(xT_lo[c][:].rearrange("p t s -> p (t s)"), bank(key)[:],
                                    xT_hi[c][:].bitcast(F32).rearrange("p t s -> p (t s)"), ALU.subtract).then_inc(made, 1)

                def keys(i, layer):
                    v.wait_ge(kt_made, at(i, 2, layer))
                    if layer == 0:
                        v.wait_ge(mask_made, at(i, 1, 0))
                        v.tensor_tensor(kt[:], kt[:], mrow[:].unsqueeze(1).to_broadcast([P, 2, LANES, PAD]), ALU.mult).then_inc(kt_masked, 1)
                        v.wait_ge(kt_masked, at(i, 1, 0))
                    v.tensor_copy(k_hi[:], kt[:]).then_inc(k_hi_made, 1)
                    v.wait_ge(k_hi_made, at(i, 2, layer))
                    v.tensor_tensor(k_lo[:], kt[:], k_hi[:].bitcast(F32), ALU.subtract).then_inc(k_split, 1)
                    for c in range(LANES):
                        kb, head = kb_hi[c], const["head"]
                        v.tensor_tensor(
                            kb[:, :, 0:GH * MAIN].rearrange("p g (h k) -> p g h k", k=MAIN),
                            k_hi[:, :, c, 0:MAIN].bitcast(F32).unsqueeze(2).to_broadcast([P, 2, GH, MAIN]),
                            head[:].unsqueeze(1).unsqueeze(3).to_broadcast([P, 2, GH, MAIN]), ALU.mult)
                        v.tensor_tensor(
                            kb[:, :, GH * MAIN:].rearrange("p g (h k) -> p g h k", k=REST),
                            k_hi[:, :, c, MAIN:PAD].bitcast(F32).unsqueeze(2).to_broadcast([P, 2, GH, REST]),
                            head[:].unsqueeze(1).unsqueeze(3).to_broadcast([P, 2, GH, REST]), ALU.mult).then_inc(kb_hi_made, 1)

                def attention(i, layer):
                    keys(i, layer)
                    for c in range(LANES):
                        v.wait_ge(v_main_made, at(i, 4, 2 * layer + c))
                        rest = v_blocks[c][:, :, 4 * GH * VC:].rearrange("p g (h v) -> p g h v", v=VC)
                        for g in range(2):
                            ins = v.tensor_tensor(rest[:, g, :, 0:HD], bank(("V", layer, c))[:, D + g * P:D + (g + 1) * P].rearrange("p (h d) -> p h d", d=HD),
                                                  const["rest"][:].unsqueeze(2).to_broadcast([P, GH, HD]), ALU.mult)
                        ins.then_inc(v_made, 1)
                    for c in range(LANES):
                        normalise(i, 2 * layer, c)
                    for c in range(LANES):
                        transposed_lo(i, ("xT", 2 * layer, c), xT_hi_made, 8, xT_made)
                    for c in range(LANES):
                        v.wait_ge(q_hi_made, at(i, 4, 2 * layer + c))
                        for g in range(2):
                            ins = v.scalar_tensor_tensor(q_lo[c][:, g, :], bank(("Q", layer, c))[:, g * S:(g + 1) * S],
                                                         const["bq"][:, layer, g:g + 1], q_hi[c][:, g, :].bitcast(F32), ALU.add, ALU.subtract)
                        ins.then_inc(q_made, 1)
                    for c in range(LANES):
                        a = 2 * layer + c
                        for u in range(4):
                            q, g = u // 2, u % 2
                            wait_filled(v, i, ("SA", layer, c, u))
                            v.tensor_reduce(max_main[c][:, q, g * GH:(g + 1) * GH], bank(("SA", layer, c, u))[:].rearrange("p (h k) -> p h k", k=MAIN),
                                            AX.X, ALU.max, negate=True).then_inc(maxima_made, 1)
                        wait_filled(v, i, ("SA", layer, c, 4))
                        v.tensor_reduce(max_rest[c][:].rearrange("p q h -> p (q h)"), bank(("SA", layer, c, 4))[:].rearrange("p (h k) -> p h k", k=REST),
                                        AX.X, ALU.max, negate=True).then_inc(maxima_made, 1)
                        v.wait_ge(maxima_made, at(i, 20, 5 * a + 4))
                        v.tensor_tensor(neg_max[c][:], max_main[c][:], max_rest[c][:], ALU.min).then_inc(neg_max_made, 1)
                    for c in range(LANES):
                        a = 2 * layer + c
                        for q in range(2):
                            key = ("PV", layer, c, q)
                            wait_filled(v, i, key)
                            out = bank(key)[:, 0:HEADS * VC].rearrange("p (h v) -> p h v", v=VC)
                            v.reciprocal(inv_sum[c][:, q, :], out[:, :, HD]).then_inc(inv_made, 1)
                            v.wait_ge(inv_made, at(i, 8, 2 * a + q))
                            v.tensor_tensor(xn[c][:, q, :].rearrange("p (h d) -> p h d", d=HD), out[:, :, 0:HD],
                                            inv_sum[c][:, q, :].unsqueeze(2).to_broadcast([P, HEADS, HD]), ALU.mult).then_inc(heads_made, 1)
                    for c in range(LANES):
                        transposed_lo(i, ("oT", layer, c), oT_hi_made, 4, oT_made)
                    for c in range(LANES):
                        a = 2 * layer + c
                        wait_filled(v, i, ("O", layer, c))
                        v.wait_ge(bias_added, at(i, 4, a))
                        if layer and c == 0:
                            v.wait_ge(x_stored, before(i, 16, 15))
                        rows = x_mid[:, 2 * c:2 * c + 2, :]
                        dst = x_out[:, 2 * c:2 * c + 2, :] if layer else rows
                        v.tensor_tensor(dst.rearrange("p q d -> p (q d)"), bank(("O", layer, c))[:], rows.rearrange("p q d -> p (q d)"),
                                        ALU.add).then_inc(x_attended, 1)
                    for c in range(LANES):
                        layer_norm(i, 2 * layer + 1, c)
                    for c in range(LANES):
                        normalise(i, 2 * layer + 1, c)
                    for c in range(LANES):
                        transposed_lo(i, ("xT", 2 * layer + 1, c), xT_hi_made, 8, xT_made)

                with v.Fori(0, BODIES) as i:
                    v.wait_ge(ctx_hi_made, at(i, 1, 0))
                    v.tensor_tensor(repeated(ctx_lo, 0), keys_of(ctxt, 0), repeated(ctx_hi, 0).bitcast(F32), ALU.subtract)
                    v.tensor_tensor(repeated(ctx_lo, 1), keys_of(ctxt, 1), repeated(ctx_hi, 1).bitcast(F32), ALU.subtract).then_inc(ctx_split, 1)
                    v.wait_ge(mrow_loaded, at(i, 16, 15))
                    v.tensor_scalar(mrow[:], mrow_i[:], 0.0, None, ALU.not_equal).then_inc(mask_made, 1)
                    v.wait_ge(mask_made, at(i, 1, 0))
                    v.tensor_scalar(neg_row[:], mrow[0:1], 1.0, NEG, ALU.subtract, ALU.mult).then_inc(neg_made, 1)
                    v.wait_ge(mcol_loaded, at(i, 16, 15))
                    v.tensor_scalar(neg_col[:], mcol_i[:], 0.0, -NEG, ALU.is_equal, ALU.mult).then_inc(neg_col_made, 1)
                    for c in range(LANES):
                        layer_norm(i, 0, c)
                    attention(i, 0)
                    for c in range(LANES):
                        for u in range(4):
                            v.wait_ge(relu_made, at(i, 8, 4 * c + u))
                            if c:
                                v.wait_ge(sq_split, at(i, 8, u))
                            v.tensor_tensor(sq[:, u, :], relu[:, u, :], relu[:, u, :], ALU.mult).then_inc(sq_made, 1)
                    for c in range(LANES):
                        wait_filled(v, i, ("down", c))
                        v.tensor_tensor(y[:], bank(("down", c))[:].rearrange("p (q d) -> p q d", q=2),
                                        const["pj_scale"][:].unsqueeze(1).to_broadcast([P, 2, D]), ALU.mult).then_inc(y_made, 1)
                        v.wait_ge(y_made, at(i, 2, c))
                        rows = x_mid[:, 2 * c:2 * c + 2, :]
                        v.tensor_tensor(rows, rows, y[:], ALU.add).then_inc(x_fed, 1)
                        v.wait_ge(x_fed, at(i, 2, c))
                    for c in range(LANES):
                        layer_norm(i, 2, c)
                    attention(i, 1)
                    for c in range(LANES):
                        wait_filled(v, i, ("gate", c))
                        v.tensor_tensor(ten["gates"][:, bass.ds(4 * i + 2 * c, 2), :], bank(("gate", c))[:, 0:2 * E].rearrange("p (q e) -> p q e", e=E),
                                        const["gate_b"][:].unsqueeze(1).to_broadcast([P, 2, E]), ALU.add).then_inc(logits_made, 1)

            @block.tensor
            def _(pe):
                def transposes(i, key, made, per_body, n, src):
                    pe.wait_ge(made, at(i, per_body, n))
                    wait_free(pe, i, key)
                    for t in range(DT):
                        for q in range(2):
                            ins = pe.transpose(bank(key)[:, t * S + q * P:t * S + (q + 1) * P], src[:, q, t * P:(t + 1) * P], const["ident"][:])
                    ins.then_inc(fill(key), 1)

                def attention(i, layer):
                    wq, wk, wv, wo = (w[f"{m}{layer}"] for m in "qkvo")
                    ctx_half, key = (ctx_hi, ctx_lo), ("K", layer)
                    pe.wait_ge(ctx_split, at(i, 1, 0))
                    wait_free(pe, i, key)
                    for g in range(2):
                        ins = three_products(pe, bank(key)[:, g * LANES * PAD:(g + 1) * LANES * PAD].rearrange("p (c k) -> p c k", k=PAD),
                                             lambda h, t: wk[:, h, t, g * P:(g + 1) * P], lambda h, t: ctx_half[h][:, t, :, MAIN:MAIN + PAD])
                    ins.then_inc(fill(key), 1)
                    for c in range(LANES):
                        key = ("V", layer, c)
                        wait_free(pe, i, key)
                        three_products(pe, bank(key)[:, 0:D],
                                       lambda h, t: ctx_half[h][:, t, c, 0:P],
                                       lambda h, t: wv[:, h, t, :])
                        three_products(pe, bank(key)[:, D:2 * D],
                                       lambda h, t: ctx_half[h][:, t, c, P:2 * P],
                                       lambda h, t: wv[:, h, t, :]).then_inc(fill(key), 1)
                    for c in range(LANES):
                        transposes(i, ("xT", 2 * layer, c), xn_made, 8, 4 * layer + c, xn[c])
                    for c in range(LANES):
                        key, xT = ("Q", layer, c), (xT_hi[c], xT_lo[c])
                        pe.wait_ge(xT_made, at(i, 8, 4 * layer + c))
                        wait_free(pe, i, key)
                        for g in range(2):
                            ins = three_products(pe, bank(key)[:, g * S:(g + 1) * S],
                                                 lambda h, t: wq[:, h, t, g * P:(g + 1) * P], lambda h, t: xT[h][:, t, :])
                        ins.then_inc(fill(key), 1)
                    for c in range(LANES):
                        a = 2 * layer + c
                        pe.wait_ge(q_made, at(i, 4, a))
                        pe.wait_ge(kb_hi_made, at(i, 4, a))
                        if layer == 0:
                            pe.wait_ge(neg_made, at(i, 1, 0))
                        for u in range(5):
                            key = ("SA", layer, c, u)
                            wait_free(pe, i, key)
                            for q, g in [(u // 2, u % 2)] if u < 4 else [(0, 0), (0, 1), (1, 0), (1, 1)]:
                                width, keys0 = (MAIN, 0) if u < 4 else (REST, MAIN)
                                out = bank(key)[:] if u < 4 else bank(key)[:, (2 * q + g) * P:(2 * q + g + 1) * P]
                                cols = kb_hi[c][:, g, 0:GH * MAIN] if u < 4 else kb_hi[c][:, g, GH * MAIN:]
                                ins = pe.matmul(out, q_hi[c][:, g, q * P:(q + 1) * P], cols, start=True, stop=layer == 1)
                                if layer == 0:
                                    ins = pe.matmul(out.rearrange("p (h k) -> p h k", k=width), const["ones_row"][:],
                                                    neg_row[:, c, keys0:keys0 + width].unsqueeze(1).to_broadcast([1, GH, width]),
                                                    start=False, stop=True)
                            ins.then_inc(fill(key), 1)
                    for c in range(LANES):
                        key = ("mT", layer, c)
                        pe.wait_ge(neg_max_made, at(i, 4, 2 * layer + c))
                        wait_free(pe, i, key)
                        for q in range(2):
                            ins = pe.transpose(bank(key)[0:HEADS, q * P:(q + 1) * P], neg_max[c][:, q, :], const["ident"][:])
                        ins.then_inc(fill(key), 1)
                    for c in range(LANES):
                        a = 2 * layer + c
                        kb, qT = (kb_hi[c], kb_lo[c]), (q_hi[c], q_lo[c])
                        pe.wait_ge(kb_lo_made, at(i, 4, a))
                        pe.wait_ge(neg_maxT_made, at(i, 4, a))
                        for u in range(5):
                            key = ("SB", layer, c, u)
                            wait_free(pe, i, key)
                            for half in range(2):
                                n = 2 * u + half
                                g, t = (n // 4, n % 4) if u < 4 else (half, 4)
                                out = bank(key)[:, half * S:(half + 1) * S]
                                three_products(pe, out, lambda h, _: kb[h][:, g, t * P:(t + 1) * P], lambda h, _: qT[h][:, g, :], parts=1, last=False)
                                first = (g * GH + 2 * t) * MAIN if t < 4 else HEADS * MAIN + g * P
                                ins = pe.matmul(out, const["onehot"][:, first:first + P], neg_maxT[c][:], start=False, stop=True)
                            ins.then_inc(fill(key), 1)
                    for c in range(LANES):
                        a = 2 * layer + c
                        pe.wait_ge(v_made, at(i, 4, a))
                        pe.wait_ge(prob_made, at(i, 20, 5 * a + 4))
                        for q in range(2):
                            key = ("PV", layer, c, q)
                            wait_free(pe, i, key)
                            for g in range(2):
                                for t in range(5):
                                    n = 4 * g + t if t < 4 else 8 + g
                                    ins = pe.matmul(bank(key)[:, g * GH * VC:(g + 1) * GH * VC], prob[c][:, n, q * P:(q + 1) * P],
                                                    v_blocks[c][:, g, t * GH * VC:(t + 1) * GH * VC], start=t == 0, stop=t == 4)
                            ins.then_inc(fill(key), 1)
                    for c in range(LANES):
                        a = 2 * layer + c
                        transposes(i, ("oT", layer, c), heads_made, 8, 2 * a + 1, xn[c])
                    for c in range(LANES):
                        key, oT = ("O", layer, c), (xT_hi[c], xT_lo[c])
                        pe.wait_ge(oT_made, at(i, 4, 2 * layer + c))
                        wait_free(pe, i, key)
                        for q in range(2):
                            ins = three_products(pe, bank(key)[:, q * D:(q + 1) * D],
                                                 lambda h, t: oT[h][:, t, q * P:(q + 1) * P], lambda h, t: wo[:, h, t, :])
                        ins.then_inc(fill(key), 1)
                    j = 2 * layer + 1
                    for c in range(LANES):
                        transposes(i, ("xT", j, c), xn_made, 8, 2 * j + c, xn[c])

                with pe.Fori(0, BODIES) as i:
                    attention(i, 0)
                    for c in range(LANES):
                        xT = (xT_hi[c], xT_lo[c])
                        pe.wait_ge(xT_made, at(i, 8, 2 + c))
                        for u in range(4):
                            key = ("up", c, u)
                            wait_free(pe, i, key)
                            for half in range(2):
                                n = 2 * u + half
                                ins = three_products(pe, bank(key)[:, half * S:(half + 1) * S],
                                                     lambda h, t: w["fc"][:, h, t, n * P:(n + 1) * P], lambda h, t: xT[h][:, t, :])
                            ins.then_inc(fill(key), 1)
                    for c in range(LANES):
                        key = ("down", c)
                        pe.wait_ge(sq_split, at(i, 8, 4 * c + 3))
                        wait_free(pe, i, key)
                        for q in range(2):
                            for t in range(HT0):
                                for h, part in enumerate((sq_hi[c], sq_lo[c])):
                                    ins = pe.matmul(bank(key)[:, q * D:(q + 1) * D], part[:, t, q * P:(q + 1) * P], w["pj"][:, t, :],
                                                    start=t == 0 and h == 0, stop=t == HT0 - 1 and h == 1)
                        ins.then_inc(fill(key), 1)
                    attention(i, 1)
                    for c in range(LANES):
                        key, xT = ("gate", c), (xT_hi[c], xT_lo[c])
                        pe.wait_ge(xT_made, at(i, 8, 6 + c))
                        wait_free(pe, i, key)
                        for q in range(2):
                            ins = three_products(pe, bank(key)[:, q * E:(q + 1) * E],
                                                 lambda h, t: xT[h][:, t, q * P:(q + 1) * P], lambda h, t: w["gate"][:, h, t, :])
                        ins.then_inc(fill(key), 1)


def routing(nc, ten, ps, const):
    with ExitStack() as ctx:
        def sb(name, shape, dt=F32):
            return ctx.enter_context(nc.sbuf_tensor(name, shape, dt))

        def sem(name):
            return ctx.enter_context(nc.semaphore(name))

        tiles = 2 * B
        full = [P, tiles, E]
        g = ten["gates"]
        key, rank, left, first_two = (sb(n, full) for n in ("key", "rank", "left", "first_two"))
        routes = sb("routes", [P, 2, B, E])
        top, best = sb("top", [P, tiles]), sb("best", [P, tiles])
        total, inv_total = sb("total", [P, 2, E]), sb("inv_total", [P, 2, E])
        rows = [sb(f"rows{h}", [P, S]) for h in range(2)]
        eight = [sb(f"eight{h}", [P, 8]) for h in range(2)]
        mark = {}
        ranked, dve, exped, turned = sem("ranked"), sem("route_dve"), sem("exped"), sem("routes_turned")

        def wide(t):
            return t[:].unsqueeze(2).to_broadcast(full)

        with nc.Block() as block:
            @block.gpsimd
            def _(pool):
                pool.iota(rank[:], pattern=[[0, tiles], [-1, E]], base=E, channel_multiplier=0,
                          allow_small_or_imprecise_dtypes=True).then_inc(ranked, 1)

            @block.scalar
            def _(sc):
                sc.wait_ge(dve, 2)
                sc.activation(g[:], g[:], ACT.Exp).then_inc(exped, 1)

            @block.vector
            def _(v):
                n = [0]

                def step(ins):
                    n[0] += 1
                    ins.then_inc(dve, 1)
                    v.wait_ge(dve, n[0])

                step(v.tensor_reduce(top[:], g[:], AX.X, ALU.max))
                step(v.tensor_tensor(g[:], g[:], wide(top), ALU.subtract))
                v.wait_ge(exped, 1)
                step(v.tensor_reduce(top[:], g[:], AX.X, ALU.add))
                step(v.reciprocal(best[:], top[:]))
                step(v.tensor_tensor(g[:], g[:], wide(best), ALU.mult))
                v.wait_ge(ranked, 1)
                for pick in range(2):
                    src = g if pick == 0 else left
                    step(v.tensor_reduce(top[:], src[:], AX.X, ALU.max))
                    step(v.tensor_tensor(key[:], src[:], wide(top), ALU.is_equal))
                    step(v.tensor_tensor(key[:], key[:], rank[:], ALU.mult))
                    step(v.tensor_reduce(best[:], key[:], AX.X, ALU.max))
                    step(v.tensor_tensor(key[:], key[:], wide(best), ALU.is_equal))
                    if pick == 0:
                        step(v.tensor_copy(first_two[:], key[:]))
                        step(v.scalar_tensor_tensor(left[:].rearrange("p t e -> p (t e)"), key[:].rearrange("p t e -> p (t e)"), -4.0,
                                                    g[:].rearrange("p t e -> p (t e)"), ALU.mult, ALU.add))
                    else:
                        step(v.tensor_tensor(first_two[:], first_two[:], key[:], ALU.add))
                step(v.tensor_tensor(g[:], g[:], first_two[:], ALU.mult))
                step(v.tensor_reduce(total[:], g[:].rearrange("p (b q) e -> p q e b", q=2), AX.X, ALU.add))
                step(v.tensor_scalar(total[:], total[:], 1e-6, None, ALU.add))
                step(v.reciprocal(inv_total[:], total[:]))
                step(v.tensor_scalar(inv_total[:], inv_total[:], CAPACITY, None, ALU.mult))
                for q in range(2):
                    v.tensor_tensor(routes[:, q], g[:].rearrange("p (b q) e -> p q b e", q=2)[:, q],
                                    inv_total[:, q, :].unsqueeze(1).to_broadcast([P, B, E]), ALU.mult).then_inc(dve, 1)
                n[0] += 2
                mark["routed"] = n[0]
                v.wait_ge(turned, 1)
                for h in range(2):
                    step(v.tensor_copy(rows[h][:], ps[h][:, 0:S]))
                for r in range(CHOSEN // 8):
                    for h in range(2):
                        v.max(eight[h][:], rows[h][:]).then_inc(dve, 1)
                    for h in range(2):
                        n[0] += 1
                        v.wait_ge(dve, n[0] + h)
                        v.match_replace(rows[h][:], eight[h][:], rows[h][:], -1.0).then_inc(dve, 1)
                    n[0] += 2
                    v.wait_ge(dve, n[0])
                for h in range(2):
                    step(v.tensor_scalar(ten["chosen"][:, h, :], rows[h][:], 0.0, None, ALU.is_lt))

            @block.tensor
            def _(pe):
                pe.wait_ge(dve, mark["routed"])
                for h in range(2):
                    for q in range(2):
                        src = routes[:, q, h * 16:(h + 1) * 16, :].rearrange("p b e -> p (b e)")
                        ins = pe.transpose(ps[h][:, q * P:(q + 1) * P], src, const["ident"][:])
                ins.then_inc(turned, 1)


def experts(nc, ten, ps, const, dram):
    banks = Banks(expert_walk())
    with ExitStack() as ctx:
        def sb(name, shape, dt=F32):
            return ctx.enter_context(nc.sbuf_tensor(name, shape, dt))

        def sem(name):
            return ctx.enter_context(nc.semaphore(name))

        w1_raw, w2_raw, b2_raw = sb("w1_raw", [P, DT, E * SUB]), sb("w2_raw", [P, HT1, D]), sb("b2_raw", [E, D])
        w1, w2 = sb("w1", [P, 2, DT, E * SUB], F32R), sb("w2", [P, 2, HT1, D], F32R)
        b1, b2 = sb("b1", [P, HT1]), sb("b2", [E, 2, D], F32R)
        pick, spread = sb("pick", [P, 2 * P], BF16), sb("spread", [P, P * SUB], BF16)
        x3, x_keep, x_out = (sb(n, [P, 2 * LANES, D]) for n in ("x3_in", "x_keep", "x4"))
        stats = [sb(f"e_stats{c}", [P, 2, 6]) for c in range(LANES)]
        moments = [sb(f"e_moments{c}", [P, 2, 2]) for c in range(LANES)]
        var_eps = [sb(f"e_var_eps{c}", [P, 2]) for c in range(LANES)]
        rstd = [sb(f"e_rstd{c}", [P, 2]) for c in range(LANES)]
        xn = [sb(f"e_xn{c}", [P, 2, D]) for c in range(LANES)]
        xT_hi = [sb(f"e_xT_hi{c}", [P, DT, S], F32R) for c in range(LANES)]
        xT_lo = [sb(f"e_xT_lo{c}", [P, DT, S], F32R) for c in range(LANES)]
        gelu = [sb(f"gelu{c}", [P, HT1, S]) for c in range(LANES)]
        hid = [sb(f"hid{c}", [P, HT1, S]) for c in range(LANES)]
        hid_hi = [sb(f"hid_hi{c}", [P, HT1, S], F32R) for c in range(LANES)]
        hid_lo = [sb(f"hid_lo{c}", [P, HT1, S], F32R) for c in range(LANES)]
        sel8 = [sb(f"sel8_{c}", [E, S], F32R) for c in range(LANES)]

        per_body = {}

        def loop_sem(name, n):
            per_body[name] = (sem(name), n)
            return per_body[name][0]

        filled = [loop_sem(f"e_bank_filled{b}", banks.count[b]) for b in range(8)]
        x_loaded, x_stored, x_kept = loop_sem("e_x_loaded", 16), loop_sem("e_x_stored", 16), loop_sem("e_x_kept", 1)
        stats_made, moments_made, var_made, rstd_made, xn_made, xT_hi_made, xT_made = (loop_sem(n, 2) for n in (
            "e_stats_made", "e_moments_made", "e_var_made", "e_rstd_made", "e_xn_made", "e_xT_hi_made", "e_xT_made"))
        gelu_made, hid_made, hid_hi_made, hid_split = (loop_sem(n, 4) for n in ("gelu_made", "hid_made", "hid_hi_made", "hid_split"))
        sel8_made, x_made = loop_sem("sel8_made", 2), loop_sem("x4_made", 2)
        loaded, tables_made, prep = sem("e_loaded"), sem("e_tables_made"), sem("e_prep")

        def bank(key):
            return ps[banks.use[key][0]]

        def wait_filled(eng, i, key):
            banks.wait_filled(eng, filled, i, key)

        def fill(key):
            return filled[banks.use[key][0]]

        def read_out(key):
            c = key[1]
            u = 2 * c + key[2] if len(key) > 2 else 0
            return {"xT": (xT_made, 2, c), "up": (gelu_made, 4, u), "sel": (hid_made, 4, u),
                    "sel8": (sel8_made, 2, c), "down": (x_made, 2, c)}[key[0]]

        def wait_free(pe, i, key):
            banks.wait_free(pe, read_out, i, key)

        def pair(t, u):
            return t[:, 2 * u:2 * u + 2, :].rearrange("p t s -> p (t s)")

        with nc.Block() as block:
            @block.sync
            def _(sp):
                for s, n in per_body.values():
                    sp.sem_inc(s, n)
                sp.dma_start(w1_raw[:], dram["W1"].rearrange("(t p) n -> p t n", p=P)).then_inc(loaded, 16)
                sp.dma_start(w2_raw[:], dram["W2"].rearrange("(t p) n -> p t n", p=P)).then_inc(loaded, 16)
                sp.dma_start(b1[:], dram["b1"]).then_inc(loaded, 16)
                sp.dma_start(b2_raw[:], dram["b2"]).then_inc(loaded, 16)

            @block.gpsimd
            def _(pool):
                pool.memset(pick[:], 1.0).then_inc(tables_made, 1)
                pool.wait_ge(tables_made, 1)
                pool.affine_select(out=pick[:], in_=pick[:], compare_op=ALU.is_equal, fill=0.0, base=0,
                                   pattern=[[-1, 2 * P]], channel_multiplier=1).then_inc(tables_made, 1)
                pool.wait_ge(tables_made, 2)
                pool.tensor_copy(spread[:].rearrange("p (r k) -> p r k", k=SUB),
                                 pick[:, 0:P].unsqueeze(2).to_broadcast([P, P, SUB])).then_inc(tables_made, 1)

            @block.vector
            def _(v):
                n = [0]

                def step(ins):
                    n[0] += 1
                    ins.then_inc(prep, 1)
                    v.wait_ge(prep, n[0])

                def split(hi, lo, src):
                    step(v.tensor_copy(hi, src))
                    step(v.tensor_tensor(lo, src, hi.bitcast(F32), ALU.subtract))

                v.wait_ge(loaded, 64)
                step(v.tensor_scalar(w2_raw[:], w2_raw[:], const["gain"][:, 3:4], None, ALU.mult))
                step(v.tensor_scalar(b2_raw[:], b2_raw[:], const["gain"][0:E, 3:4], None, ALU.mult))
                split(w1[:, 0], w1[:, 1], w1_raw[:])
                split(w2[:, 0], w2[:, 1], w2_raw[:])
                split(b2[:, 0], b2[:, 1], b2_raw[:])

        with nc.Block() as block:
            @block.sync
            def _(sp):
                sp.dma_start(x3[:], dram["x3"][0]).then_inc(x_loaded, 16)
                with sp.Fori(0, BODIES - 1) as i:
                    sp.wait_ge(x_kept, at(i, 1, 0))
                    sp.dma_start(x3[:], dram["x3"][bass.ds(i + 1, 1)].squeeze(0)).then_inc(x_loaded, 16)
                    sp.wait_ge(x_made, at(i, 2, 1))
                    sp.dma_start(dram["out"][bass.ds(i, 1)].squeeze(0), x_out[:]).then_inc(x_stored, 16)
                last = BODIES - 1
                sp.wait_ge(x_made, at(last, 2, 1))
                sp.dma_start(dram["out"][last], x_out[:]).then_inc(x_stored, 16)
                sp.wait_ge(x_stored, 16 * (BODIES + 1))

            @block.gpsimd
            def _(pool):
                with pool.Fori(0, BODIES) as i:
                    for c in range(LANES):
                        pool.wait_ge(var_made, at(i, 2, c))
                        pool.tensor_tensor(rstd[c][:], var_eps[c][:], const["minus_half"][:], ALU.pow).then_inc(rstd_made, 1)
                    pool.wait_ge(x_made, before(i, 2, 1))
                    pool.wait_ge(xn_made, at(i, 2, 1))
                    pool.sem_inc(const["passed"], 1)
                    pool.tensor_copy(x_keep[:], x3[:]).then_inc(x_kept, 1)
                    for c in range(LANES):
                        for u in range(2):
                            pool.wait_ge(hid_hi_made, at(i, 4, 2 * c + u))
                            pool.tensor_tensor(pair(hid_lo[c], u), pair(hid[c], u), pair(hid_hi[c], u).bitcast(F32),
                                               ALU.subtract).then_inc(hid_split, 1)

            @block.scalar
            def _(sc):
                sc.preload_act_table(ACT.Gelu)
                with sc.Fori(0, BODIES) as i:
                    for c in range(LANES):
                        wait_filled(sc, i, ("xT", c))
                        sc.copy(xT_hi[c][:].rearrange("p t s -> p (t s)"), bank(("xT", c))[:]).then_inc(xT_hi_made, 1)
                    for c in range(LANES):
                        for u in range(2):
                            key = ("up", c, u)
                            wait_filled(sc, i, key)
                            for h in range(2):
                                t = 2 * u + h
                                ins = sc.activation(gelu[c][:, t, :], bank(key)[:, h * S:(h + 1) * S], ACT.Gelu, bias=b1[:, t:t + 1])
                            ins.then_inc(gelu_made, 1)
                    for c in range(LANES):
                        for u in range(2):
                            sc.wait_ge(hid_made, at(i, 4, 2 * c + u))
                            sc.copy(pair(hid_hi[c], u), pair(hid[c], u)).then_inc(hid_hi_made, 1)
                    for c in range(LANES):
                        wait_filled(sc, i, ("sel8", c))
                        sc.copy(sel8[c][:], bank(("sel8", c))[0:E, 0:S]).then_inc(sel8_made, 1)

            @block.vector
            def _(v):
                with v.Fori(0, BODIES) as i:
                    v.wait_ge(x_loaded, at(i, 16, 15))
                    for c in range(LANES):
                        for q in range(2):
                            ins = v.bn_stats(stats[c][:, q, :], x3[:, 2 * c + q, :])
                        ins.then_inc(stats_made, 1)
                        v.wait_ge(stats_made, at(i, 2, c))
                        v.sem_inc(const["passed"], 1)
                        for q in range(2):
                            ins = v.bn_aggr(moments[c][:, q, :], stats[c][:, q, :])
                        ins.then_inc(moments_made, 1)
                        v.wait_ge(moments_made, at(i, 2, c))
                        v.tensor_scalar(var_eps[c][:], moments[c][:, :, 1], LN_EPS, None, ALU.add).then_inc(var_made, 1)
                    for c in range(LANES):
                        v.wait_ge(rstd_made, at(i, 2, c))
                        for q in range(2):
                            ins = v.tensor_scalar(xn[c][:, q, :], x3[:, 2 * c + q, :], moments[c][:, q, 0:1],
                                                  rstd[c][:, q:q + 1], ALU.subtract, ALU.mult)
                        ins.then_inc(xn_made, 1)
                    for c in range(LANES):
                        v.wait_ge(xT_hi_made, at(i, 2, c))
                        v.tensor_tensor(xT_lo[c][:].rearrange("p t s -> p (t s)"), bank(("xT", c))[:],
                                        xT_hi[c][:].bitcast(F32).rearrange("p t s -> p (t s)"), ALU.subtract).then_inc(xT_made, 1)
                    for c in range(LANES):
                        for u in range(2):
                            v.wait_ge(gelu_made, at(i, 4, 2 * c + u))
                            wait_filled(v, i, ("sel", c, u))
                            v.tensor_tensor(pair(hid[c], u), bank(("sel", c, u))[:], pair(gelu[c], u), ALU.mult).then_inc(hid_made, 1)
                    v.wait_ge(x_stored, before(i, 16, 15))
                    for c in range(LANES):
                        v.wait_ge(x_kept, at(i, 1, 0))
                        wait_filled(v, i, ("down", c))
                        v.tensor_tensor(x_out[:, 2 * c:2 * c + 2, :].rearrange("p q d -> p (q d)"), bank(("down", c))[:],
                                        x_keep[:, 2 * c:2 * c + 2, :].rearrange("p q d -> p (q d)"), ALU.add).then_inc(x_made, 1)

            @block.tensor
            def _(pe):
                def body(i, half):
                    for c in range(LANES):
                        key = ("xT", c)
                        pe.wait_ge(xn_made, at(i, 2, c))
                        wait_free(pe, i, key)
                        for t in range(DT):
                            for q in range(2):
                                ins = pe.transpose(bank(key)[:, t * S + q * P:t * S + (q + 1) * P], xn[c][:, q, t * P:(t + 1) * P], const["ident"][:])
                        ins.then_inc(fill(key), 1)
                    for c in range(LANES):
                        row = 8 * (2 * i + c) - P * half
                        for u in range(2):
                            key = ("sel", c, u)
                            wait_free(pe, i, key)
                            for h in range(2):
                                first = (row + 2 * (2 * u + h)) * SUB
                                ins = pe.matmul(bank(key)[:, h * S:(h + 1) * S], spread[:, bass.ds(first, P)], ten["chosen"][:, half, :],
                                                start=True, stop=True)
                            ins.then_inc(fill(key), 1)
                    for c in range(LANES):
                        xT = (xT_hi[c], xT_lo[c])
                        pe.wait_ge(xT_made, at(i, 2, c))
                        for u in range(2):
                            key = ("up", c, u)
                            wait_free(pe, i, key)
                            for h in range(2):
                                n = 2 * u + h
                                ins = three_products(pe, bank(key)[:, h * S:(h + 1) * S],
                                                     lambda a, t: w1[:, a, t, n * P:(n + 1) * P], lambda a, t: xT[a][:, t, :])
                            ins.then_inc(fill(key), 1)
                    for c in range(LANES):
                        row, key = 8 * (2 * i + c) - P * half, ("sel8", c)
                        wait_free(pe, i, key)
                        pe.matmul(bank(key)[:, 0:S], pick[:, bass.ds(row, P)], ten["chosen"][:, half, :],
                                  start=True, stop=True).then_inc(fill(key), 1)
                    for c in range(LANES):
                        key, hh = ("down", c), (hid_hi[c], hid_lo[c])
                        pe.wait_ge(hid_split, at(i, 4, 2 * c + 1))
                        pe.wait_ge(sel8_made, at(i, 2, c))
                        wait_free(pe, i, key)
                        for q in range(2):
                            out = bank(key)[:, q * D:(q + 1) * D]
                            three_products(pe, out, lambda a, t: hh[a][:, t, q * P:(q + 1) * P], lambda a, t: w2[:, a, t, :],
                                           parts=HT1, last=False)
                            for a in range(2):
                                ins = pe.matmul(out, sel8[c][:, q * P:(q + 1) * P], b2[:, a, :], start=False, stop=a == 1)
                        ins.then_inc(fill(key), 1)

                for half in range(2):
                    with pe.Fori(half * BODIES // 2, (half + 1) * BODIES // 2) as i:
                        body(i, half)


def program(nc, dram):
    with ExitStack() as ctx:
        def sb(name, shape, dt=F32):
            return ctx.enter_context(nc.sbuf_tensor(name, shape, dt))

        ps = [ctx.enter_context(nc.psum_tensor(f"bank{b}", [P, 512], F32)) for b in range(8)]
        const = {"ident": sb("ident", [P, P]), "minus_half": sb("minus_half", [P, 2]), "gain": sb("gain", [P, 4]),
                 "passed": ctx.enter_context(nc.semaphore("passed"))}
        ten = {"gates": sb("gates", [P, 2 * B, E]), "chosen": sb("chosen", [P, 2, S], BF16)}
        with ExitStack() as inner:
            def sbi(name, shape, dt=F32):
                return inner.enter_context(nc.sbuf_tensor(name, shape, dt))

            ten["V_blocks"] = [sbi(f"v_blocks{c}", [P, 2, 5 * GH * VC]) for c in range(LANES)]
            w = {f"{m}{layer}": sbi(f"w_{m}{layer}", [P, 2, DT, D], F32R) for layer in range(2) for m in "qkvo"}
            w["fc"] = sbi("w_fc", [P, 2, DT, HID0], F32R)
            w["pj"] = sbi("w_pj", [P, HT0, D], F32R)
            w["gate"] = sbi("w_gate", [P, 2, DT, E], F32R)
            const.update(
                head=sbi("head_mask", [P, GH]), rest=sbi("rest_mask", [P, GH]), bq=sbi("bq", [P, 2, DT]), bk=sbi("bk", [P, 2, DT]),
                bo=sbi("bo", [P, 2, D]), pj_scale=sbi("pj_scale", [P, D]), gate_b=sbi("gate_b", [P, E]),
                onehot=sbi("onehot", [HEADS, HEADS * PAD], F32R), ones_row=sbi("ones_row", [1, P], F32R))
            prepare(nc, ten, ps, w, const, dram)
            layers(nc, ten, ps, w, const, dram)
        routing(nc, ten, ps, const)
        experts(nc, ten, ps, const, dram)


def kernel(**inputs):
    import numpy as np
    import concourse.bacc as bacc
    from concourse.bass_utils import run_bass_kernel_spmd as run

    def a(name):
        return np.asarray(inputs[name])

    def padded(t):
        return np.concatenate([t, t[:, :PAD - KEYS]], axis=1)

    def tokens(t):
        return t.reshape(BODIES, LANES, 2, P, D).transpose(0, 3, 1, 2, 4).reshape(BODIES, P, 2 * LANES, D)

    def columns(t):
        return t.reshape(-1, P).T

    mask = padded(a("mask_Bx1x1xS2_if1").reshape(B, KEYS))
    main = np.concatenate([mask[:, 0:MAIN]] * 2, axis=1)
    rest = np.concatenate([mask[:, MAIN:]] * GH, axis=1)
    arrays = {
        "x": tokens(a("x")),
        "ctxT": padded(a("ctx_1024")).reshape(BODIES, LANES, PAD, DT, P).transpose(0, 4, 3, 1, 2),
        "mask_row": mask.reshape(BODIES, LANES, PAD),
        "mask_col": np.stack([main, rest], axis=-1).reshape(BODIES, LANES, P, 2).transpose(0, 2, 1, 3),
        "g_xattn": a("g_xattn"), "g_ffn": a("g_ffn"), "gate": a("L0_ffn_gate").reshape(1),
        "fcT": a("L0_ffn_w_fc").T, "pjT": a("L0_ffn_w_proj").T, "fast_b": a("L0_ffn_fast_b"), "uT": a("L0_ffn_u").T, "v": a("L0_ffn_v"),
        "w_gate": a("L1_ffn_w_gate_w"), "gate_b": a("L1_ffn_w_gate_b"),
        "W1": a("L1_ffn_W1").transpose(1, 0, 2).reshape(D, E * SUB), "b1": columns(a("L1_ffn_b1").reshape(-1)),
        "W2": a("L1_ffn_W2").reshape(E * SUB, D), "b2": a("L1_ffn_b2"),
    }
    for layer in range(2):
        for m in "qkvo":
            arrays[f"L{layer}_W{m}T"] = a(f"L{layer}_xattn_W{m}").T
            bias = a(f"L{layer}_xattn_b{m}")
            arrays[f"L{layer}_b{m}"] = bias if m == "o" else columns(bias)
    nc = bacc.Bacc("TRN2", target_bir_lowering=False, num_devices=1)
    arrays = {f"in_{n}": np.ascontiguousarray(t) for n, t in arrays.items()}
    dram = {n[3:]: nc.dram_tensor(n, t.shape, mybir.dt.from_np(t.dtype), kind="ExternalInput").ap() for n, t in arrays.items()}
    dram["x3"] = nc.dram_tensor("x3_scratch", (BODIES, P, 2 * LANES, D), F32, kind="Internal").ap()
    dram["out"] = nc.dram_tensor("out_0", (BODIES, P, 2 * LANES, D), F32, kind="ExternalOutput").ap()
    program(nc, dram)
    got = run(nc, [arrays], core_ids=[0]).results[0]["out_0"]
    return got.reshape(BODIES, P, LANES, 2, D).transpose(0, 2, 3, 1, 4).reshape(B, S, D)
```

```python
from contextlib import ExitStack

import concourse.bass as bass
from concourse import mybir

F32 = mybir.dt.float32
F32R = mybir.dt.float32r
BF16 = mybir.dt.bfloat16
I32 = mybir.dt.int32
ACT = mybir.ActivationFunctionType
ALU = mybir.AluOpType
AX = mybir.AxisListType

P = 128
B, S, D = 32, 256, 256
KEYS, MAIN, REST = 77, 64, 16
PAD = MAIN + REST
HEADS, HD = 16, 16
GH = P // HD
DT = D // P
HID0, HT0 = 1024, 8
RANK = 16
E, SUB = 8, 64
HT1 = E * SUB // P
CHOSEN = S // 2
CAPACITY = float(B)
BODIES = B // 2
LANES = 2
SLOTS = 4
GROUPS = B // SLOTS
VC = HD + 1
NEG = 1000079360.0
LN_EPS = 1e-5


def at(i, per_body, k):
    return i * per_body + (per_body + k + 1)


def before(i, per_body, k):
    return i * per_body + (k + 1)


class Banks:

    def __init__(self, walk, first_bank):
        self.bank, self.users = {}, {}
        for n, (key, ahead) in enumerate(walk):
            self.bank[key] = first_bank + n % 4
            self.users.setdefault(self.bank[key], []).append((key, ahead))

    def previous(self, key, with_next):
        users = self.users[self.bank[key]]
        n = [k for k, _ in users].index(key)
        ahead = users[n][1]
        for m in range(n - 1, -len(users) - 1, -1):
            other, other_ahead = users[m]
            wrapped = m < 0
            if with_next or wrapped or not other_ahead:
                return other, ahead - other_ahead + wrapped


def front_walk():
    for c in range(LANES):
        yield from ((("SA", 0, c, u), 0) for u in range(5))
        yield ("mT", 0, c, 0), 0
        yield from ((("SB", 0, c, u), 0) for u in range(5))
        yield from ((("PV", 0, c, q), 0) for q in range(2))
        yield ("oT", 0, c, 0), 0
        yield ("O", 0, c, 0), 0
        yield ("V", 1, c, 0), 0
        yield ("xT", 1, c, 0), 0
        yield from ((("up", 0, c, u), 0) for u in range(4))
        yield ("down", 0, c, 0), 0


def back_walk():
    for c in range(LANES):
        yield ("V", 0, 1 - c, 0), c
        yield ("xT", 2, c, 0), 0
        yield ("Q", 1, c, 0), 0
        yield from ((("SA", 1, c, u), 0) for u in range(5))
        yield ("mT", 1, c, 0), 0
        yield from ((("SB", 1, c, u), 0) for u in range(5))
        yield from ((("PV", 1, c, q), 0) for q in range(2))
        yield ("oT", 1, c, 0), 0
        yield ("O", 1, c, 0), 0
        yield ("xT", 0, c, 0), 1
        yield ("K", c, 0, 0), 1
        yield ("Q", 0, c, 0), 1
        yield ("xT", 3, c, 0), 0
        yield ("gate", 0, c, 0), 0


def three_products(pe, out, lhs, rhs, parts=DT, first=True, last=True):
    n = 3 * parts
    for j in range(parts):
        for m, (a, b) in enumerate(((0, 0), (0, 1), (1, 0))):
            k = 3 * j + m
            ins = pe.matmul(out, lhs(a, j), rhs(b, j), start=first and k == 0, stop=last and k == n - 1)
    return ins


def prepare(nc, ten, ps, w, const, dram):
    with ExitStack() as ctx:
        def sb(name, shape, dt=F32):
            return ctx.enter_context(nc.sbuf_tensor(name, shape, dt))

        def sem(name):
            return ctx.enter_context(nc.semaphore(name))

        names = [f"{m}{layer}" for layer in range(2) for m in "qkvo"]
        raw = {n: sb(f"raw_{n}", [P, DT, D]) for n in names}
        fc, fc_abs = sb("raw_fc", [P, DT, HID0]), sb("fc_abs", [P, DT, HID0])
        pj, pj_abs = sb("raw_pj", [P, HT0, D]), sb("pj_abs", [P, HT0, D])
        fc_scale = sb("fc_scale", [P, HID0])
        fc_half, fc_neg = sb("fc_half", [P, HID0]), sb("fc_neg", [P, HID0])
        pj_half, pj_neg = sb("pj_half", [P, D]), sb("pj_neg", [P, D])
        fast, uT, vr, fu = sb("fast", [RANK, RANK]), sb("uT", [RANK, HID0]), sb("vr", [RANK, D]), sb("fu", [RANK, HID0])
        gate, gx = sb("gate", [P, 1]), sb("gx", [P, 4])
        wg = sb("wg_raw", [P, DT, E])
        bvc, bvb, bo = sb("bvc", [P, 2, DT]), sb("bvb", [P, 2, DT, P]), sb("bo_raw", [P, 2, D])
        ones, ohf, kb = sb("ones", [P, P]), sb("ohf", [HEADS, HEADS * MAIN + HEADS * REST]), sb("kb_raw", [P, 2, DT])
        loaded, made, dve, act, pe_s = sem("w_loaded"), sem("tables_made"), sem("prep_dve"), sem("prep_act"), sem("prep_pe")
        mark = {}

        loads = [(raw[n][:], dram[f"L{n[1]}_W{n[0]}T"].rearrange("(t p) n -> p t n", p=P)) for n in names]
        loads += [(fc[:], dram["fcT"].rearrange("(t p) n -> p t n", p=P)),
                  (pj[:], dram["pjT"].rearrange("(t p) n -> p t n", p=P)),
                  (fast[:], dram["fast_b"]), (uT[:], dram["uT"]), (vr[:], dram["v"]),
                  (gate[:], dram["gate"].partition_broadcast(P)), (gx[:, 0:2], dram["g_xattn"].partition_broadcast(P)),
                  (gx[:, 2:4], dram["g_ffn"].partition_broadcast(P)),
                  (wg[:], dram["w_gate"].rearrange("(t p) n -> p t n", p=P)),
                  (const["gate_b"][:], dram["gate_b"].partition_broadcast(P))]
        for layer in range(2):
            loads += [(const["bq"][:, layer, :], dram[f"L{layer}_bq"]), (kb[:, layer, :], dram[f"L{layer}_bk"]),
                      (bvc[:, layer, :], dram[f"L{layer}_bv"]),
                      (bo[:, layer, :], dram[f"L{layer}_bo"].partition_broadcast(P))]

        with nc.Block() as block:
            @block.sync
            def _(sp):
                for dst, src in loads:
                    sp.dma_start(dst, src).then_inc(loaded, 16)

            @block.gpsimd
            def _(pool):
                n = [0]

                def step(ins):
                    n[0] += 1
                    ins.then_inc(made, 1)
                    pool.wait_ge(made, n[0])

                def band(t, pattern, low, high, mult):
                    step(pool.affine_select(out=t, in_=t, compare_op=ALU.is_ge, fill=0.0, base=-low,
                                            pattern=pattern, channel_multiplier=mult))
                    step(pool.affine_select(out=t, in_=t, compare_op=ALU.is_ge, fill=0.0, base=high,
                                            pattern=[[-s, c] for s, c in pattern], channel_multiplier=-mult))

                for t in (ones, ohf, const["head"], const["rest"], const["ident"]):
                    step(pool.memset(t[:], 1.0))
                step(pool.memset(const["minus_half"][:], -0.5))
                band(const["ident"][:], [[-1, P]], 0, 0, 1)
                band(const["head"][:], [[-HD, GH]], 0, HD - 1, 1)
                band(const["rest"][:], [[-REST, GH]], 0, KEYS - MAIN - 1, 1)
                band(ohf[:, 0:HEADS * MAIN], [[1, HEADS * MAIN]], 0, MAIN - 1, -MAIN)
                band(ohf[:, HEADS * MAIN:], [[1, HEADS * REST]], 0, REST - 1, -REST)
                for c in range(LANES):
                    vb = ten["V_blocks"][c]
                    step(pool.memset(vb[:], 0.0))
                    pairs = vb[:].rearrange("p g (t s) -> p g t s", s=GH * VC + 2 * VC)
                    step(pool.memset(pairs[0:MAIN, :, :, HD:VC], 1.0))
                    step(pool.memset(pairs[MAIN:P, :, :, VC + HD:2 * VC], 1.0))
                    for g in range(2):
                        rest = vb[:, g, 4 * GH * VC:].rearrange("p (h v) -> p h v", v=VC)
                        step(pool.tensor_copy(rest[:, :, HD], const["rest"][:]))

            tables = 6 + 10 + LANES * 5

            @block.scalar
            def _(sc):
                sc.wait_ge(loaded, 16 * len(loads))
                sc.activation(const["gain"][:], gx[:], ACT.Tanh).then_inc(act, 1)
                for t in range(DT):
                    sc.activation(fc_abs[:, t, :], fc[:, t, :], ACT.Abs).then_inc(act, 1)
                sc.activation(pj_abs[:], pj[:], ACT.Abs).then_inc(act, 1)

            @block.vector
            def _(v):
                n = [0]

                def step(ins):
                    n[0] += 1
                    ins.then_inc(dve, 1)
                    v.wait_ge(dve, n[0])

                def split(hi, lo, src):
                    step(v.tensor_copy(hi, src))
                    step(v.tensor_tensor(lo, src, hi.bitcast(F32), ALU.subtract))

                v.wait_ge(loaded, 16 * len(loads))
                v.wait_ge(made, tables)
                step(v.tensor_copy(bvb[:], bvc[:].unsqueeze(3).to_broadcast([P, 2, DT, P])))
                mark["bv"] = n[0]
                v.wait_ge(pe_s, 2)
                v.tensor_copy(fu[:, 0:512], ps[3][0:RANK, :])
                step(v.tensor_copy(fu[:, 512:1024], ps[4][0:RANK, :]))
                mark["fu"] = n[0]
                for j in range(2):
                    v.tensor_scalar(fc_scale[:, j * 512:(j + 1) * 512], ps[j][:], 1.0 / D, 1e-5, ALU.mult, ALU.max)
                step(v.tensor_scalar(const["pj_scale"][:], ps[2][:, 0:D], 1.0 / HID0, 1e-5, ALU.mult, ALU.max))
                mark["scales"] = n[0]
                step(v.tensor_scalar(fc_half[:], fc_scale[:], 0.5, None, ALU.mult))
                step(v.tensor_scalar(fc_neg[:], fc_scale[:], -0.5, None, ALU.mult))
                step(v.tensor_scalar(pj_half[:], const["pj_scale"][:], 0.5, None, ALU.mult))
                step(v.tensor_scalar(pj_neg[:], const["pj_scale"][:], -0.5, None, ALU.mult))
                wide = [P, DT, HID0]
                step(v.tensor_tensor(fc_abs[:], fc[:], fc_half[:].unsqueeze(1).to_broadcast(wide), ALU.is_gt))
                step(v.tensor_tensor(fc[:], fc[:], fc_neg[:].unsqueeze(1).to_broadcast(wide), ALU.is_lt))
                step(v.tensor_tensor(fc[:], fc_abs[:], fc[:], ALU.subtract))
                step(v.tensor_tensor(fc[:], fc[:], fc_scale[:].unsqueeze(1).to_broadcast(wide), ALU.mult))
                for j in range(2):
                    v.wait_ge(pe_s, 4 + j)
                    for t in range(DT):
                        part = fc[:, t, j * 512:(j + 1) * 512]
                        step(v.scalar_tensor_tensor(part, ps[(6, 0)[j] + t][:], gate[:, 0:1], part, ALU.mult, ALU.add))
                split(w["fc"][:, 0], w["fc"][:, 1], fc[:])
                wide = [P, HT0, D]
                step(v.tensor_tensor(pj_abs[:], pj[:], pj_half[:].unsqueeze(1).to_broadcast(wide), ALU.is_gt))
                step(v.tensor_tensor(pj[:], pj[:], pj_neg[:].unsqueeze(1).to_broadcast(wide), ALU.is_lt))
                step(v.tensor_tensor(w["pj"][:], pj_abs[:], pj[:], ALU.subtract))
                v.wait_ge(act, 4)
                step(v.tensor_scalar(const["pj_scale"][:], const["pj_scale"][:], const["gain"][:, 2:3], None, ALU.mult))
                v.wait_ge(pe_s, 3)
                for layer in range(2):
                    step(v.tensor_tensor(const["bo"][:, layer, :], ps[5][:, layer * D:(layer + 1) * D], bo[:, layer, :], ALU.add))
                    step(v.tensor_scalar(const["bo"][:, layer, :], const["bo"][:, layer, :],
                                         const["gain"][:, layer:layer + 1], None, ALU.mult))
                    step(v.tensor_scalar(raw[f"o{layer}"][:], raw[f"o{layer}"][:],
                                         const["gain"][:, layer:layer + 1], None, ALU.mult))
                step(v.tensor_scalar(const["bk"][:], kb[:], HD ** -0.5, None, ALU.mult))
                step(v.tensor_copy(const["onehot"][:], ohf[:]))
                step(v.tensor_copy(const["ones_row"][:], ones[0:1, :]))
                for name in names:
                    split(w[name][:, 0], w[name][:, 1], raw[name][:])
                split(w["gate"][:, 0], w["gate"][:, 1], wg[:])

            @block.tensor
            def _(pe):
                pe.wait_ge(made, tables)
                pe.wait_ge(act, 4)
                pe.wait_ge(loaded, 16 * len(loads))
                for j in range(2):
                    for t in range(DT):
                        pe.matmul(ps[j][:], ones[:], fc_abs[:, t, j * 512:(j + 1) * 512], start=t == 0, stop=t == DT - 1)
                for t in range(HT0):
                    ins = pe.matmul(ps[2][:, 0:D], ones[:], pj_abs[:, t, :], start=t == 0, stop=t == HT0 - 1)
                ins.then_inc(pe_s, 1)
                for j in range(2):
                    ins = pe.matmul(ps[3 + j][0:RANK, :], fast[:], uT[:, j * 512:(j + 1) * 512], start=True, stop=True)
                ins.then_inc(pe_s, 1)
                pe.wait_ge(dve, mark["bv"])
                for layer in range(2):
                    for t in range(DT):
                        ins = pe.matmul(ps[5][:, layer * D:(layer + 1) * D], bvb[:, layer, t, :],
                                        raw[f"o{layer}"][:, t, :], start=t == 0, stop=t == DT - 1)
                ins.then_inc(pe_s, 1)
                for j in range(2):
                    pe.wait_ge(dve, mark["scales"] if j else mark["fu"])
                    for t in range(DT):
                        ins = pe.matmul(ps[(6, 0)[j] + t][:], vr[:, t * P:(t + 1) * P], fu[:, j * 512:(j + 1) * 512],
                                        start=True, stop=True)
                    ins.then_inc(pe_s, 1)


def layers(nc, ten, ps, w, const, dram):
    front_banks, back_banks = Banks(front_walk(), 0), Banks(back_walk(), 4)
    with ExitStack() as ctx:
        def sb(name, shape, dt=F32):
            return ctx.enter_context(nc.sbuf_tensor(name, shape, dt))

        def sem(name):
            return ctx.enter_context(nc.semaphore(name))

        def lanes(name, shape, dt=F32):
            return [sb(f"{name}{c}", shape, dt) for c in range(LANES)]

        x_in, x_mid = lanes("x_in", [P, 2, D]), lanes("x_mid", [P, 2, D])
        ctxt = sb("ctxt", [P, DT, LANES, PAD])
        ctx_hi, ctx_lo = (sb(n, [P, DT, LANES, 2 * P], F32R) for n in ("ctx_hi", "ctx_lo"))
        mrow_i, mrow, neg_row = sb("mrow_i", [P, LANES, PAD], I32), sb("mrow", [P, LANES, PAD]), sb("neg_row", [1, LANES, PAD], F32R)
        mcol_i, neg_col = sb("mcol_i", [P, LANES, 2], I32), sb("neg_col", [P, LANES, 2])
        stats, moments, var_eps, rstd = ([lanes(f"{n}_{g}_", s) for g in ("first", "later")] for n, s in (
            ("stats", [P, 2, 6]), ("moments", [P, 2, 2]), ("var_eps", [P, 2]), ("rstd", [P, 2])))
        xn_first, xn_later = sb("xn_first", [P, 2, D]), lanes("xn", [P, 2, D])
        xT_first, xT_later = [sb(f"xT_first_{h}", [P, DT, S], F32R) for h in ("hi", "lo")], [lanes(f"xT_{h}", [P, DT, S], F32R) for h in ("hi", "lo")]
        q_hi, q_lo = lanes("q_hi", [P, 2, S], F32R), lanes("q_lo", [P, 2, S], F32R)
        kt = sb("kt", [P, 2, LANES, PAD])
        k_hi, k_lo = ([sb(f"{n}{layer}", [P, 2, LANES, PAD], F32R) for layer in range(2)] for n in ("k_hi", "k_lo"))
        kb_hi, kb_lo = lanes("kb_hi", [P, 2, GH * PAD], F32R), lanes("kb_lo", [P, 2, GH * PAD], F32R)
        max_main, max_rest, neg_max = (lanes(n, [P, 2, HEADS]) for n in ("max_main", "max_rest", "neg_max"))
        neg_maxT = lanes("neg_maxT", [HEADS, S], F32R)
        prob = lanes("prob", [P, 10, S])
        inv_sum = lanes("inv_sum", [P, 2, HEADS])
        relu = [prob[c][:, 0:4, :].rearrange("p (u t) s -> p u (t s)", t=2) for c in range(LANES)]
        sq = [prob[c][:, 4:10, :].rearrange("p (u t) s -> p u (t s)", t=2) for c in range(LANES)]
        sq_hi, sq_lo = lanes("sq_hi", [P, HT0, S], F32R), lanes("sq_lo", [P, HT0, S], F32R)
        v_blocks = ten["V_blocks"]

        per_body = {}

        def loop_sem(name, n):
            per_body[name] = (sem(name), n)
            return per_body[name][0]

        def lane_sems(name, n):
            return [loop_sem(f"{name}{c}", n) for c in range(LANES)]

        def turn(kind, stage, u):
            if kind == "xT":
                return (1, 0) if stage == 0 else (3, stage - 1)
            units = {"SA": 5, "SB": 5, "PV": 2, "up": 4}.get(kind, 1)
            return units * (1 if kind in ("up", "down", "gate") else 2), units * stage + u

        def name_of(key):
            return ("xT0" if key[0] == "xT" and key[1] == 0 else key[0]), key[2]

        x_loaded, x_stored = lane_sems("x_loaded", 16), lane_sems("x_stored", 16)
        ctx_loaded, mrow_loaded, mcol_loaded = (loop_sem(n, 16) for n in ("ctx_loaded", "mrow_loaded", "mcol_loaded"))
        ctx_hi_made, ctx_split, mask_made, neg_made, neg_col_made, kt_masked = (loop_sem(n, 1) for n in (
            "ctx_hi_made", "ctx_split", "mask_made", "neg_made", "neg_col_made", "kt_masked"))
        kt_made, k_hi_made, k_split = (loop_sem(n, 2) for n in ("kt_made", "k_hi_made", "k_split"))
        stats_made, moments_made, var_made, rstd_made, xn_made, xT_hi_made, xT_made = (
            (lane_sems(f"{n}_first", 1), lane_sems(n, 3)) for n in (
                "stats_made", "moments_made", "var_made", "rstd_made", "xn_made", "xT_hi_made", "xT_made"))
        q_hi_made, q_made, kb_hi_made, kb_lo_made, v_main_made, v_made = (lane_sems(n, 2) for n in (
            "q_hi_made", "q_made", "kb_hi_made", "kb_lo_made", "v_main_made", "v_made"))
        neg_max_made, neg_maxT_made, oT_hi_made, oT_made, bias_added, x_attended = (lane_sems(n, 2) for n in (
            "neg_max_made", "neg_maxT_made", "oT_hi_made", "oT_made", "bias_added", "x_attended"))
        maxima_made, prob_made = lane_sems("maxima_made", 10), lane_sems("prob_made", 10)
        inv_made, heads_made = lane_sems("inv_made", 4), lane_sems("heads_made", 4)
        relu_made, sq_made, sq_hi_made, sq_split = (lane_sems(n, 4) for n in ("relu_made", "sq_made", "sq_hi_made", "sq_split"))
        y_made, x_fed, logits_made = (lane_sems(n, 1) for n in ("y_made", "x_fed", "logits_made"))
        read_out = {"V": v_made, "xT0": xT_made[0], "xT": xT_made[1], "Q": q_made, "SA": maxima_made, "mT": neg_maxT_made, "SB": prob_made,
                    "PV": heads_made, "oT": oT_made, "O": x_attended, "up": relu_made, "down": y_made, "gate": logits_made, "K": [kt_made]}
        filled = {}
        for key, _ in [*front_walk(), *back_walk()]:
            if name_of(key) not in filled:
                filled[name_of(key)] = loop_sem(f"{name_of(key)[0]}_filled{key[2]}", turn(key[0], key[1], key[3])[0])

        with nc.Block() as block:
            @block.sync
            def _(sp):
                for s, n in per_body.values():
                    sp.sem_inc(s, n)

        def banks_of(key):
            return front_banks if key in front_banks.bank else back_banks

        def bank(*key):
            return ps[banks_of(key).bank[key]]

        def wait_filled(eng, i, *key):
            eng.wait_ge(filled[name_of(key)], at(i, *turn(key[0], key[1], key[3])))

        def wait_free(pe, i, with_next, waited, *key):
            other, back = banks_of(key).previous(key, with_next)
            name, c = name_of(other)
            value = at(i - back, *turn(other[0], other[1], other[3]))
            if read_out[name][c] is not waited and (not isinstance(value, int) or value > 0):
                pe.wait_ge(read_out[name][c], value)

        def fill(*key):
            return filled[name_of(key)]

        def repeated(t, rest):
            return t[:].rearrange("p t c k -> p (t c) k")[:, :, rest * P:(rest + 1) * P].rearrange("p n (r k) -> p n r k", r=(2, GH)[rest])

        def keys_of(t, rest):
            keys = t[:].rearrange("p t c k -> p (t c) k")[:, :, MAIN:PAD] if rest else t[:].rearrange("p t c k -> p (t c) k")[:, :, 0:MAIN]
            return keys.unsqueeze(2).to_broadcast([P, DT * LANES, (2, GH)[rest], (MAIN, REST)[rest]])

        def flat(t):
            return t[:].rearrange("p t s -> p (t s)")

        def pair(t, u):
            return t[:, 2 * u:2 * u + 2, :].rearrange("p t s -> p (t s)")

        def group(stage):
            return min(stage, 1)

        def nth(stage):
            return (1, 0) if stage == 0 else (3, stage - 1)

        def xn_of(stage, c):
            return xn_later[c] if stage else xn_first

        def xT_of(stage, c):
            return [t[c] for t in xT_later] if stage else xT_first

        def schedule(eng, half):
            half(-1, 0, False, False, True)
            half(-1, 1, True, False, True)
            with eng.Fori(0, BODIES - 1) as i:
                half(i, 0, True, True, True)
                half(i, 1, True, True, True)
            half(BODIES - 1, 0, True, True, False)
            half(BODIES - 1, 1, False, True, False)

        with nc.Block() as block:
            @block.sync
            def _(sp):
                def body_of(name, i):
                    return dram[name][i] if isinstance(i, int) else dram[name][bass.ds(i, 1)].squeeze(0)

                def load_x(i, c):
                    sp.dma_start(x_in[c][:], body_of("x", i)[:, 2 * c:2 * c + 2, :]).then_inc(x_loaded[c], 16)

                def load_keys(i):
                    sp.dma_start(ctxt[:], body_of("ctxT", i)).then_inc(ctx_loaded, 16)
                    sp.dma_start(mrow_i[:], body_of("mask_row", i).partition_broadcast(P)).then_inc(mrow_loaded, 16)
                    sp.dma_start(mcol_i[:], body_of("mask_col", i)).then_inc(mcol_loaded, 16)

                def store_x(i, c):
                    sp.wait_ge(x_attended[c], at(i, 2, 1))
                    sp.dma_start(body_of("x3", i)[:, 2 * c:2 * c + 2, :], x_mid[c][:]).then_inc(x_stored[c], 16)

                load_x(0, 0)
                load_keys(0)
                load_x(0, 1)
                with sp.Fori(0, BODIES - 1) as i:
                    sp.wait_ge(bias_added[0], at(i, 2, 0))
                    load_x(i + 1, 0)
                    sp.wait_ge(ctx_split, at(i, 1, 0))
                    sp.wait_ge(neg_col_made, at(i, 1, 0))
                    load_keys(i + 1)
                    sp.wait_ge(bias_added[1], at(i, 2, 0))
                    load_x(i + 1, 1)
                    for c in range(LANES):
                        store_x(i, c)
                for c in range(LANES):
                    store_x(BODIES - 1, c)
                for c in range(LANES):
                    sp.wait_ge(x_stored[c], 16 * (BODIES + 1))

            @block.gpsimd
            def _(pool):
                def inv_std(i, stage, c):
                    g = group(stage)
                    pool.wait_ge(var_made[g][c], at(i, *nth(stage)))
                    pool.tensor_tensor(rstd[g][c][:], var_eps[g][c][:], const["minus_half"][:], ALU.pow).then_inc(rstd_made[g][c], 1)

                def add_bias(i, layer, c):
                    pool.wait_ge(xn_made[layer][c], at(i, *nth(2 * layer)))
                    if layer == 0:
                        pool.wait_ge(x_stored[c], before(i, 16, 15))
                        pool.wait_ge(xn_made[1][c], before(i, *nth(3)))
                    src = (x_in, x_mid)[layer][c]
                    pool.tensor_tensor(x_mid[c][:], src[:], const["bo"][:, layer, :].unsqueeze(1).to_broadcast([P, 2, D]),
                                       ALU.add).then_inc(bias_added[c], 1)

                def key_blocks_lo(i, layer, c):
                    pool.wait_ge(k_split, at(i, 2, layer))
                    pool.wait_ge(filled["SB", c], at(i, 10, 4) if layer else before(i, 10, 9))
                    kb, head = kb_lo[c], const["head"]
                    pool.tensor_tensor(
                        kb[:, :, 0:GH * MAIN].rearrange("p g (h k) -> p g h k", k=MAIN),
                        k_lo[layer][:, :, c, 0:MAIN].bitcast(F32).unsqueeze(2).to_broadcast([P, 2, GH, MAIN]),
                        head[:].unsqueeze(1).unsqueeze(3).to_broadcast([P, 2, GH, MAIN]), ALU.mult)
                    pool.tensor_tensor(
                        kb[:, :, GH * MAIN:].rearrange("p g (h k) -> p g h k", k=REST),
                        k_lo[layer][:, :, c, MAIN:PAD].bitcast(F32).unsqueeze(2).to_broadcast([P, 2, GH, REST]),
                        head[:].unsqueeze(1).unsqueeze(3).to_broadcast([P, 2, GH, REST]), ALU.mult).then_inc(kb_lo_made[c], 1)

                def square_lo(i, c, u):
                    pool.wait_ge(sq_hi_made[c], at(i, 4, u))
                    pool.wait_ge(sq_made[c], at(i, 4, u))
                    pool.tensor_tensor(pair(sq_lo[c], u), sq[c][:, u % 3, :], pair(sq_hi[c], u).bitcast(F32),
                                       ALU.subtract).then_inc(sq_split[c], 1)

                def half(i, b, front, back, ahead):
                    f, j = 1 - b, i + b
                    if back:
                        inv_std(i, 2, b)
                        key_blocks_lo(i, 1, b)
                        add_bias(i, 1, b)
                    if front:
                        add_bias(j, 0, f)
                        inv_std(j, 1, f)
                    if ahead:
                        inv_std(i + 1, 0, b)
                    if front:
                        square_lo(j, f, 0)
                        square_lo(j, f, 1)
                    if back:
                        inv_std(i, 3, b)
                    if front:
                        square_lo(j, f, 2)
                        square_lo(j, f, 3)
                    if ahead:
                        key_blocks_lo(i + 1, 0, b)

                schedule(pool, half)

            @block.scalar
            def _(sc):
                def transposed_hi(i, stage, c):
                    wait_filled(sc, i, "xT", stage, c, 0)
                    sc.copy(flat(xT_of(stage, c)[0]), bank("xT", stage, c, 0)[:]).then_inc(xT_hi_made[group(stage)][c], 1)

                def heads_hi(i, layer, c):
                    wait_filled(sc, i, "oT", layer, c, 0)
                    sc.copy(flat(xT_later[0][c]), bank("oT", layer, c, 0)[:]).then_inc(oT_hi_made[c], 1)

                def keys(i, layer):
                    wait_filled(sc, i, "K", layer, 0, 0)
                    sc.wait_ge(k_split, at(i, 2, 0) if layer else before(i, 2, 1))
                    for g in range(2):
                        ins = sc.activation(kt[:, g].rearrange("p c k -> p (c k)"), bank("K", layer, 0, 0)[:, g * LANES * PAD:(g + 1) * LANES * PAD],
                                            ACT.Identity, bias=const["bk"][:, layer, g:g + 1], scale=HD ** -0.5)
                    ins.then_inc(kt_made, 1)

                def values(i, layer, c):
                    wait_filled(sc, i, "V", layer, c, 0)
                    blocks = v_blocks[c][:].rearrange("p g (t s) -> p g t s", s=GH * VC + 2 * VC)
                    rows = bank("V", layer, c, 0)[:, 0:D].rearrange("p (g t e d) -> p g t e d", g=2, t=4, e=2)
                    sc.copy(blocks[0:MAIN, :, :, 0:HD], rows[0:MAIN, :, :, 0])
                    sc.copy(blocks[MAIN:P, :, :, VC:VC + HD], rows[MAIN:P, :, :, 1]).then_inc(v_main_made[c], 1)

                def queries(i, layer, c):
                    wait_filled(sc, i, "Q", layer, c, 0)
                    for g in range(2):
                        ins = sc.activation(q_hi[c][:, g, :], bank("Q", layer, c, 0)[:, g * S:(g + 1) * S], ACT.Identity,
                                            bias=const["bq"][:, layer, g:g + 1])
                    ins.then_inc(q_hi_made[c], 1)

                def maxima(i, layer, c):
                    wait_filled(sc, i, "mT", layer, c, 0)
                    sc.copy(neg_maxT[c][:], bank("mT", layer, c, 0)[0:HEADS, 0:S]).then_inc(neg_maxT_made[c], 1)

                def exponentials(i, layer, c, u):
                    wait_filled(sc, i, "SB", layer, c, u)
                    if layer == 0 and u == 0:
                        sc.wait_ge(neg_col_made, at(i, 1, 0))
                    bias = neg_col[:, c, u // 4:u // 4 + 1] if layer == 0 else 0.0
                    sc.activation(pair(prob[c], u), bank("SB", layer, c, u)[:], ACT.Exp, bias=bias).then_inc(prob_made[c], 1)

                def squares_hi(i, c, u):
                    wait_filled(sc, i, "up", 0, c, u)
                    if u > 1:
                        sc.wait_ge(sq_made[c], at(i, 4, u - 2))
                    sc.activation(relu[c][:, u % 2, :], bank("up", 0, c, u)[:], ACT.Relu).then_inc(relu_made[c], 1)
                    sc.wait_ge(relu_made[c], at(i, 4, u))
                    sc.activation(pair(sq_hi[c], u), relu[c][:, u % 2, :], ACT.Square).then_inc(sq_hi_made[c], 1)

                def context_hi(i):
                    sc.wait_ge(ctx_loaded, at(i, 16, 15))
                    sc.copy(repeated(ctx_hi, 0), keys_of(ctxt, 0))
                    sc.copy(repeated(ctx_hi, 1), keys_of(ctxt, 1)).then_inc(ctx_hi_made, 1)

                def half(i, b, front, back, ahead):
                    f, j = 1 - b, i + b
                    if front:
                        values(j, 0, f)
                        maxima(j, 0, f)
                        exponentials(j, 0, f, 0)
                    if back:
                        transposed_hi(i, 2, b)
                    if front:
                        exponentials(j, 0, f, 1)
                        exponentials(j, 0, f, 2)
                    if back:
                        queries(i, 1, b)
                    if front:
                        exponentials(j, 0, f, 3)
                        exponentials(j, 0, f, 4)
                    if back:
                        maxima(i, 1, b)
                        exponentials(i, 1, b, 0)
                    if front:
                        heads_hi(j, 0, f)
                    if back:
                        for u in range(1, 5):
                            exponentials(i, 1, b, u)
                    if front:
                        values(j, 1, f)
                    if ahead:
                        if b == 0:
                            context_hi(i + 1)
                    if front:
                        transposed_hi(j, 1, f)
                        squares_hi(j, f, 0)
                    if back:
                        heads_hi(i, 1, b)
                    if front:
                        squares_hi(j, f, 1)
                        squares_hi(j, f, 2)
                    if ahead:
                        transposed_hi(i + 1, 0, b)
                    if front:
                        squares_hi(j, f, 3)
                    if ahead:
                        keys(i + 1, b)
                        queries(i + 1, 0, b)
                    if back:
                        transposed_hi(i, 3, b)

                sc.preload_act_table(ACT.Exp)
                schedule(sc, half)

            @block.vector
            def _(v):
                def x_of(stage, c):
                    return x_mid[c] if stage else x_in[c]

                def layer_norm(i, stage, c):
                    statistics(i, stage, c)
                    aggregates(i, stage, c)
                    variances(i, stage, c)

                def statistics(i, stage, c):
                    g = group(stage)
                    if stage == 0:
                        v.wait_ge(x_loaded[c], at(i, 16, 15))
                    elif stage == 2:
                        v.wait_ge(x_fed[c], at(i, 1, 0))
                    else:
                        v.wait_ge(x_attended[c], at(i, 2, stage // 2))
                    for q in range(2):
                        ins = v.bn_stats(stats[g][c][:, q, :], x_of(stage, c)[:, q, :])
                    ins.then_inc(stats_made[g][c], 1)

                def aggregates(i, stage, c):
                    g = group(stage)
                    v.wait_ge(stats_made[g][c], at(i, *nth(stage)))
                    v.sem_inc(const["passed"], 1)
                    for q in range(2):
                        ins = v.bn_aggr(moments[g][c][:, q, :], stats[g][c][:, q, :])
                    ins.then_inc(moments_made[g][c], 1)

                def variances(i, stage, c):
                    g = group(stage)
                    v.wait_ge(moments_made[g][c], at(i, *nth(stage)))
                    v.tensor_scalar(var_eps[g][c][:], moments[g][c][:, :, 1], LN_EPS, None, ALU.add).then_inc(var_made[g][c], 1)

                def normalise(i, stage, c):
                    g = group(stage)
                    v.wait_ge(rstd_made[g][c], at(i, *nth(stage)))
                    for q in range(2):
                        ins = v.tensor_scalar(xn_of(stage, c)[:, q, :], x_of(stage, c)[:, q, :], moments[g][c][:, q, 0:1],
                                              rstd[g][c][:, q:q + 1], ALU.subtract, ALU.mult)
                    ins.then_inc(xn_made[g][c], 1)

                def transposed_lo(i, stage, c):
                    g, (hi, lo) = group(stage), xT_of(stage, c)
                    v.wait_ge(xT_hi_made[g][c], at(i, *nth(stage)))
                    v.tensor_tensor(flat(lo), bank("xT", stage, c, 0)[:], flat(hi).bitcast(F32), ALU.subtract).then_inc(xT_made[g][c], 1)

                def heads_lo(i, layer, c):
                    hi, lo = xT_of(1, c)
                    v.wait_ge(oT_hi_made[c], at(i, 2, layer))
                    v.tensor_tensor(flat(lo), bank("oT", layer, c, 0)[:], flat(hi).bitcast(F32), ALU.subtract).then_inc(oT_made[c], 1)

                def masks(i):
                    v.wait_ge(mrow_loaded, at(i, 16, 15))
                    v.tensor_scalar(mrow[:], mrow_i[:], 0.0, None, ALU.not_equal).then_inc(mask_made, 1)
                    v.wait_ge(mask_made, at(i, 1, 0))
                    v.tensor_scalar(neg_row[:], mrow[0:1], 1.0, NEG, ALU.subtract, ALU.mult).then_inc(neg_made, 1)
                    v.wait_ge(mcol_loaded, at(i, 16, 15))
                    v.tensor_scalar(neg_col[:], mcol_i[:], 0.0, -NEG, ALU.is_equal, ALU.mult).then_inc(neg_col_made, 1)

                def context_lo(i):
                    v.wait_ge(ctx_hi_made, at(i, 1, 0))
                    v.tensor_tensor(repeated(ctx_lo, 0), keys_of(ctxt, 0), repeated(ctx_hi, 0).bitcast(F32), ALU.subtract)
                    v.tensor_tensor(repeated(ctx_lo, 1), keys_of(ctxt, 1), repeated(ctx_hi, 1).bitcast(F32), ALU.subtract).then_inc(ctx_split, 1)

                def keys(i, layer):
                    v.wait_ge(kt_made, at(i, 2, layer))
                    if layer == 0:
                        v.wait_ge(mask_made, at(i, 1, 0))
                        v.tensor_tensor(kt[:], kt[:], mrow[:].unsqueeze(1).to_broadcast([P, 2, LANES, PAD]), ALU.mult).then_inc(kt_masked, 1)
                        v.wait_ge(kt_masked, at(i, 1, 0))
                    v.tensor_copy(k_hi[layer][:], kt[:]).then_inc(k_hi_made, 1)
                    v.wait_ge(k_hi_made, at(i, 2, layer))
                    v.wait_ge(kb_lo_made[1], before(i, 2, layer))
                    v.tensor_tensor(k_lo[layer][:], kt[:], k_hi[layer][:].bitcast(F32), ALU.subtract).then_inc(k_split, 1)

                def key_blocks_hi(i, layer, c):
                    v.wait_ge(k_hi_made, at(i, 2, layer))
                    kb, head = kb_hi[c], const["head"]
                    v.tensor_tensor(
                        kb[:, :, 0:GH * MAIN].rearrange("p g (h k) -> p g h k", k=MAIN),
                        k_hi[layer][:, :, c, 0:MAIN].bitcast(F32).unsqueeze(2).to_broadcast([P, 2, GH, MAIN]),
                        head[:].unsqueeze(1).unsqueeze(3).to_broadcast([P, 2, GH, MAIN]), ALU.mult)
                    v.tensor_tensor(
                        kb[:, :, GH * MAIN:].rearrange("p g (h k) -> p g h k", k=REST),
                        k_hi[layer][:, :, c, MAIN:PAD].bitcast(F32).unsqueeze(2).to_broadcast([P, 2, GH, REST]),
                        head[:].unsqueeze(1).unsqueeze(3).to_broadcast([P, 2, GH, REST]), ALU.mult).then_inc(kb_hi_made[c], 1)

                def values(i, layer, c):
                    v.wait_ge(v_main_made[c], at(i, 2, layer))
                    rest = v_blocks[c][:, :, 4 * GH * VC:].rearrange("p g (h v) -> p g h v", v=VC)
                    for g in range(2):
                        ins = v.tensor_tensor(rest[:, g, :, 0:HD], bank("V", layer, c, 0)[:, D + g * P:D + (g + 1) * P].rearrange("p (h d) -> p h d", d=HD),
                                              const["rest"][:].unsqueeze(2).to_broadcast([P, GH, HD]), ALU.mult)
                    ins.then_inc(v_made[c], 1)

                def queries(i, layer, c):
                    v.wait_ge(q_hi_made[c], at(i, 2, layer))
                    for g in range(2):
                        ins = v.scalar_tensor_tensor(q_lo[c][:, g, :], bank("Q", layer, c, 0)[:, g * S:(g + 1) * S],
                                                     const["bq"][:, layer, g:g + 1], q_hi[c][:, g, :].bitcast(F32), ALU.add, ALU.subtract)
                    ins.then_inc(q_made[c], 1)

                def maximum(i, layer, c, u):
                    wait_filled(v, i, "SA", layer, c, u)
                    scores = bank("SA", layer, c, u)
                    if u < 4:
                        q, g = u // 2, u % 2
                        v.tensor_reduce(max_main[c][:, q, g * GH:(g + 1) * GH], scores[:].rearrange("p (h k) -> p h k", k=MAIN),
                                        AX.X, ALU.max, negate=True).then_inc(maxima_made[c], 1)
                    else:
                        v.tensor_reduce(max_rest[c][:].rearrange("p q h -> p (q h)"), scores[:].rearrange("p (h k) -> p h k", k=REST),
                                        AX.X, ALU.max, negate=True).then_inc(maxima_made[c], 1)
                        v.wait_ge(maxima_made[c], at(i, 10, 5 * layer + 4))
                        v.tensor_tensor(neg_max[c][:], max_main[c][:], max_rest[c][:], ALU.min).then_inc(neg_max_made[c], 1)

                def divide(i, layer, c):
                    for q in range(2):
                        wait_filled(v, i, "PV", layer, c, q)
                        out = bank("PV", layer, c, q)[:, 0:HEADS * VC].rearrange("p (h v) -> p h v", v=VC)
                        v.reciprocal(inv_sum[c][:, q, :], out[:, :, HD]).then_inc(inv_made[c], 1)
                        v.wait_ge(inv_made[c], at(i, 4, 2 * layer + q))
                        v.tensor_tensor(xn_later[c][:, q, :].rearrange("p (h d) -> p h d", d=HD), out[:, :, 0:HD],
                                        inv_sum[c][:, q, :].unsqueeze(2).to_broadcast([P, HEADS, HD]), ALU.mult).then_inc(heads_made[c], 1)

                def attended(i, layer, c):
                    wait_filled(v, i, "O", layer, c, 0)
                    v.wait_ge(bias_added[c], at(i, 2, layer))
                    v.tensor_tensor(flat(x_mid[c]), bank("O", layer, c, 0)[:], flat(x_mid[c]), ALU.add).then_inc(x_attended[c], 1)

                def square(i, c, u):
                    v.wait_ge(relu_made[c], at(i, 4, u))
                    if u > 2:
                        v.wait_ge(sq_split[c], at(i, 4, u - 3))
                    v.tensor_tensor(sq[c][:, u % 3, :], relu[c][:, u % 2, :], relu[c][:, u % 2, :], ALU.mult).then_inc(sq_made[c], 1)

                def fed(i, c):
                    y = xn_later[c]
                    wait_filled(v, i, "down", 0, c, 0)
                    v.tensor_tensor(y[:], bank("down", 0, c, 0)[:].rearrange("p (q d) -> p q d", q=2),
                                    const["pj_scale"][:].unsqueeze(1).to_broadcast([P, 2, D]), ALU.mult).then_inc(y_made[c], 1)
                    v.wait_ge(y_made[c], at(i, 1, 0))
                    v.tensor_tensor(x_mid[c][:], x_mid[c][:], y[:], ALU.add).then_inc(x_fed[c], 1)

                def logits(i, c):
                    wait_filled(v, i, "gate", 0, c, 0)
                    v.tensor_tensor(ten["gates"][:, bass.ds(4 * i + 2 * c, 2), :], bank("gate", 0, c, 0)[:, 0:2 * E].rearrange("p (q e) -> p q e", e=E),
                                    const["gate_b"][:].unsqueeze(1).to_broadcast([P, 2, E]), ALU.add).then_inc(logits_made[c], 1)

                def half(i, b, front, back, ahead):
                    f, j = 1 - b, i + b
                    if back:
                        statistics(i, 2, b)
                    if front:
                        maximum(j, 0, f, 0)
                    if back:
                        aggregates(i, 2, b)
                    if front:
                        maximum(j, 0, f, 1)
                    if back:
                        variances(i, 2, b)
                    if front:
                        maximum(j, 0, f, 2)
                        maximum(j, 0, f, 3)
                        maximum(j, 0, f, 4)
                    if back:
                        normalise(i, 2, b)
                    if front:
                        values(j, 0, f)
                    if back:
                        key_blocks_hi(i, 1, b)
                        transposed_lo(i, 2, b)
                        queries(i, 1, b)
                        for u in range(5):
                            maximum(i, 1, b, u)
                    if front:
                        divide(j, 0, f)
                        heads_lo(j, 0, f)
                    if ahead:
                        layer_norm(i + 1, 0, b)
                    if front:
                        attended(j, 0, f)
                        layer_norm(j, 1, f)
                        normalise(j, 1, f)
                        values(j, 1, f)
                    if ahead:
                        normalise(i + 1, 0, b)
                        if b == 0:
                            masks(i + 1)
                            context_lo(i + 1)
                    if front:
                        transposed_lo(j, 1, f)
                    if back:
                        divide(i, 1, b)
                        heads_lo(i, 1, b)
                    if front:
                        square(j, f, 0)
                        square(j, f, 1)
                        square(j, f, 2)
                    if back:
                        attended(i, 1, b)
                        layer_norm(i, 3, b)
                    if ahead:
                        transposed_lo(i + 1, 0, b)
                    if front:
                        square(j, f, 3)
                    if back:
                        normalise(i, 3, b)
                    if ahead:
                        keys(i + 1, b)
                        key_blocks_hi(i + 1, 0, b)
                        queries(i + 1, 0, b)
                    if back:
                        transposed_lo(i, 3, b)
                    if front:
                        fed(j, f)
                    if back:
                        logits(i, b)

                schedule(v, half)

            @block.tensor
            def _(pe):
                def half(i, b, front, back, ahead):
                    f, j = 1 - b, i + b

                    def free(body, *key, waited=None):
                        wait_free(pe, body, ahead, waited, *key)

                    def transposes(body, stage, c):
                        key, src = ("xT", stage, c, 0), xn_of(stage, c)
                        pe.wait_ge(xn_made[group(stage)][c], at(body, *nth(stage)))
                        free(body, *key)
                        for t in range(DT):
                            for q in range(2):
                                ins = pe.transpose(bank(*key)[:, t * S + q * P:t * S + (q + 1) * P], src[:, q, t * P:(t + 1) * P], const["ident"][:])
                        ins.then_inc(fill(*key), 1)

                    def heads_transposed(body, layer, c):
                        key = ("oT", layer, c, 0)
                        pe.wait_ge(heads_made[c], at(body, 4, 2 * layer + 1))
                        free(body, *key, waited=heads_made[c])
                        for t in range(DT):
                            for q in range(2):
                                ins = pe.transpose(bank(*key)[:, t * S + q * P:t * S + (q + 1) * P], xn_later[c][:, q, t * P:(t + 1) * P], const["ident"][:])
                        ins.then_inc(fill(*key), 1)

                    def keys(body, layer):
                        key, wk, ctx_half = ("K", layer, 0, 0), w[f"k{layer}"], (ctx_hi, ctx_lo)
                        pe.wait_ge(ctx_split, at(body, 1, 0))
                        free(body, *key)
                        for g in range(2):
                            ins = three_products(pe, bank(*key)[:, g * LANES * PAD:(g + 1) * LANES * PAD].rearrange("p (c k) -> p c k", k=PAD),
                                                 lambda h, t: wk[:, h, t, g * P:(g + 1) * P], lambda h, t: ctx_half[h][:, t, :, MAIN:MAIN + PAD])
                        ins.then_inc(fill(*key), 1)

                    def values(body, layer, c):
                        key, wv, ctx_half = ("V", layer, c, 0), w[f"v{layer}"], (ctx_hi, ctx_lo)
                        free(body, *key)
                        three_products(pe, bank(*key)[:, 0:D], lambda h, t: ctx_half[h][:, t, c, 0:P], lambda h, t: wv[:, h, t, :])
                        three_products(pe, bank(*key)[:, D:2 * D], lambda h, t: ctx_half[h][:, t, c, P:2 * P],
                                       lambda h, t: wv[:, h, t, :]).then_inc(fill(*key), 1)

                    def queries(body, layer, c):
                        key, wq, xT = ("Q", layer, c, 0), w[f"q{layer}"], xT_of(2 * layer, c)
                        pe.wait_ge(xT_made[layer][c], at(body, *nth(2 * layer)))
                        free(body, *key)
                        for g in range(2):
                            ins = three_products(pe, bank(*key)[:, g * S:(g + 1) * S],
                                                 lambda h, t: wq[:, h, t, g * P:(g + 1) * P], lambda h, t: xT[h][:, t, :])
                        ins.then_inc(fill(*key), 1)

                    def scores_for_maxima(body, layer, c, units):
                        pe.wait_ge(q_made[c], at(body, 2, layer))
                        pe.wait_ge(kb_hi_made[c], at(body, 2, layer))
                        if layer == 0:
                            pe.wait_ge(neg_made, at(body, 1, 0))
                        for u in units:
                            key = ("SA", layer, c, u)
                            free(body, *key)
                            for q, g in [(u // 2, u % 2)] if u < 4 else [(0, 0), (0, 1), (1, 0), (1, 1)]:
                                width, keys0 = (MAIN, 0) if u < 4 else (REST, MAIN)
                                out = bank(*key)[:] if u < 4 else bank(*key)[:, (2 * q + g) * P:(2 * q + g + 1) * P]
                                cols = kb_hi[c][:, g, 0:GH * MAIN] if u < 4 else kb_hi[c][:, g, GH * MAIN:]
                                ins = pe.matmul(out, q_hi[c][:, g, q * P:(q + 1) * P], cols, start=True, stop=layer == 1)
                                if layer == 0:
                                    ins = pe.matmul(out.rearrange("p (h k) -> p h k", k=width), const["ones_row"][:],
                                                    neg_row[:, c, keys0:keys0 + width].unsqueeze(1).to_broadcast([1, GH, width]),
                                                    start=False, stop=True)
                            ins.then_inc(fill(*key), 1)

                    def maxima_transposed(body, layer, c):
                        key = ("mT", layer, c, 0)
                        pe.wait_ge(neg_max_made[c], at(body, 2, layer))
                        free(body, *key)
                        for q in range(2):
                            ins = pe.transpose(bank(*key)[0:HEADS, q * P:(q + 1) * P], neg_max[c][:, q, :], const["ident"][:])
                        ins.then_inc(fill(*key), 1)

                    def scores(body, layer, c, units):
                        kb, qT = (kb_hi[c], kb_lo[c]), (q_hi[c], q_lo[c])
                        for u in units:
                            key = ("SB", layer, c, u)
                            if u == 0:
                                pe.wait_ge(kb_lo_made[c], at(body, 2, layer))
                                pe.wait_ge(neg_maxT_made[c], at(body, 2, layer))
                            free(body, *key)
                            for h2 in range(2):
                                n = 2 * u + h2
                                g, t = (n // 4, n % 4) if u < 4 else (h2, 4)
                                out = bank(*key)[:, h2 * S:(h2 + 1) * S]
                                three_products(pe, out, lambda h, _: kb[h][:, g, t * P:(t + 1) * P], lambda h, _: qT[h][:, g, :], parts=1, last=False)
                                first = (g * GH + 2 * t) * MAIN if t < 4 else HEADS * MAIN + g * P
                                ins = pe.matmul(out, const["onehot"][:, first:first + P], neg_maxT[c][:], start=False, stop=True)
                            ins.then_inc(fill(*key), 1)

                    def outputs(body, layer, c, q):
                        key = ("PV", layer, c, q)
                        pe.wait_ge(v_made[c], at(body, 2, layer))
                        pe.wait_ge(prob_made[c], at(body, 10, 5 * layer + 4))
                        free(body, *key, waited=prob_made[c])
                        for g in range(2):
                            for t in range(5):
                                n = 4 * g + t if t < 4 else 8 + g
                                ins = pe.matmul(bank(*key)[:, g * GH * VC:(g + 1) * GH * VC], prob[c][:, n, q * P:(q + 1) * P],
                                                v_blocks[c][:, g, t * GH * VC:(t + 1) * GH * VC], start=t == 0, stop=t == 4)
                        ins.then_inc(fill(*key), 1)

                    def projection(body, layer, c):
                        key, wo, oT = ("O", layer, c, 0), w[f"o{layer}"], xT_of(1, c)
                        pe.wait_ge(oT_made[c], at(body, 2, layer))
                        free(body, *key, waited=oT_made[c])
                        for q in range(2):
                            ins = three_products(pe, bank(*key)[:, q * D:(q + 1) * D],
                                                 lambda h, t: oT[h][:, t, q * P:(q + 1) * P], lambda h, t: wo[:, h, t, :])
                        ins.then_inc(fill(*key), 1)

                    def up(body, c, units):
                        xT = xT_of(1, c)
                        for u in units:
                            key = ("up", 0, c, u)
                            if u == 0:
                                pe.wait_ge(xT_made[1][c], at(body, *nth(1)))
                            free(body, *key)
                            for h2 in range(2):
                                n = 2 * u + h2
                                ins = three_products(pe, bank(*key)[:, h2 * S:(h2 + 1) * S],
                                                     lambda h, t: w["fc"][:, h, t, n * P:(n + 1) * P], lambda h, t: xT[h][:, t, :])
                            ins.then_inc(fill(*key), 1)

                    def down(body, c):
                        key = ("down", 0, c, 0)
                        pe.wait_ge(sq_split[c], at(body, 4, 3))
                        free(body, *key)
                        for q in range(2):
                            for t in range(HT0):
                                for h, part in enumerate((sq_hi[c], sq_lo[c])):
                                    ins = pe.matmul(bank(*key)[:, q * D:(q + 1) * D], part[:, t, q * P:(q + 1) * P], w["pj"][:, t, :],
                                                    start=t == 0 and h == 0, stop=t == HT0 - 1 and h == 1)
                        ins.then_inc(fill(*key), 1)

                    def gate(body, c):
                        key, xT = ("gate", 0, c, 0), xT_of(3, c)
                        pe.wait_ge(xT_made[1][c], at(body, *nth(3)))
                        free(body, *key)
                        for q in range(2):
                            ins = three_products(pe, bank(*key)[:, q * E:(q + 1) * E],
                                                 lambda h, t: xT[h][:, t, q * P:(q + 1) * P], lambda h, t: w["gate"][:, h, t, :])
                        ins.then_inc(fill(*key), 1)

                    if front:
                        scores_for_maxima(j, 0, f, range(4))
                        values(j, 0, f)
                        scores_for_maxima(j, 0, f, [4])
                        maxima_transposed(j, 0, f)
                        scores(j, 0, f, [0])
                    if back:
                        transposes(i, 2, b)
                    if front:
                        scores(j, 0, f, [1, 2])
                    if back:
                        queries(i, 1, b)
                    if front:
                        scores(j, 0, f, [3, 4])
                    if back:
                        scores_for_maxima(i, 1, b, range(5))
                    if front:
                        outputs(j, 0, f, 0)
                    if back:
                        maxima_transposed(i, 1, b)
                    if front:
                        outputs(j, 0, f, 1)
                    if back:
                        scores(i, 1, b, [0])
                    if front:
                        heads_transposed(j, 0, f)
                    if back:
                        scores(i, 1, b, [1, 2])
                    if front:
                        projection(j, 0, f)
                    if back:
                        scores(i, 1, b, [3, 4])
                    if front:
                        values(j, 1, f)
                    if back:
                        outputs(i, 1, b, 0)
                    if front:
                        transposes(j, 1, f)
                    if back:
                        outputs(i, 1, b, 1)
                    if front:
                        up(j, f, [0])
                    if back:
                        heads_transposed(i, 1, b)
                    if front:
                        up(j, f, [1, 2])
                    if back:
                        projection(i, 1, b)
                    if ahead:
                        transposes(i + 1, 0, b)
                    if front:
                        up(j, f, [3])
                    if ahead:
                        keys(i + 1, b)
                        queries(i + 1, 0, b)
                    if back:
                        transposes(i, 3, b)
                    if front:
                        down(j, f)
                    if back:
                        gate(i, b)

                schedule(pe, half)


def routing(nc, ten, ps, const):
    with ExitStack() as ctx:
        def sb(name, shape, dt=F32):
            return ctx.enter_context(nc.sbuf_tensor(name, shape, dt))

        def sem(name):
            return ctx.enter_context(nc.semaphore(name))

        tiles = 2 * B
        full = [P, tiles, E]
        g = ten["gates"]
        key, rank, left, first_two = (sb(n, full) for n in ("key", "rank", "left", "first_two"))
        routes = sb("routes", [P, 2, B, E])
        top, best = sb("top", [P, tiles]), sb("best", [P, tiles])
        total, inv_total = sb("total", [P, 2, E]), sb("inv_total", [P, 2, E])
        rows = [sb(f"rows{h}", [P, S]) for h in range(2)]
        eight = [sb(f"eight{h}", [P, 8]) for h in range(2)]
        mark = {}
        ranked, dve, exped, turned = sem("ranked"), sem("route_dve"), sem("exped"), sem("routes_turned")

        def wide(t):
            return t[:].unsqueeze(2).to_broadcast(full)

        with nc.Block() as block:
            @block.gpsimd
            def _(pool):
                pool.iota(rank[:], pattern=[[0, tiles], [-1, E]], base=E, channel_multiplier=0,
                          allow_small_or_imprecise_dtypes=True).then_inc(ranked, 1)

            @block.scalar
            def _(sc):
                sc.wait_ge(dve, 2)
                sc.activation(g[:], g[:], ACT.Exp).then_inc(exped, 1)

            @block.vector
            def _(v):
                n = [0]

                def step(ins):
                    n[0] += 1
                    ins.then_inc(dve, 1)
                    v.wait_ge(dve, n[0])

                step(v.tensor_reduce(top[:], g[:], AX.X, ALU.max))
                step(v.tensor_tensor(g[:], g[:], wide(top), ALU.subtract))
                v.wait_ge(exped, 1)
                step(v.tensor_reduce(top[:], g[:], AX.X, ALU.add))
                step(v.reciprocal(best[:], top[:]))
                step(v.tensor_tensor(g[:], g[:], wide(best), ALU.mult))
                v.wait_ge(ranked, 1)
                for pick in range(2):
                    src = g if pick == 0 else left
                    step(v.tensor_reduce(top[:], src[:], AX.X, ALU.max))
                    step(v.tensor_tensor(key[:], src[:], wide(top), ALU.is_equal))
                    step(v.tensor_tensor(key[:], key[:], rank[:], ALU.mult))
                    step(v.tensor_reduce(best[:], key[:], AX.X, ALU.max))
                    step(v.tensor_tensor(key[:], key[:], wide(best), ALU.is_equal))
                    if pick == 0:
                        step(v.tensor_copy(first_two[:], key[:]))
                        step(v.scalar_tensor_tensor(left[:].rearrange("p t e -> p (t e)"), key[:].rearrange("p t e -> p (t e)"), -4.0,
                                                    g[:].rearrange("p t e -> p (t e)"), ALU.mult, ALU.add))
                    else:
                        step(v.tensor_tensor(first_two[:], first_two[:], key[:], ALU.add))
                step(v.tensor_tensor(g[:], g[:], first_two[:], ALU.mult))
                step(v.tensor_reduce(total[:], g[:].rearrange("p (b q) e -> p q e b", q=2), AX.X, ALU.add))
                step(v.tensor_scalar(total[:], total[:], 1e-6, None, ALU.add))
                step(v.reciprocal(inv_total[:], total[:]))
                step(v.tensor_scalar(inv_total[:], inv_total[:], CAPACITY, None, ALU.mult))
                for q in range(2):
                    v.tensor_tensor(routes[:, q], g[:].rearrange("p (b q) e -> p q b e", q=2)[:, q],
                                    inv_total[:, q, :].unsqueeze(1).to_broadcast([P, B, E]), ALU.mult).then_inc(dve, 1)
                n[0] += 2
                mark["routed"] = n[0]
                v.wait_ge(turned, 1)
                for h in range(2):
                    step(v.tensor_copy(rows[h][:], ps[h][:, 0:S]))
                for r in range(CHOSEN // 8):
                    for h in range(2):
                        v.max(eight[h][:], rows[h][:]).then_inc(dve, 1)
                    for h in range(2):
                        n[0] += 1
                        v.wait_ge(dve, n[0] + h)
                        v.match_replace(rows[h][:], eight[h][:], rows[h][:], -1.0).then_inc(dve, 1)
                    n[0] += 2
                    v.wait_ge(dve, n[0])
                for h in range(2):
                    step(v.tensor_scalar(ten["chosen"][:, h, :], rows[h][:], 0.0, None, ALU.is_lt))

            @block.tensor
            def _(pe):
                pe.wait_ge(dve, mark["routed"])
                for h in range(2):
                    for q in range(2):
                        src = routes[:, q, h * 16:(h + 1) * 16, :].rearrange("p b e -> p (b e)")
                        ins = pe.transpose(ps[h][:, q * P:(q + 1) * P], src, const["ident"][:])
                ins.then_inc(turned, 1)


def experts(nc, ten, ps, const, dram):
    with ExitStack() as ctx:
        def sb(name, shape, dt=F32):
            return ctx.enter_context(nc.sbuf_tensor(name, shape, dt))

        def sem(name):
            return ctx.enter_context(nc.semaphore(name))

        def two(name, shape, dt=F32):
            return [sb(f"{name}_{n}", shape, dt) for n in range(2)]

        w1_raw, w2_raw, b2_raw = sb("w1_raw", [P, DT, E * SUB]), sb("w2_raw", [P, HT1, D]), sb("b2_raw", [E, D])
        w1, w2 = sb("w1", [P, 2, DT, E * SUB], F32R), sb("w2", [P, 2, HT1, D], F32R)
        b1, b2 = sb("b1", [P, HT1]), sb("b2", [E, 2, D], F32R)
        pick, spread = sb("pick", [P, 2 * P], BF16), sb("spread", [P, P * SUB], BF16)
        x = [sb(f"x_expert{c}", [P, 2, D]) for c in range(SLOTS)]
        stats, moments, var_eps, rstd = two("e_stats", [P, 2, 6]), two("e_moments", [P, 2, 2]), two("e_var_eps", [P, 2]), two("e_rstd", [P, 2])
        xn, xT_hi, xT_lo = two("e_xn", [P, 2, D]), two("e_xT_hi", [P, DT, S], F32R), two("e_xT_lo", [P, DT, S], F32R)
        gelu, hid = two("gelu", [P, HT1, S]), two("hid", [P, HT1, S])
        hid_hi, hid_lo = two("hid_hi", [P, HT1, S], F32R), two("hid_lo", [P, HT1, S], F32R)
        sel8 = two("sel8", [E, S], F32R)

        per_group = {}

        def loop_sem(name, n):
            per_group[name] = (sem(name), n)
            return per_group[name][0]

        x_loaded, x_stored = ([loop_sem(f"{n}{c}", 16) for c in range(SLOTS)] for n in ("e_x_loaded", "e_x_stored"))
        stats_made, moments_made, var_made, rstd_made, xn_made, xT_hi_made, xT_made = (loop_sem(n, SLOTS) for n in (
            "e_stats_made", "e_moments_made", "e_var_made", "e_rstd_made", "e_xn_made", "e_xT_hi_made", "e_xT_made"))
        sel8_made, x_made = loop_sem("sel8_made", SLOTS), loop_sem("x4_made", SLOTS)
        xT_filled, sel8_filled, down_filled = loop_sem("e_xT_filled", SLOTS), loop_sem("sel8_filled", SLOTS), loop_sem("e_down_filled", SLOTS)
        gelu_made, hid_made, hid_hi_made, hid_split = (loop_sem(n, 2 * SLOTS) for n in ("gelu_made", "hid_made", "hid_hi_made", "hid_split"))
        sel_filled, up_filled = loop_sem("sel_filled", 2 * SLOTS), loop_sem("e_up_filled", 2 * SLOTS)
        loaded, tables_made, prep = sem("e_loaded"), sem("e_tables_made"), sem("e_prep")

        sel_bank, up_bank, xT_bank, down_bank = ps[0:2], ps[2:4], ps[4:6], ps[6:8]

        def one(i, c):
            return at(i, SLOTS, c)

        def of_pair(i, c, u):
            return at(i, 2 * SLOTS, 2 * c + u)

        def later(i, c, turns):
            return i + (c + turns) // SLOTS, (c + turns) % SLOTS

        def pair(t, u):
            return t[:, 2 * u:2 * u + 2, :].rearrange("p t s -> p (t s)")

        def flat(t):
            return t[:].rearrange("p t s -> p (t s)")

        def schedule(eng, turn):
            turn(-1, SLOTS - 2, lambda n: n == 2)
            turn(-1, SLOTS - 1, lambda n: n > 0)
            with eng.Fori(0, GROUPS - 1) as i:
                for c in range(SLOTS):
                    turn(i, c, lambda n: True)
            for c in range(SLOTS):
                turn(GROUPS - 1, c, lambda n, c=c: c + n < SLOTS)

        with nc.Block() as block:
            @block.sync
            def _(sp):
                for s, n in per_group.values():
                    sp.sem_inc(s, n)
                sp.dma_start(w1_raw[:], dram["W1"].rearrange("(t p) n -> p t n", p=P)).then_inc(loaded, 16)
                sp.dma_start(w2_raw[:], dram["W2"].rearrange("(t p) n -> p t n", p=P)).then_inc(loaded, 16)
                sp.dma_start(b1[:], dram["b1"]).then_inc(loaded, 16)
                sp.dma_start(b2_raw[:], dram["b2"]).then_inc(loaded, 16)

            @block.gpsimd
            def _(pool):
                pool.memset(pick[:], 1.0).then_inc(tables_made, 1)
                pool.wait_ge(tables_made, 1)
                pool.affine_select(out=pick[:], in_=pick[:], compare_op=ALU.is_equal, fill=0.0, base=0,
                                   pattern=[[-1, 2 * P]], channel_multiplier=1).then_inc(tables_made, 1)
                pool.wait_ge(tables_made, 2)
                pool.tensor_copy(spread[:, P * SUB // 2:].rearrange("p (r k) -> p r k", k=SUB),
                                 pick[:, P // 2:P].unsqueeze(2).to_broadcast([P, P // 2, SUB])).then_inc(tables_made, 1)

            @block.scalar
            def _(sc):
                sc.wait_ge(tables_made, 2)
                sc.copy(spread[:, 0:P * SUB // 2].rearrange("p (r k) -> p r k", k=SUB),
                        pick[:, 0:P // 2].unsqueeze(2).to_broadcast([P, P // 2, SUB])).then_inc(tables_made, 1)

            @block.vector
            def _(v):
                n = [0]

                def step(ins):
                    n[0] += 1
                    ins.then_inc(prep, 1)
                    v.wait_ge(prep, n[0])

                def split(hi, lo, src):
                    step(v.tensor_copy(hi, src))
                    step(v.tensor_tensor(lo, src, hi.bitcast(F32), ALU.subtract))

                v.wait_ge(loaded, 64)
                step(v.tensor_scalar(w2_raw[:], w2_raw[:], const["gain"][:, 3:4], None, ALU.mult))
                step(v.tensor_scalar(b2_raw[:], b2_raw[:], const["gain"][0:E, 3:4], None, ALU.mult))
                split(w1[:, 0], w1[:, 1], w1_raw[:])
                split(w2[:, 0], w2[:, 1], w2_raw[:])
                split(b2[:, 0], b2[:, 1], b2_raw[:])

        with nc.Block() as block:
            @block.sync
            def _(sp):
                def rows(name, i, c):
                    body = 2 * i + c // 2
                    t = dram[name][body] if isinstance(i, int) else dram[name][bass.ds(body, 1)].squeeze(0)
                    return t[:, 2 * (c % 2):2 * (c % 2) + 2, :]

                def load(i, c):
                    sp.dma_start(x[c][:], rows("x3", i, c)).then_inc(x_loaded[c], 16)

                def store(i, c):
                    sp.wait_ge(x_made, one(i, c))
                    sp.dma_start(rows("out", i, c), x[c][:]).then_inc(x_stored[c], 16)

                for c in range(SLOTS):
                    load(0, c)
                with sp.Fori(0, GROUPS - 1) as i:
                    store(i, 0)
                    for c in range(1, SLOTS):
                        store(i, c)
                        sp.wait_ge(x_stored[c - 1], at(i, 16, 15))
                        load(i + 1, c - 1)
                    sp.wait_ge(x_stored[SLOTS - 1], at(i, 16, 15))
                    load(i + 1, SLOTS - 1)
                for c in range(SLOTS):
                    store(GROUPS - 1, c)
                for c in range(SLOTS):
                    sp.wait_ge(x_stored[c], 16 * (GROUPS + 1))

            @block.gpsimd
            def _(pool):
                def turn(i, c, has):
                    if has(2):
                        j, d = later(i, c, 2)
                        pool.wait_ge(var_made, one(j, d))
                        pool.tensor_tensor(rstd[d % 2][:], var_eps[d % 2][:], const["minus_half"][:], ALU.pow).then_inc(rstd_made, 1)
                    if has(1):
                        j, d = later(i, c, 1)
                        for u in range(2):
                            pool.wait_ge(hid_hi_made, of_pair(j, d, u))
                            pool.tensor_tensor(pair(hid_lo[d % 2], u), pair(hid[d % 2], u), pair(hid_hi[d % 2], u).bitcast(F32),
                                               ALU.subtract).then_inc(hid_split, 1)

                schedule(pool, turn)

            @block.scalar
            def _(sc):
                def turn(i, c, has):
                    if has(1):
                        j, d = later(i, c, 1)
                        sc.wait_ge(sel8_filled, one(j, d))
                        sc.copy(sel8[d % 2][:], down_bank[d % 2][0:E, 0:S]).then_inc(sel8_made, 1)
                        for u in range(2):
                            sc.wait_ge(up_filled, of_pair(j, d, u))
                            for h in range(2):
                                t = 2 * u + h
                                ins = sc.activation(gelu[d % 2][:, t, :], up_bank[u][:, h * S:(h + 1) * S], ACT.Gelu, bias=b1[:, t:t + 1])
                            ins.then_inc(gelu_made, 1)
                        sc.wait_ge(hid_made, of_pair(j, d, 0))
                        sc.copy(pair(hid_hi[d % 2], 0), pair(hid[d % 2], 0)).then_inc(hid_hi_made, 1)
                    if has(2):
                        k, e = later(i, c, 2)
                        sc.wait_ge(xT_filled, one(k, e))
                        sc.copy(flat(xT_hi[e % 2]), xT_bank[e % 2][:]).then_inc(xT_hi_made, 1)
                    if has(1):
                        sc.wait_ge(hid_made, of_pair(j, d, 1))
                        sc.copy(pair(hid_hi[d % 2], 1), pair(hid[d % 2], 1)).then_inc(hid_hi_made, 1)

                sc.preload_act_table(ACT.Gelu)
                schedule(sc, turn)

            @block.vector
            def _(v):
                def layer_norm(i, c):
                    n = c % 2
                    v.wait_ge(x_loaded[c], at(i, 16, 15))
                    for q in range(2):
                        ins = v.bn_stats(stats[n][:, q, :], x[c][:, q, :])
                    ins.then_inc(stats_made, 1)
                    v.wait_ge(stats_made, one(i, c))
                    v.sem_inc(const["passed"], 1)
                    for q in range(2):
                        ins = v.bn_aggr(moments[n][:, q, :], stats[n][:, q, :])
                    ins.then_inc(moments_made, 1)
                    v.wait_ge(moments_made, one(i, c))
                    v.tensor_scalar(var_eps[n][:], moments[n][:, :, 1], LN_EPS, None, ALU.add).then_inc(var_made, 1)

                def normalise(i, c):
                    n = c % 2
                    v.wait_ge(rstd_made, one(i, c))
                    for q in range(2):
                        ins = v.tensor_scalar(xn[n][:, q, :], x[c][:, q, :], moments[n][:, q, 0:1], rstd[n][:, q:q + 1], ALU.subtract, ALU.mult)
                    ins.then_inc(xn_made, 1)

                def masked(i, c, u):
                    v.wait_ge(gelu_made, of_pair(i, c, u))
                    v.wait_ge(sel_filled, of_pair(i, c, u))
                    v.tensor_tensor(pair(hid[c % 2], u), sel_bank[u][:], pair(gelu[c % 2], u), ALU.mult).then_inc(hid_made, 1)

                def turn(i, c, has):
                    j, d = later(i, c, 1)
                    k, e = later(i, c, 2)
                    if has(2):
                        layer_norm(k, e)
                    if has(1):
                        masked(j, d, 0)
                    if has(2):
                        normalise(k, e)
                    if has(1):
                        masked(j, d, 1)
                    if has(2):
                        v.wait_ge(xT_hi_made, one(k, e))
                        v.tensor_tensor(flat(xT_lo[e % 2]), xT_bank[e % 2][:], flat(xT_hi[e % 2]).bitcast(F32), ALU.subtract).then_inc(xT_made, 1)
                    if has(0):
                        v.wait_ge(down_filled, one(i, c))
                        v.tensor_tensor(flat(x[c]), down_bank[c % 2][:], flat(x[c]), ALU.add).then_inc(x_made, 1)

                schedule(v, turn)

            @block.tensor
            def _(pe):
                def choices(i, c, half):
                    row = 8 * (SLOTS * i + c) - P * half
                    for u in range(2):
                        j, d = later(i, c, -1)
                        pe.wait_ge(hid_made, of_pair(j, d, u))
                        for h in range(2):
                            first = (row + 2 * (2 * u + h)) * SUB
                            ins = pe.matmul(sel_bank[u][:, h * S:(h + 1) * S], spread[:, bass.ds(first, P)], ten["chosen"][:, half, :],
                                            start=True, stop=True)
                        ins.then_inc(sel_filled, 1)
                    j, d = later(i, c, -2)
                    pe.wait_ge(x_made, one(j, d))
                    pe.matmul(down_bank[c % 2][:, 0:S], pick[:, bass.ds(row, P)], ten["chosen"][:, half, :],
                              start=True, stop=True).then_inc(sel8_filled, 1)

                def up(i, c):
                    xT = (xT_hi[c % 2], xT_lo[c % 2])
                    pe.wait_ge(xT_made, one(i, c))
                    for u in range(2):
                        j, d = later(i, c, -1)
                        pe.wait_ge(gelu_made, of_pair(j, d, u))
                        for h in range(2):
                            n = 2 * u + h
                            ins = three_products(pe, up_bank[u][:, h * S:(h + 1) * S],
                                                 lambda a, t: w1[:, a, t, n * P:(n + 1) * P], lambda a, t: xT[a][:, t, :])
                        ins.then_inc(up_filled, 1)

                def transposes(i, c):
                    pe.wait_ge(xn_made, one(i, c))
                    for t in range(DT):
                        for q in range(2):
                            ins = pe.transpose(xT_bank[c % 2][:, t * S + q * P:t * S + (q + 1) * P], xn[c % 2][:, q, t * P:(t + 1) * P], const["ident"][:])
                    ins.then_inc(xT_filled, 1)

                def down(i, c, q):
                    hh = (hid_hi[c % 2], hid_lo[c % 2])
                    if q == 0:
                        pe.wait_ge(hid_split, of_pair(i, c, 1))
                        pe.wait_ge(sel8_made, one(i, c))
                    out = down_bank[c % 2][:, q * D:(q + 1) * D]
                    three_products(pe, out, lambda a, t: hh[a][:, t, q * P:(q + 1) * P], lambda a, t: w2[:, a, t, :], parts=HT1, last=False)
                    for a in range(2):
                        ins = pe.matmul(out, sel8[c % 2][:, q * P:(q + 1) * P], b2[:, a, :], start=False, stop=a == 1)
                    return ins

                def turn(i, c, has, half):
                    j, d = later(i, c, 1)
                    k, e = later(i, c, 2)
                    if has(1):
                        choices(j, d, half)
                        up(j, d)
                    if has(0):
                        down(i, c, 0)
                    if has(2):
                        transposes(k, e)
                    if has(0):
                        down(i, c, 1).then_inc(down_filled, 1)

                turn(-1, SLOTS - 2, lambda n: n == 2, 0)
                turn(-1, SLOTS - 1, lambda n: n > 0, 0)
                for half in range(2):
                    last = (half + 1) * GROUPS // 2 - 1
                    with pe.Fori(half * GROUPS // 2, last) as i:
                        for c in range(SLOTS):
                            turn(i, c, lambda n: True, half)
                    for c in range(SLOTS):
                        turn(last, c, lambda n, c=c: half == 0 or c + n < SLOTS, half if c + 1 < SLOTS else 1)


def program(nc, dram):
    with ExitStack() as ctx:
        def sb(name, shape, dt=F32):
            return ctx.enter_context(nc.sbuf_tensor(name, shape, dt))

        ps = [ctx.enter_context(nc.psum_tensor(f"bank{b}", [P, 512], F32)) for b in range(8)]
        const = {"ident": sb("ident", [P, P]), "minus_half": sb("minus_half", [P, 2]), "gain": sb("gain", [P, 4]),
                 "passed": ctx.enter_context(nc.semaphore("passed"))}
        ten = {"gates": sb("gates", [P, 2 * B, E]), "chosen": sb("chosen", [P, 2, S], BF16)}
        with ExitStack() as inner:
            def sbi(name, shape, dt=F32):
                return inner.enter_context(nc.sbuf_tensor(name, shape, dt))

            ten["V_blocks"] = [sbi(f"v_blocks{c}", [P, 2, 5 * GH * VC]) for c in range(LANES)]
            w = {f"{m}{layer}": sbi(f"w_{m}{layer}", [P, 2, DT, D], F32R) for layer in range(2) for m in "qkvo"}
            w["fc"] = sbi("w_fc", [P, 2, DT, HID0], F32R)
            w["pj"] = sbi("w_pj", [P, HT0, D], F32R)
            w["gate"] = sbi("w_gate", [P, 2, DT, E], F32R)
            const.update(
                head=sbi("head_mask", [P, GH]), rest=sbi("rest_mask", [P, GH]), bq=sbi("bq", [P, 2, DT]), bk=sbi("bk", [P, 2, DT]),
                bo=sbi("bo", [P, 2, D]), pj_scale=sbi("pj_scale", [P, D]), gate_b=sbi("gate_b", [P, E]),
                onehot=sbi("onehot", [HEADS, HEADS * PAD], F32R), ones_row=sbi("ones_row", [1, P], F32R))
            prepare(nc, ten, ps, w, const, dram)
            layers(nc, ten, ps, w, const, dram)
        routing(nc, ten, ps, const)
        experts(nc, ten, ps, const, dram)


def kernel(**inputs):
    import numpy as np
    import concourse.bacc as bacc
    from concourse.bass_utils import run_bass_kernel_spmd as run

    def a(name):
        return np.asarray(inputs[name])

    def padded(t):
        return np.concatenate([t, t[:, :PAD - KEYS]], axis=1)

    def tokens(t):
        return t.reshape(BODIES, LANES, 2, P, D).transpose(0, 3, 1, 2, 4).reshape(BODIES, P, 2 * LANES, D)

    def columns(t):
        return t.reshape(-1, P).T

    mask = padded(a("mask_Bx1x1xS2_if1").reshape(B, KEYS))
    main = np.concatenate([mask[:, 0:MAIN]] * 2, axis=1)
    rest = np.concatenate([mask[:, MAIN:]] * GH, axis=1)
    arrays = {
        "x": tokens(a("x")),
        "ctxT": padded(a("ctx_1024")).reshape(BODIES, LANES, PAD, DT, P).transpose(0, 4, 3, 1, 2),
        "mask_row": mask.reshape(BODIES, LANES, PAD),
        "mask_col": np.stack([main, rest], axis=-1).reshape(BODIES, LANES, P, 2).transpose(0, 2, 1, 3),
        "g_xattn": a("g_xattn"), "g_ffn": a("g_ffn"), "gate": a("L0_ffn_gate").reshape(1),
        "fcT": a("L0_ffn_w_fc").T, "pjT": a("L0_ffn_w_proj").T, "fast_b": a("L0_ffn_fast_b"), "uT": a("L0_ffn_u").T, "v": a("L0_ffn_v"),
        "w_gate": a("L1_ffn_w_gate_w"), "gate_b": a("L1_ffn_w_gate_b"),
        "W1": a("L1_ffn_W1").transpose(1, 0, 2).reshape(D, E * SUB), "b1": columns(a("L1_ffn_b1").reshape(-1)),
        "W2": a("L1_ffn_W2").reshape(E * SUB, D), "b2": a("L1_ffn_b2"),
    }
    for layer in range(2):
        for m in "qkvo":
            arrays[f"L{layer}_W{m}T"] = a(f"L{layer}_xattn_W{m}").T
            bias = a(f"L{layer}_xattn_b{m}")
            arrays[f"L{layer}_b{m}"] = bias if m == "o" else columns(bias)
    nc = bacc.Bacc("TRN2", target_bir_lowering=False, num_devices=1)
    arrays = {f"in_{n}": np.ascontiguousarray(t) for n, t in arrays.items()}
    dram = {n[3:]: nc.dram_tensor(n, t.shape, mybir.dt.from_np(t.dtype), kind="ExternalInput").ap() for n, t in arrays.items()}
    dram["x3"] = nc.dram_tensor("x3_scratch", (BODIES, P, 2 * LANES, D), F32, kind="Internal").ap()
    dram["out"] = nc.dram_tensor("out_0", (BODIES, P, 2 * LANES, D), F32, kind="ExternalOutput").ap()
    program(nc, dram)
    got = run(nc, [arrays], core_ids=[0]).results[0]["out_0"]
    return got.reshape(BODIES, P, LANES, 2, D).transpose(0, 2, 3, 1, 4).reshape(B, S, D)
```

```python
from contextlib import ExitStack

import concourse.bass as bass
from concourse import mybir

F32 = mybir.dt.float32
F32R = mybir.dt.float32r
BF16 = mybir.dt.bfloat16
I32 = mybir.dt.int32
ACT = mybir.ActivationFunctionType
ALU = mybir.AluOpType
AX = mybir.AxisListType

P = 128
B, S, D = 32, 256, 256
KEYS, MAIN, REST = 77, 64, 16
PAD = MAIN + REST
HEADS, HD = 16, 16
GH = P // HD
DT = D // P
HID0, HT0 = 1024, 8
RANK = 16
E, SUB = 8, 64
HT1 = E * SUB // P
CHOSEN = S // 2
CAPACITY = float(B)
BODIES = B // 2
LANES = 2
SLOTS = 4
GROUPS = B // SLOTS
VC = HD + 1
NEG = 1e9
LN_EPS = 1e-5


def at(i, per_body, k):
    return i * per_body + (per_body + k + 1)


def before(i, per_body, k):
    return i * per_body + (k + 1)


class Banks:

    def __init__(self, walk, first_bank):
        self.bank, self.users = {}, {}
        for n, (key, ahead) in enumerate(walk):
            self.bank[key] = first_bank + n % 4
            self.users.setdefault(self.bank[key], []).append((key, ahead))

    def previous(self, key, with_next):
        users = self.users[self.bank[key]]
        n = [k for k, _ in users].index(key)
        ahead = users[n][1]
        for m in range(n - 1, -len(users) - 1, -1):
            other, other_ahead = users[m]
            wrapped = m < 0
            if with_next or wrapped or other_ahead < 1:
                return other, ahead - other_ahead + wrapped


def front_walk():
    for c in range(LANES):
        yield ("mT", 0, c, 0), 0
        yield from ((("SB", 0, c, u), 0) for u in range(5))
        yield from ((("PV", 0, c, q), 0) for q in range(2))
        yield ("V", 1, c, 0), 0
        yield ("oT", 0, c, 0), 0
        yield ("O", 0, c, 0), 0
        yield ("xT", 1, c, 0), 0
        yield from ((("up", 0, c, u), 0) for u in range(4))
        yield ("V", 0, 1 - c, 0), c
        yield ("down", 0, c, 0), 0


def back_walk():
    for c in range(LANES):
        yield ("xT", 3, 1 - c, 0), c - 1
        yield ("xT", 2, c, 0), 0
        yield ("gate", 0, 1 - c, 0), c - 1
        yield ("Q", 1, c, 0), 0
        yield from ((("SA", 1, c, u), 0) for u in range(5))
        yield ("mT", 1, c, 0), 0
        yield from ((("SB", 1, c, u), 0) for u in range(5))
        yield ("K", c, 0, 0), 1
        yield ("PV", 1, c, 0), 0
        yield ("xT", 0, c, 0), 1
        yield ("PV", 1, c, 1), 0
        yield ("oT", 1, c, 0), 0
        yield ("Q", 0, c, 0), 1
        yield ("O", 1, c, 0), 0
        yield from ((("SA", 0, c, u), 1) for u in range(5))


def three_products(pe, out, lhs, rhs, parts=DT, first=True, last=True):
    n = 3 * parts
    for j in range(parts):
        for m, (a, b) in enumerate(((0, 0), (0, 1), (1, 0))):
            k = 3 * j + m
            ins = pe.matmul(out, lhs(a, j), rhs(b, j), start=first and k == 0, stop=last and k == n - 1)
    return ins


def prepare(nc, ten, ps, w, const, dram):
    with ExitStack() as ctx:
        def sb(name, shape, dt=F32):
            return ctx.enter_context(nc.sbuf_tensor(name, shape, dt))

        def sem(name):
            return ctx.enter_context(nc.semaphore(name))

        names = [f"{m}{layer}" for layer in range(2) for m in "qkvo"]
        raw = {n: sb(f"raw_{n}", [P, DT, D]) for n in names}
        fc, fc_abs = sb("raw_fc", [P, DT, HID0]), sb("fc_abs", [P, DT, HID0])
        pj, pj_abs = sb("raw_pj", [P, HT0, D]), sb("pj_abs", [P, HT0, D])
        fc_scale = sb("fc_scale", [P, HID0])
        fc_half, pj_half = sb("fc_half", [P, HID0]), sb("pj_half", [P, D])
        fast, uT, vr, fu = sb("fast", [RANK, RANK]), sb("uT", [RANK, HID0]), sb("vr", [RANK, D]), sb("fu", [RANK, HID0])
        gate, gx = sb("gate", [P, 1]), sb("gx", [P, 4])
        wg = sb("wg_raw", [P, DT, E])
        bvc, bvb, bo = sb("bvc", [P, 2, DT]), sb("bvb", [P, 2, DT, P]), sb("bo_raw", [P, 2, D])
        ones, ohf, kb = sb("ones", [P, P]), sb("ohf", [HEADS, HEADS * MAIN + HEADS * REST]), sb("kb_raw", [P, 2, DT])
        loaded, made, dve, act, pe_s = sem("w_loaded"), sem("tables_made"), sem("prep_dve"), sem("prep_act"), sem("prep_pe")
        ffn_loaded = sem("ffn_loaded")
        mark = {}
        tables = 6 + 10 + LANES * 5

        loads = [(raw[n][:], dram[f"L{n[1]}_W{n[0]}T"].rearrange("(t p) n -> p t n", p=P)) for n in names]
        ffn_loads = [(fc[:], dram["fcT"].rearrange("(t p) n -> p t n", p=P)),
                     (pj[:], dram["pjT"].rearrange("(t p) n -> p t n", p=P))]
        loads += [(fast[:], dram["fast_b"]), (uT[:], dram["uT"]), (vr[:], dram["v"]),
                  (gate[:], dram["gate"].partition_broadcast(P)), (gx[:, 0:2], dram["g_xattn"].partition_broadcast(P)),
                  (gx[:, 2:4], dram["g_ffn"].partition_broadcast(P)),
                  (wg[:], dram["w_gate"].rearrange("(t p) n -> p t n", p=P)),
                  (const["gate_b"][:], dram["gate_b"].partition_broadcast(P))]
        for layer in range(2):
            loads += [(const["bq"][:, layer, :], dram[f"L{layer}_bq"]), (kb[:, layer, :], dram[f"L{layer}_bk"]),
                      (bvc[:, layer, :], dram[f"L{layer}_bv"]),
                      (bo[:, layer, :], dram[f"L{layer}_bo"].partition_broadcast(P))]

        with nc.Block() as block:
            @block.sync
            def _(sp):
                for dst, src in loads:
                    sp.dma_start(dst, src).then_inc(loaded, 16)

            @block.vector
            def _(v):
                n = [0]

                def step(ins):
                    n[0] += 1
                    ins.then_inc(dve, 1)
                    v.wait_ge(dve, n[0])

                def split(hi, lo, src):
                    step(v.tensor_copy(hi, src))
                    step(v.tensor_tensor(lo, src, hi.bitcast(F32), ALU.subtract))

                v.wait_ge(loaded, 16 * len(loads))
                v.wait_ge(made, tables)
                step(v.tensor_copy(bvb[:], bvc[:].unsqueeze(3).to_broadcast([P, 2, DT, P])))
                mark["bv"] = n[0]
                for name in names:
                    if name[0] != "o":
                        split(w[name][:, 0], w[name][:, 1], raw[name][:])
                split(w["gate"][:, 0], w["gate"][:, 1], wg[:])
                step(v.tensor_scalar(const["bk"][:], kb[:], HD ** -0.5, None, ALU.mult))
                step(v.tensor_copy(const["onehot"][:], ohf[:]))
                v.wait_ge(pe_s, 2)
                for j in range(2):
                    v.tensor_scalar(fc_scale[:, j * 512:(j + 1) * 512], ps[j][:], 1.0 / D, 1e-5, ALU.mult, ALU.max)
                step(v.tensor_scalar(const["pj_scale"][:], ps[2][:, 0:D], 1.0 / HID0, 1e-5, ALU.mult, ALU.max))
                mark["scales"] = n[0]
                v.tensor_copy(fu[:, 0:512], ps[3][0:RANK, :])
                step(v.tensor_copy(fu[:, 512:1024], ps[4][0:RANK, :]))
                mark["fu"] = n[0]
                step(v.tensor_scalar(fc_half[:], fc_scale[:], 0.5, None, ALU.mult))
                step(v.tensor_scalar(pj_half[:], const["pj_scale"][:], 0.5, None, ALU.mult))
                v.wait_ge(act, 5)
                wide = [P, DT, HID0]
                step(v.tensor_tensor(fc_abs[:], fc_abs[:], fc_half[:].unsqueeze(1).to_broadcast(wide), ALU.is_gt))
                step(v.tensor_tensor(fc_abs[:], fc_abs[:], fc[:], ALU.mult))
                mark["ternary"] = n[0]
                step(v.tensor_tensor(pj_abs[:], pj_abs[:], pj_half[:].unsqueeze(1).to_broadcast([P, HT0, D]), ALU.is_gt))
                step(v.tensor_tensor(w["pj"][:], pj_abs[:], pj[:], ALU.mult))
                v.wait_ge(act, 6)
                step(v.tensor_scalar(const["pj_scale"][:], const["pj_scale"][:], const["gain"][:, 2:3], None, ALU.mult))
                v.wait_ge(made, tables + 1)
                for j in range(2):
                    v.wait_ge(pe_s, 4 + j)
                    for t in range(DT):
                        part = fc[:, t, j * 512:(j + 1) * 512]
                        v.scalar_tensor_tensor(part, ps[(6, 0)[j] + t][:], gate[:, 0:1], part, ALU.mult, ALU.add).then_inc(dve, 1)
                        n[0] += 1
                mark["folded"] = n[0]
                for layer in range(2):
                    step(v.tensor_tensor(const["bo"][:, layer, :], ps[5][:, layer * D:(layer + 1) * D], bo[:, layer, :], ALU.add))
                    step(v.tensor_scalar(const["bo"][:, layer, :], const["bo"][:, layer, :],
                                         const["gain"][:, layer:layer + 1], None, ALU.mult))
                    o = raw[f"o{layer}"]
                    step(v.tensor_scalar(o[:], o[:], const["gain"][:, layer:layer + 1], None, ALU.mult))
                    split(w[f"o{layer}"][:, 0], w[f"o{layer}"][:, 1], o[:])
                v.wait_ge(act, 7)
                step(v.tensor_tensor(w["fc"][:, 1], fc[:], w["fc"][:, 0].bitcast(F32), ALU.subtract))

            @block.gpsimd
            def _(pool):
                n = [0]

                def step(ins):
                    n[0] += 1
                    ins.then_inc(made, 1)
                    pool.wait_ge(made, n[0])

                def band(t, pattern, low, high, mult):
                    step(pool.affine_select(out=t, in_=t, compare_op=ALU.is_ge, fill=0.0, base=-low,
                                            pattern=pattern, channel_multiplier=mult))
                    step(pool.affine_select(out=t, in_=t, compare_op=ALU.is_ge, fill=0.0, base=high,
                                            pattern=[[-s, c] for s, c in pattern], channel_multiplier=-mult))

                for t in (ones, ohf, const["head"], const["rest"], const["ident"]):
                    step(pool.memset(t[:], 1.0))
                step(pool.memset(const["minus_half"][:], -0.5))
                band(const["ident"][:], [[-1, P]], 0, 0, 1)
                band(const["head"][:], [[-HD, GH]], 0, HD - 1, 1)
                band(const["rest"][:], [[-REST, GH]], 0, KEYS - MAIN - 1, 1)
                band(ohf[:, 0:HEADS * MAIN], [[1, HEADS * MAIN]], 0, MAIN - 1, -MAIN)
                band(ohf[:, HEADS * MAIN:], [[1, HEADS * REST]], 0, REST - 1, -REST)
                for c in range(LANES):
                    vb = ten["V_blocks"][c]
                    step(pool.memset(vb[:], 0.0))
                    pairs = vb[:].rearrange("p g (t s) -> p g t s", s=GH * VC + 2 * VC)
                    step(pool.memset(pairs[0:MAIN, :, :, HD:VC], 1.0))
                    step(pool.memset(pairs[MAIN:P, :, :, VC + HD:2 * VC], 1.0))
                    for g in range(2):
                        rest = vb[:, g, 4 * GH * VC:].rearrange("p (h v) -> p h v", v=VC)
                        step(pool.tensor_copy(rest[:, :, HD], const["rest"][:]))

                pool.wait_ge(dve, mark["ternary"])
                pool.tensor_tensor(fc[:], fc_abs[:], fc_scale[:].unsqueeze(1).to_broadcast([P, DT, HID0]), ALU.mult).then_inc(made, 1)


            @block.scalar
            def _(sc):
                for dst, src in ffn_loads:
                    sc.dma_start(dst, src).then_inc(ffn_loaded, 16)
                sc.wait_ge(ffn_loaded, 16 * len(ffn_loads))
                for t in range(DT):
                    sc.activation(fc_abs[:, t, :], fc[:, t, :], ACT.Abs).then_inc(act, 1)
                sc.activation(pj_abs[:], pj[:], ACT.Abs).then_inc(act, 1)
                sc.wait_ge(act, 3)
                sc.activation(fc[:], fc[:], ACT.Sign).then_inc(act, 1)
                sc.activation(pj[:], pj[:], ACT.Sign).then_inc(act, 1)
                sc.wait_ge(loaded, 16 * len(loads))
                sc.activation(const["gain"][:], gx[:], ACT.Tanh).then_inc(act, 1)
                sc.wait_ge(dve, mark["folded"])
                sc.copy(w["fc"][:, 0], fc[:]).then_inc(act, 1)

            @block.tensor
            def _(pe):
                pe.wait_ge(made, tables)
                pe.wait_ge(act, 3)
                pe.wait_ge(loaded, 16 * len(loads))
                for j in range(2):
                    for t in range(DT):
                        pe.matmul(ps[j][:], ones[:], fc_abs[:, t, j * 512:(j + 1) * 512], start=t == 0, stop=t == DT - 1)
                for t in range(HT0):
                    ins = pe.matmul(ps[2][:, 0:D], ones[:], pj_abs[:, t, :], start=t == 0, stop=t == HT0 - 1)
                ins.then_inc(pe_s, 1)
                for j in range(2):
                    ins = pe.matmul(ps[3 + j][0:RANK, :], fast[:], uT[:, j * 512:(j + 1) * 512], start=True, stop=True)
                ins.then_inc(pe_s, 1)
                pe.wait_ge(dve, mark["bv"])
                for layer in range(2):
                    for t in range(DT):
                        ins = pe.matmul(ps[5][:, layer * D:(layer + 1) * D], bvb[:, layer, t, :],
                                        raw[f"o{layer}"][:, t, :], start=t == 0, stop=t == DT - 1)
                ins.then_inc(pe_s, 1)
                for j in range(2):
                    pe.wait_ge(dve, mark["scales"] if j else mark["fu"])
                    for t in range(DT):
                        ins = pe.matmul(ps[(6, 0)[j] + t][:], vr[:, t * P:(t + 1) * P], fu[:, j * 512:(j + 1) * 512],
                                        start=True, stop=True)
                    ins.then_inc(pe_s, 1)


def layers(nc, ten, ps, w, const, dram):
    front_banks, back_banks = Banks(front_walk(), 0), Banks(back_walk(), 4)
    with ExitStack() as ctx:
        def sb(name, shape, dt=F32):
            return ctx.enter_context(nc.sbuf_tensor(name, shape, dt))

        def sem(name):
            return ctx.enter_context(nc.semaphore(name))

        def lanes(name, shape, dt=F32):
            return [sb(f"{name}{c}", shape, dt) for c in range(LANES)]

        x_in, x_mid = lanes("x_in", [P, 2, D]), lanes("x_mid", [P, 2, D])
        ctxt = sb("ctxt", [P, DT, LANES, PAD])
        ctx_hi, ctx_lo = (sb(n, [P, DT, LANES, P], F32R) for n in ("ctx_hi", "ctx_lo"))
        mrow_i, mrow, masked = sb("mrow_i", [P, LANES, PAD], I32), sb("mrow", [P, LANES, PAD]), sb("masked", [P, LANES, PAD])
        left, at_least_one, some, inv_left = (sb(n, [P, LANES]) for n in ("keys_left", "at_least_one", "some_left", "inv_left"))
        k_sum, k_fill = sb("k_sum", [P, 2, LANES]), sb("k_fill", [P, 2, LANES, PAD])
        mcol_i, neg_col = sb("mcol_i", [P, LANES, 2], I32), sb("neg_col", [P, LANES, 2])
        stats, moments, var_eps, rstd = ([lanes(f"{n}_{g}_", s) for g in ("first", "later")] for n, s in (
            ("stats", [P, 2, 6]), ("moments", [P, 2, 2]), ("var_eps", [P, 2]), ("rstd", [P, 2])))
        xn_first, xn_later = sb("xn_first", [P, 2, D]), lanes("xn", [P, 2, D])
        xT_first, xT_later = [sb(f"xT_first_{h}", [P, DT, S], F32R) for h in ("hi", "lo")], [lanes(f"xT_{h}", [P, DT, S], F32R) for h in ("hi", "lo")]
        q_hi, q_lo = lanes("q_hi", [P, 2, S], F32R), lanes("q_lo", [P, 2, S], F32R)
        kt = sb("kt", [P, 2, LANES, PAD])
        k_hi, k_lo = ([sb(f"{n}{layer}", [P, 2, LANES, PAD], F32R) for layer in range(2)] for n in ("k_hi", "k_lo"))
        kb_hi, kb_lo = lanes("kb_hi", [P, 2, GH * PAD], F32R), lanes("kb_lo", [P, 2, GH * PAD], F32R)
        max_main, max_rest, neg_max = (lanes(n, [P, 2, HEADS]) for n in ("max_main", "max_rest", "neg_max"))
        neg_maxT = lanes("neg_maxT", [HEADS, S], F32R)
        prob = lanes("prob", [P, 10, S])
        inv_sum = lanes("inv_sum", [P, 2, HEADS])
        relu = [prob[c][:, 0:4, :].rearrange("p (u t) s -> p u (t s)", t=2) for c in range(LANES)]
        sq = [prob[c][:, 4:10, :].rearrange("p (u t) s -> p u (t s)", t=2) for c in range(LANES)]
        sq_hi, sq_lo = lanes("sq_hi", [P, HT0, S], F32R), lanes("sq_lo", [P, HT0, S], F32R)
        v_blocks = ten["V_blocks"]

        per_body = {}

        def loop_sem(name, n):
            per_body[name] = (sem(name), n)
            return per_body[name][0]

        def lane_sems(name, n):
            return [loop_sem(f"{name}{c}", n) for c in range(LANES)]

        def turn(kind, stage, u):
            if kind == "xT":
                return (1, 0) if stage == 0 else (3, stage - 1)
            units = {"SA": 5, "SB": 5, "PV": 2, "up": 4}.get(kind, 1)
            return units * (1 if kind in ("up", "down", "gate") else 2), units * stage + u

        def name_of(key):
            return ("xT0" if key[0] == "xT" and key[1] == 0 else key[0]), key[2]

        x_loaded, x_stored = lane_sems("x_loaded", 16), lane_sems("x_stored", 16)
        keys_loaded = loop_sem("keys_loaded", 48)
        ctx_hi_made, ctx_split, neg_col_made = (loop_sem(n, 1) for n in ("ctx_hi_made", "ctx_split", "neg_col_made"))
        mask_made, kt_masked, kt_filled = loop_sem("mask_made", 4), loop_sem("kt_masked", 4), loop_sem("kt_filled", 1)
        kt_made, k_hi_made, k_split = (loop_sem(n, 2) for n in ("kt_made", "k_hi_made", "k_split"))
        stats_made, moments_made, var_made, rstd_made, xn_made, xT_hi_made, xT_made = (
            (lane_sems(f"{n}_first", 1), lane_sems(n, 3)) for n in (
                "stats_made", "moments_made", "var_made", "rstd_made", "xn_made", "xT_hi_made", "xT_made"))
        q_hi_made, q_made, kb_hi_made, kb_lo_made, v_main_made, v_made = (lane_sems(n, 2) for n in (
            "q_hi_made", "q_made", "kb_hi_made", "kb_lo_made", "v_main_made", "v_made"))
        neg_max_made, neg_maxT_made, oT_hi_made, oT_made, bias_added, x_attended = (lane_sems(n, 2) for n in (
            "neg_max_made", "neg_maxT_made", "oT_hi_made", "oT_made", "bias_added", "x_attended"))
        maxima_made, prob_made = lane_sems("maxima_made", 10), lane_sems("prob_made", 10)
        inv_made, heads_made = lane_sems("inv_made", 4), lane_sems("heads_made", 4)
        relu_made, sq_made, sq_hi_made, sq_split = (lane_sems(n, 4) for n in ("relu_made", "sq_made", "sq_hi_made", "sq_split"))
        y_made, x_fed, logits_made = (lane_sems(n, 1) for n in ("y_made", "x_fed", "logits_made"))
        read_out = {"V": v_made, "xT0": xT_made[0], "xT": xT_made[1], "Q": q_made, "SA": maxima_made, "mT": neg_maxT_made, "SB": prob_made,
                    "PV": heads_made, "oT": oT_made, "O": x_attended, "up": relu_made, "down": y_made, "gate": logits_made, "K": [kt_made]}
        filled = {}
        for key, _ in [*front_walk(), *back_walk()]:
            if name_of(key) not in filled:
                filled[name_of(key)] = loop_sem(f"{name_of(key)[0]}_filled{key[2]}", turn(key[0], key[1], key[3])[0])

        credits = list(per_body.values())
        with nc.Block() as block:
            @block.sync
            def _(sp):
                for c in range(LANES):
                    sp.dma_start(x_in[c][:], dram["x"][0][:, 2 * c:2 * c + 2, :]).then_inc(x_loaded[c], 16)
                for t, name in ((ctxt[:], "ctxT"), (mcol_i[:], "mask_col")):
                    sp.dma_start(t, dram[name][0]).then_inc(keys_loaded, 16)
                sp.dma_start(mrow_i[:], dram["mask_row"][0].partition_broadcast(P)).then_inc(keys_loaded, 16)

            @block.scalar
            def _(sc):
                for s, n in credits[0::3]:
                    sc.sem_inc(s, n)

            @block.vector
            def _(v):
                for s, n in credits[1::3]:
                    v.sem_inc(s, n)

            @block.gpsimd
            def _(pool):
                for s, n in credits[2::3]:
                    pool.sem_inc(s, n)

        def banks_of(key):
            return front_banks if key in front_banks.bank else back_banks

        def bank(*key):
            return ps[banks_of(key).bank[key]]

        def wait_filled(eng, i, *key):
            eng.wait_ge(filled[name_of(key)], at(i, *turn(key[0], key[1], key[3])))

        def wait_free(pe, i, with_next, waited, *key):
            other, back = banks_of(key).previous(key, with_next)
            name, c = name_of(other)
            value = at(i - back, *turn(other[0], other[1], other[3]))
            if read_out[name][c] is not waited and (not isinstance(value, int) or value > 0):
                pe.wait_ge(read_out[name][c], value)

        def fill(*key):
            return filled[name_of(key)]

        def repeated(t, rest):
            return t[:].rearrange("p t c k -> p (t c) k")[:, :, rest * MAIN:(rest + 1) * MAIN].rearrange("p n (r k) -> p n r k", r=(1, 4)[rest])

        def keys_of(t, rest):
            keys = t[:].rearrange("p t c k -> p (t c) k")[:, :, MAIN:PAD] if rest else t[:].rearrange("p t c k -> p (t c) k")[:, :, 0:MAIN]
            return keys.unsqueeze(2).to_broadcast([P, DT * LANES, (1, 4)[rest], (MAIN, REST)[rest]])

        def flat(t):
            return t[:].rearrange("p t s -> p (t s)")

        def pair(t, u):
            return t[:, 2 * u:2 * u + 2, :].rearrange("p t s -> p (t s)")

        def group(stage):
            return min(stage, 1)

        def nth(stage):
            return (1, 0) if stage == 0 else (3, stage - 1)

        def xn_of(stage, c):
            return xn_later[c] if stage else xn_first

        def xT_of(stage, c):
            return [t[c] for t in xT_later] if stage else xT_first

        def schedule(eng, half):
            half(-1, 0, False, False, False, True)
            half(-1, 1, False, True, False, True)
            half(0, 0, False, True, True, True)
            half(0, 1, True, True, True, True)
            with eng.Fori(1, BODIES - 1) as i:
                half(i, 0, True, True, True, True)
                half(i, 1, True, True, True, True)
            half(BODIES - 1, 0, True, True, True, False)
            half(BODIES - 1, 1, True, False, True, False)
            half(BODIES, 0, True, False, False, False)

        with nc.Block() as block:
            @block.sync
            def _(sp):
                def body_of(name, i):
                    return dram[name][i] if isinstance(i, int) else dram[name][bass.ds(i, 1)].squeeze(0)

                def load_x(i, c):
                    sp.dma_start(x_in[c][:], body_of("x", i)[:, 2 * c:2 * c + 2, :]).then_inc(x_loaded[c], 16)

                def load_keys(i):
                    sp.dma_start(ctxt[:], body_of("ctxT", i)).then_inc(keys_loaded, 16)
                    sp.dma_start(mrow_i[:], body_of("mask_row", i).partition_broadcast(P)).then_inc(keys_loaded, 16)
                    sp.dma_start(mcol_i[:], body_of("mask_col", i)).then_inc(keys_loaded, 16)

                def store_x(i, c):
                    sp.wait_ge(x_attended[c], at(i, 2, 1))
                    sp.dma_start(body_of("x3", i)[:, 2 * c:2 * c + 2, :], x_mid[c][:]).then_inc(x_stored[c], 16)

                with sp.Fori(0, BODIES - 1) as i:
                    sp.wait_ge(bias_added[0], at(i, 2, 0))
                    load_x(i + 1, 0)
                    sp.wait_ge(ctx_split, at(i, 1, 0))
                    sp.wait_ge(neg_col_made, at(i, 1, 0))
                    load_keys(i + 1)
                    sp.wait_ge(bias_added[1], at(i, 2, 0))
                    load_x(i + 1, 1)
                    for c in range(LANES):
                        store_x(i, c)
                for c in range(LANES):
                    store_x(BODIES - 1, c)
                for c in range(LANES):
                    sp.wait_ge(x_stored[c], 16 * (BODIES + 1))

            @block.gpsimd
            def _(pool):
                def context_lo(i):
                    pool.wait_ge(ctx_hi_made, at(i, 1, 0))
                    pool.tensor_tensor(repeated(ctx_lo, 0), keys_of(ctxt, 0), repeated(ctx_hi, 0).bitcast(F32), ALU.subtract)
                    pool.tensor_tensor(repeated(ctx_lo, 1), keys_of(ctxt, 1), repeated(ctx_hi, 1).bitcast(F32), ALU.subtract).then_inc(ctx_split, 1)

                def inv_std(i, stage, c):
                    g = group(stage)
                    pool.wait_ge(var_made[g][c], at(i, *nth(stage)))
                    pool.tensor_tensor(rstd[g][c][:], var_eps[g][c][:], const["minus_half"][:], ALU.pow).then_inc(rstd_made[g][c], 1)

                def add_bias(i, layer, c):
                    pool.wait_ge(xn_made[layer][c], at(i, *nth(2 * layer)))
                    if layer == 0:
                        pool.wait_ge(x_stored[c], before(i, 16, 15))
                        pool.wait_ge(xn_made[1][c], before(i, *nth(3)))
                    src = (x_in, x_mid)[layer][c]
                    pool.tensor_tensor(x_mid[c][:], src[:], const["bo"][:, layer, :].unsqueeze(1).to_broadcast([P, 2, D]),
                                       ALU.add).then_inc(bias_added[c], 1)

                def key_blocks_lo(i, layer, c):
                    pool.wait_ge(k_split, at(i, 2, layer))
                    pool.wait_ge(filled["SB", c], at(i, 10, 4) if layer else before(i, 10, 9))
                    kb, head = kb_lo[c], const["head"]
                    pool.tensor_tensor(
                        kb[:, :, 0:GH * MAIN].rearrange("p g (h k) -> p g h k", k=MAIN),
                        k_lo[layer][:, :, c, 0:MAIN].bitcast(F32).unsqueeze(2).to_broadcast([P, 2, GH, MAIN]),
                        head[:].unsqueeze(1).unsqueeze(3).to_broadcast([P, 2, GH, MAIN]), ALU.mult)
                    pool.tensor_tensor(
                        kb[:, :, GH * MAIN:].rearrange("p g (h k) -> p g h k", k=REST),
                        k_lo[layer][:, :, c, MAIN:PAD].bitcast(F32).unsqueeze(2).to_broadcast([P, 2, GH, REST]),
                        head[:].unsqueeze(1).unsqueeze(3).to_broadcast([P, 2, GH, REST]), ALU.mult).then_inc(kb_lo_made[c], 1)

                def square_lo(i, c, u):
                    pool.wait_ge(sq_hi_made[c], at(i, 4, u))
                    pool.wait_ge(sq_made[c], at(i, 4, u))
                    pool.tensor_tensor(pair(sq_lo[c], u), sq[c][:, u % 3, :], pair(sq_hi[c], u).bitcast(F32),
                                       ALU.subtract).then_inc(sq_split[c], 1)

                def half(i, b, tail, front, back, ahead):
                    f, j = 1 - b, i + b
                    if back:
                        inv_std(i, 2, b)
                    if front:
                        add_bias(j, 0, f)
                    if back:
                        key_blocks_lo(i, 1, b)
                        add_bias(i, 1, b)
                    if ahead:
                        if b == 0:
                            context_lo(i + 1)
                        inv_std(i + 1, 0, b)
                    if front:
                        inv_std(j, 1, f)
                    if ahead:
                        key_blocks_lo(i + 1, 0, b)
                    if front:
                        square_lo(j, f, 0)
                        square_lo(j, f, 1)
                        square_lo(j, f, 2)
                        square_lo(j, f, 3)
                    if back:
                        inv_std(i, 3, b)

                schedule(pool, half)

            @block.scalar
            def _(sc):
                def transposed_hi(i, stage, c):
                    wait_filled(sc, i, "xT", stage, c, 0)
                    sc.copy(flat(xT_of(stage, c)[0]), bank("xT", stage, c, 0)[:]).then_inc(xT_hi_made[group(stage)][c], 1)

                def heads_hi(i, layer, c):
                    wait_filled(sc, i, "oT", layer, c, 0)
                    sc.copy(flat(xT_later[0][c]), bank("oT", layer, c, 0)[:]).then_inc(oT_hi_made[c], 1)

                def keys(i, layer):
                    wait_filled(sc, i, "K", layer, 0, 0)
                    sc.wait_ge(k_split, at(i, 2, 0) if layer else before(i, 2, 1))
                    for g in range(2):
                        ins = sc.activation(kt[:, g].rearrange("p c k -> p (c k)"), bank("K", layer, 0, 0)[:, g * LANES * PAD:(g + 1) * LANES * PAD],
                                            ACT.Identity, bias=const["bk"][:, layer, g:g + 1], scale=HD ** -0.5)
                    ins.then_inc(kt_made, 1)

                def values(i, layer, c):
                    wait_filled(sc, i, "V", layer, c, 0)
                    blocks = v_blocks[c][:].rearrange("p g (t s) -> p g t s", s=GH * VC + 2 * VC)
                    rows = bank("V", layer, c, 0)[:, 0:D].rearrange("p (g t e d) -> p g t e d", g=2, t=4, e=2)
                    sc.copy(blocks[0:MAIN, :, :, 0:HD], rows[0:MAIN, :, :, 0])
                    sc.copy(blocks[MAIN:P, :, :, VC:VC + HD], rows[0:MAIN, :, :, 1]).then_inc(v_main_made[c], 1)

                def queries(i, layer, c):
                    wait_filled(sc, i, "Q", layer, c, 0)
                    for g in range(2):
                        ins = sc.activation(q_hi[c][:, g, :], bank("Q", layer, c, 0)[:, g * S:(g + 1) * S], ACT.Identity,
                                            bias=const["bq"][:, layer, g:g + 1])
                    ins.then_inc(q_hi_made[c], 1)

                def maxima(i, layer, c):
                    wait_filled(sc, i, "mT", layer, c, 0)
                    sc.copy(neg_maxT[c][:], bank("mT", layer, c, 0)[0:HEADS, 0:S]).then_inc(neg_maxT_made[c], 1)

                def exponentials(i, layer, c, u):
                    wait_filled(sc, i, "SB", layer, c, u)
                    if layer == 0 and u == 0:
                        sc.wait_ge(neg_col_made, at(i, 1, 0))
                    bias = neg_col[:, c, u // 4:u // 4 + 1] if layer == 0 else 0.0
                    sc.activation(pair(prob[c], u), bank("SB", layer, c, u)[:], ACT.Exp, bias=bias).then_inc(prob_made[c], 1)

                def squares_hi(i, c, u):
                    wait_filled(sc, i, "up", 0, c, u)
                    if u > 1:
                        sc.wait_ge(sq_made[c], at(i, 4, u - 2))
                    sc.activation(relu[c][:, u % 2, :], bank("up", 0, c, u)[:], ACT.Relu).then_inc(relu_made[c], 1)
                    sc.wait_ge(relu_made[c], at(i, 4, u))
                    sc.activation(pair(sq_hi[c], u), relu[c][:, u % 2, :], ACT.Square).then_inc(sq_hi_made[c], 1)

                def context_hi(i):
                    sc.wait_ge(keys_loaded, at(i, 48, 47))
                    sc.copy(repeated(ctx_hi, 0), keys_of(ctxt, 0))
                    sc.copy(repeated(ctx_hi, 1), keys_of(ctxt, 1)).then_inc(ctx_hi_made, 1)

                def half(i, b, tail, front, back, ahead):
                    f, j = 1 - b, i + b
                    if front:
                        maxima(j, 0, f)
                    if tail:
                        transposed_hi(j - 1, 3, f)
                    if front:
                        for u in range(4):
                            exponentials(j, 0, f, u)
                    if back:
                        transposed_hi(i, 2, b)
                    if front:
                        exponentials(j, 0, f, 4)
                    if back:
                        queries(i, 1, b)
                        maxima(i, 1, b)
                    if front:
                        values(j, 1, f)
                        heads_hi(j, 0, f)
                    if back:
                        exponentials(i, 1, b, 0)
                    if ahead:
                        if b == 0:
                            context_hi(i + 1)
                    if back:
                        for u in range(1, 5):
                            exponentials(i, 1, b, u)
                    if ahead:
                        keys(i + 1, b)
                    if front:
                        transposed_hi(j, 1, f)
                    if ahead:
                        transposed_hi(i + 1, 0, b)
                    if front:
                        squares_hi(j, f, 0)
                    if back:
                        heads_hi(i, 1, b)
                    if front:
                        squares_hi(j, f, 1)
                        squares_hi(j, f, 2)
                    if ahead:
                        queries(i + 1, 0, b)
                    if front:
                        squares_hi(j, f, 3)
                    if ahead:
                        values(i + 1, 0, b)

                sc.preload_act_table(ACT.Exp)
                schedule(sc, half)

            @block.vector
            def _(v):
                def x_of(stage, c):
                    return x_mid[c] if stage else x_in[c]

                def layer_norm(i, stage, c):
                    statistics(i, stage, c)
                    aggregates(i, stage, c)
                    variances(i, stage, c)

                def statistics(i, stage, c):
                    g = group(stage)
                    if stage == 0:
                        v.wait_ge(x_loaded[c], at(i, 16, 15))
                    elif stage == 2:
                        v.wait_ge(x_fed[c], at(i, 1, 0))
                    else:
                        v.wait_ge(x_attended[c], at(i, 2, stage // 2))
                    for q in range(2):
                        ins = v.bn_stats(stats[g][c][:, q, :], x_of(stage, c)[:, q, :])
                    ins.then_inc(stats_made[g][c], 1)

                def aggregates(i, stage, c):
                    g = group(stage)
                    v.wait_ge(stats_made[g][c], at(i, *nth(stage)))
                    v.sem_inc(const["passed"], 1)
                    for q in range(2):
                        ins = v.bn_aggr(moments[g][c][:, q, :], stats[g][c][:, q, :])
                    ins.then_inc(moments_made[g][c], 1)

                def variances(i, stage, c):
                    g = group(stage)
                    v.wait_ge(moments_made[g][c], at(i, *nth(stage)))
                    v.tensor_scalar(var_eps[g][c][:], moments[g][c][:, :, 1], LN_EPS, None, ALU.add).then_inc(var_made[g][c], 1)

                def normalise(i, stage, c):
                    g = group(stage)
                    v.wait_ge(rstd_made[g][c], at(i, *nth(stage)))
                    for q in range(2):
                        ins = v.tensor_scalar(xn_of(stage, c)[:, q, :], x_of(stage, c)[:, q, :], moments[g][c][:, q, 0:1],
                                              rstd[g][c][:, q:q + 1], ALU.subtract, ALU.mult)
                    ins.then_inc(xn_made[g][c], 1)

                def transposed_lo(i, stage, c):
                    g, (hi, lo) = group(stage), xT_of(stage, c)
                    v.wait_ge(xT_hi_made[g][c], at(i, *nth(stage)))
                    v.tensor_tensor(flat(lo), bank("xT", stage, c, 0)[:], flat(hi).bitcast(F32), ALU.subtract).then_inc(xT_made[g][c], 1)

                def heads_lo(i, layer, c):
                    hi, lo = xT_of(1, c)
                    v.wait_ge(oT_hi_made[c], at(i, 2, layer))
                    v.tensor_tensor(flat(lo), bank("oT", layer, c, 0)[:], flat(hi).bitcast(F32), ALU.subtract).then_inc(oT_made[c], 1)

                def masks(i):
                    v.wait_ge(keys_loaded, at(i, 48, 47))
                    v.tensor_scalar(neg_col[:], mcol_i[:], 0.0, -NEG, ALU.is_equal, ALU.mult)
                    v.tensor_scalar(masked[:], mrow_i[:], 0.0, None, ALU.is_equal)
                    v.tensor_scalar(mrow[:], mrow_i[:], 0.0, None, ALU.not_equal).then_inc(mask_made, 1)
                    v.wait_ge(mask_made, at(i, 4, 0))
                    v.tensor_reduce(left[:], mrow[:], AX.X, ALU.add).then_inc(mask_made, 1)
                    v.wait_ge(mask_made, at(i, 4, 1))
                    v.tensor_scalar(at_least_one[:], left[:], 1.0, None, ALU.max)
                    v.tensor_scalar(some[:], left[:], 1.0, None, ALU.min).then_inc(mask_made, 1)
                    v.wait_ge(mask_made, at(i, 4, 2))
                    v.reciprocal(inv_left[:], at_least_one[:]).then_inc(mask_made, 1)
                    v.tensor_tensor(neg_col[:], neg_col[:], some[:].unsqueeze(2).to_broadcast([P, LANES, 2]), ALU.mult).then_inc(neg_col_made, 1)

                def keys(i, layer):
                    v.wait_ge(kt_made, at(i, 2, layer))
                    if layer == 0:
                        v.wait_ge(mask_made, at(i, 4, 3))
                        full = [P, 2, LANES, PAD]
                        v.tensor_tensor(kt[:], kt[:], mrow[:].unsqueeze(1).to_broadcast(full), ALU.mult).then_inc(kt_masked, 1)
                        v.wait_ge(kt_masked, at(i, 4, 0))
                        v.tensor_reduce(k_sum[:].rearrange("p g c -> p (g c)"), kt[:].rearrange("p g c k -> p (g c) k"), AX.X, ALU.add).then_inc(kt_masked, 1)
                        v.wait_ge(kt_masked, at(i, 4, 1))
                        v.tensor_tensor(k_sum[:], k_sum[:], inv_left[:].unsqueeze(1).to_broadcast([P, 2, LANES]), ALU.mult).then_inc(kt_masked, 1)
                        v.wait_ge(kt_masked, at(i, 4, 2))
                        for g in range(2):
                            ins = v.tensor_tensor(k_fill[:, g], masked[:], k_sum[:, g, :].unsqueeze(2).to_broadcast([P, LANES, PAD]), ALU.mult)
                        ins.then_inc(kt_masked, 1)
                        v.wait_ge(kt_masked, at(i, 4, 3))
                        v.tensor_tensor(kt[:], kt[:], k_fill[:], ALU.add).then_inc(kt_filled, 1)
                        v.wait_ge(kt_filled, at(i, 1, 0))
                    v.tensor_copy(k_hi[layer][:], kt[:]).then_inc(k_hi_made, 1)
                    v.wait_ge(k_hi_made, at(i, 2, layer))
                    v.wait_ge(kb_lo_made[1], before(i, 2, layer))
                    v.tensor_tensor(k_lo[layer][:], kt[:], k_hi[layer][:].bitcast(F32), ALU.subtract).then_inc(k_split, 1)

                def key_blocks_hi(i, layer, c):
                    v.wait_ge(k_hi_made, at(i, 2, layer))
                    kb, head = kb_hi[c], const["head"]
                    v.tensor_tensor(
                        kb[:, :, 0:GH * MAIN].rearrange("p g (h k) -> p g h k", k=MAIN),
                        k_hi[layer][:, :, c, 0:MAIN].bitcast(F32).unsqueeze(2).to_broadcast([P, 2, GH, MAIN]),
                        head[:].unsqueeze(1).unsqueeze(3).to_broadcast([P, 2, GH, MAIN]), ALU.mult)
                    v.tensor_tensor(
                        kb[:, :, GH * MAIN:].rearrange("p g (h k) -> p g h k", k=REST),
                        k_hi[layer][:, :, c, MAIN:PAD].bitcast(F32).unsqueeze(2).to_broadcast([P, 2, GH, REST]),
                        head[:].unsqueeze(1).unsqueeze(3).to_broadcast([P, 2, GH, REST]), ALU.mult).then_inc(kb_hi_made[c], 1)

                def values(i, layer, c):
                    v.wait_ge(v_main_made[c], at(i, 2, layer))
                    rest = v_blocks[c][:, :, 4 * GH * VC:].rearrange("p g (h v) -> p g h v", v=VC)
                    rows = bank("V", layer, c, 0)[MAIN:P, 0:D].rearrange("p (g h d) -> p g h d", g=2, h=GH)
                    for n in range(2):
                        heads = slice(n * 4, n * 4 + 4)
                        for g in range(2):
                            ins = v.tensor_tensor(rest[n * MAIN:(n + 1) * MAIN, g, heads, 0:HD], rows[:, g, heads, :],
                                                  const["rest"][MAIN:P, 4:GH].unsqueeze(2).to_broadcast([MAIN, 4, HD]), ALU.mult)
                    ins.then_inc(v_made[c], 1)

                def queries(i, layer, c):
                    v.wait_ge(q_hi_made[c], at(i, 2, layer))
                    for g in range(2):
                        ins = v.scalar_tensor_tensor(q_lo[c][:, g, :], bank("Q", layer, c, 0)[:, g * S:(g + 1) * S],
                                                     const["bq"][:, layer, g:g + 1], q_hi[c][:, g, :].bitcast(F32), ALU.add, ALU.subtract)
                    ins.then_inc(q_made[c], 1)

                def maximum(i, layer, c, u):
                    wait_filled(v, i, "SA", layer, c, u)
                    scores = bank("SA", layer, c, u)
                    if u < 4:
                        q, g = u // 2, u % 2
                        v.tensor_reduce(max_main[c][:, q, g * GH:(g + 1) * GH], scores[:].rearrange("p (h k) -> p h k", k=MAIN),
                                        AX.X, ALU.max, negate=True).then_inc(maxima_made[c], 1)
                    else:
                        v.tensor_reduce(max_rest[c][:].rearrange("p q h -> p (q h)"), scores[:].rearrange("p (h k) -> p h k", k=REST),
                                        AX.X, ALU.max, negate=True).then_inc(maxima_made[c], 1)
                        v.wait_ge(maxima_made[c], at(i, 10, 5 * layer + 4))
                        v.tensor_tensor(neg_max[c][:], max_main[c][:], max_rest[c][:], ALU.min).then_inc(neg_max_made[c], 1)

                def divide(i, layer, c):
                    for q in range(2):
                        wait_filled(v, i, "PV", layer, c, q)
                        out = bank("PV", layer, c, q)[:, 0:HEADS * VC].rearrange("p (h v) -> p h v", v=VC)
                        v.reciprocal(inv_sum[c][:, q, :], out[:, :, HD]).then_inc(inv_made[c], 1)
                        v.wait_ge(inv_made[c], at(i, 4, 2 * layer + q))
                        v.tensor_tensor(xn_later[c][:, q, :].rearrange("p (h d) -> p h d", d=HD), out[:, :, 0:HD],
                                        inv_sum[c][:, q, :].unsqueeze(2).to_broadcast([P, HEADS, HD]), ALU.mult).then_inc(heads_made[c], 1)

                def attended(i, layer, c):
                    wait_filled(v, i, "O", layer, c, 0)
                    v.wait_ge(bias_added[c], at(i, 2, layer))
                    v.tensor_tensor(flat(x_mid[c]), bank("O", layer, c, 0)[:], flat(x_mid[c]), ALU.add).then_inc(x_attended[c], 1)

                def square(i, c, u):
                    v.wait_ge(relu_made[c], at(i, 4, u))
                    if u > 2:
                        v.wait_ge(sq_split[c], at(i, 4, u - 3))
                    v.tensor_tensor(sq[c][:, u % 3, :], relu[c][:, u % 2, :], relu[c][:, u % 2, :], ALU.mult).then_inc(sq_made[c], 1)

                def fed(i, c):
                    y = xn_later[c]
                    wait_filled(v, i, "down", 0, c, 0)
                    v.tensor_tensor(y[:], bank("down", 0, c, 0)[:].rearrange("p (q d) -> p q d", q=2),
                                    const["pj_scale"][:].unsqueeze(1).to_broadcast([P, 2, D]), ALU.mult).then_inc(y_made[c], 1)
                    v.wait_ge(y_made[c], at(i, 1, 0))
                    v.tensor_tensor(x_mid[c][:], x_mid[c][:], y[:], ALU.add).then_inc(x_fed[c], 1)

                def logits(i, c):
                    wait_filled(v, i, "gate", 0, c, 0)
                    v.tensor_tensor(ten["gates"][:, bass.ds(4 * i + 2 * c, 2), :], bank("gate", 0, c, 0)[:, 0:2 * E].rearrange("p (q e) -> p q e", e=E),
                                    const["gate_b"][:].unsqueeze(1).to_broadcast([P, 2, E]), ALU.add).then_inc(logits_made[c], 1)

                def half(i, b, tail, front, back, ahead):
                    f, j = 1 - b, i + b
                    if back:
                        layer_norm(i, 2, b)
                    if tail:
                        transposed_lo(j - 1, 3, f)
                    if back:
                        normalise(i, 2, b)
                        key_blocks_hi(i, 1, b)
                        transposed_lo(i, 2, b)
                        queries(i, 1, b)
                    if tail:
                        logits(j - 1, f)
                    if back:
                        for u in range(5):
                            maximum(i, 1, b, u)
                    if front:
                        divide(j, 0, f)
                        values(j, 1, f)
                        heads_lo(j, 0, f)
                    if ahead:
                        layer_norm(i + 1, 0, b)
                    if front:
                        attended(j, 0, f)
                        layer_norm(j, 1, f)
                    if ahead:
                        if b == 0:
                            masks(i + 1)
                        normalise(i + 1, 0, b)
                    if front:
                        normalise(j, 1, f)
                    if ahead:
                        keys(i + 1, b)
                    if front:
                        transposed_lo(j, 1, f)
                    if ahead:
                        transposed_lo(i + 1, 0, b)
                    if back:
                        divide(i, 1, b)
                    if ahead:
                        key_blocks_hi(i + 1, 0, b)
                    if back:
                        heads_lo(i, 1, b)
                    if front:
                        square(j, f, 0)
                        square(j, f, 1)
                        square(j, f, 2)
                    if ahead:
                        queries(i + 1, 0, b)
                    if front:
                        square(j, f, 3)
                    if back:
                        attended(i, 1, b)
                    if ahead:
                        maximum(i + 1, 0, b, 0)
                    if back:
                        layer_norm(i, 3, b)
                    if ahead:
                        for u in range(1, 4):
                            maximum(i + 1, 0, b, u)
                    if back:
                        normalise(i, 3, b)
                    if ahead:
                        maximum(i + 1, 0, b, 4)
                        values(i + 1, 0, b)
                    if front:
                        fed(j, f)

                schedule(v, half)

            @block.tensor
            def _(pe):
                def half(i, b, tail, front, back, ahead):
                    f, j = 1 - b, i + b

                    def free(body, *key, waited=None):
                        if front or back or ahead:
                            wait_free(pe, body, ahead, waited, *key)

                    def transposes(body, stage, c):
                        key, src = ("xT", stage, c, 0), xn_of(stage, c)
                        pe.wait_ge(xn_made[group(stage)][c], at(body, *nth(stage)))
                        free(body, *key)
                        for t in range(DT):
                            for q in range(2):
                                ins = pe.transpose(bank(*key)[:, t * S + q * P:t * S + (q + 1) * P], src[:, q, t * P:(t + 1) * P], const["ident"][:])
                        ins.then_inc(fill(*key), 1)

                    def heads_transposed(body, layer, c):
                        key = ("oT", layer, c, 0)
                        pe.wait_ge(heads_made[c], at(body, 4, 2 * layer + 1))
                        free(body, *key, waited=heads_made[c])
                        for t in range(DT):
                            for q in range(2):
                                ins = pe.transpose(bank(*key)[:, t * S + q * P:t * S + (q + 1) * P], xn_later[c][:, q, t * P:(t + 1) * P], const["ident"][:])
                        ins.then_inc(fill(*key), 1)

                    def keys(body, layer):
                        key, wk, ctx_half = ("K", layer, 0, 0), w[f"k{layer}"], (ctx_hi, ctx_lo)
                        pe.wait_ge(ctx_split, at(body, 1, 0))
                        free(body, *key)
                        for g in range(2):
                            ins = three_products(pe, bank(*key)[:, g * LANES * PAD:(g + 1) * LANES * PAD].rearrange("p (c k) -> p c k", k=PAD),
                                                 lambda h, t: wk[:, h, t, g * P:(g + 1) * P], lambda h, t: ctx_half[h][:, t, :, 0:PAD])
                        ins.then_inc(fill(*key), 1)

                    def values(body, layer, c):
                        key, wv, ctx_half = ("V", layer, c, 0), w[f"v{layer}"], (ctx_hi, ctx_lo)
                        free(body, *key)
                        three_products(pe, bank(*key)[:, 0:D], lambda h, t: ctx_half[h][:, t, c, :],
                                       lambda h, t: wv[:, h, t, :]).then_inc(fill(*key), 1)

                    def queries(body, layer, c):
                        key, wq, xT = ("Q", layer, c, 0), w[f"q{layer}"], xT_of(2 * layer, c)
                        pe.wait_ge(xT_made[layer][c], at(body, *nth(2 * layer)))
                        free(body, *key)
                        for g in range(2):
                            ins = three_products(pe, bank(*key)[:, g * S:(g + 1) * S],
                                                 lambda h, t: wq[:, h, t, g * P:(g + 1) * P], lambda h, t: xT[h][:, t, :])
                        ins.then_inc(fill(*key), 1)

                    def scores_for_maxima(body, layer, c, units):
                        if 0 in units:
                            pe.wait_ge(q_made[c], at(body, 2, layer))
                            pe.wait_ge(kb_hi_made[c], at(body, 2, layer))
                        for u in units:
                            key = ("SA", layer, c, u)
                            free(body, *key)
                            for q, g in [(u // 2, u % 2)] if u < 4 else [(0, 0), (0, 1), (1, 0), (1, 1)]:
                                out = bank(*key)[:] if u < 4 else bank(*key)[:, (2 * q + g) * P:(2 * q + g + 1) * P]
                                cols = kb_hi[c][:, g, 0:GH * MAIN] if u < 4 else kb_hi[c][:, g, GH * MAIN:]
                                ins = pe.matmul(out, q_hi[c][:, g, q * P:(q + 1) * P], cols, start=True, stop=True)
                            ins.then_inc(fill(*key), 1)

                    def maxima_transposed(body, layer, c):
                        key = ("mT", layer, c, 0)
                        pe.wait_ge(neg_max_made[c], at(body, 2, layer))
                        free(body, *key)
                        for q in range(2):
                            ins = pe.transpose(bank(*key)[0:HEADS, q * P:(q + 1) * P], neg_max[c][:, q, :], const["ident"][:])
                        ins.then_inc(fill(*key), 1)

                    def scores(body, layer, c, units):
                        kb, qT = (kb_hi[c], kb_lo[c]), (q_hi[c], q_lo[c])
                        for u in units:
                            key = ("SB", layer, c, u)
                            if u == 0:
                                pe.wait_ge(kb_lo_made[c], at(body, 2, layer))
                                pe.wait_ge(neg_maxT_made[c], at(body, 2, layer))
                            free(body, *key)
                            for h2 in range(2):
                                n = 2 * u + h2
                                g, t = (n // 4, n % 4) if u < 4 else (h2, 4)
                                out = bank(*key)[:, h2 * S:(h2 + 1) * S]
                                three_products(pe, out, lambda h, _: kb[h][:, g, t * P:(t + 1) * P], lambda h, _: qT[h][:, g, :], parts=1, last=False)
                                first = (g * GH + 2 * t) * MAIN if t < 4 else HEADS * MAIN + g * P
                                ins = pe.matmul(out, const["onehot"][:, first:first + P], neg_maxT[c][:], start=False, stop=True)
                            ins.then_inc(fill(*key), 1)

                    def outputs(body, layer, c, q):
                        key = ("PV", layer, c, q)
                        pe.wait_ge(v_made[c], at(body, 2, layer))
                        pe.wait_ge(prob_made[c], at(body, 10, 5 * layer + 4))
                        free(body, *key, waited=prob_made[c])
                        for g in range(2):
                            for t in range(5):
                                n = 4 * g + t if t < 4 else 8 + g
                                ins = pe.matmul(bank(*key)[:, g * GH * VC:(g + 1) * GH * VC], prob[c][:, n, q * P:(q + 1) * P],
                                                v_blocks[c][:, g, t * GH * VC:(t + 1) * GH * VC], start=t == 0, stop=t == 4)
                        ins.then_inc(fill(*key), 1)

                    def projection(body, layer, c):
                        key, wo, oT = ("O", layer, c, 0), w[f"o{layer}"], xT_of(1, c)
                        pe.wait_ge(oT_made[c], at(body, 2, layer))
                        free(body, *key, waited=oT_made[c])
                        for q in range(2):
                            ins = three_products(pe, bank(*key)[:, q * D:(q + 1) * D],
                                                 lambda h, t: oT[h][:, t, q * P:(q + 1) * P], lambda h, t: wo[:, h, t, :])
                        ins.then_inc(fill(*key), 1)

                    def up(body, c, units):
                        xT = xT_of(1, c)
                        for u in units:
                            key = ("up", 0, c, u)
                            if u == 0:
                                pe.wait_ge(xT_made[1][c], at(body, *nth(1)))
                            free(body, *key)
                            for h2 in range(2):
                                n = 2 * u + h2
                                ins = three_products(pe, bank(*key)[:, h2 * S:(h2 + 1) * S],
                                                     lambda h, t: w["fc"][:, h, t, n * P:(n + 1) * P], lambda h, t: xT[h][:, t, :])
                            ins.then_inc(fill(*key), 1)

                    def down(body, c):
                        key = ("down", 0, c, 0)
                        pe.wait_ge(sq_split[c], at(body, 4, 3))
                        free(body, *key)
                        for q in range(2):
                            for t in range(HT0):
                                for h, part in enumerate((sq_hi[c], sq_lo[c])):
                                    ins = pe.matmul(bank(*key)[:, q * D:(q + 1) * D], part[:, t, q * P:(q + 1) * P], w["pj"][:, t, :],
                                                    start=t == 0 and h == 0, stop=t == HT0 - 1 and h == 1)
                        ins.then_inc(fill(*key), 1)

                    def gate(body, c):
                        key, xT = ("gate", 0, c, 0), xT_of(3, c)
                        pe.wait_ge(xT_made[1][c], at(body, *nth(3)))
                        free(body, *key)
                        for q in range(2):
                            ins = three_products(pe, bank(*key)[:, q * E:(q + 1) * E],
                                                 lambda h, t: xT[h][:, t, q * P:(q + 1) * P], lambda h, t: w["gate"][:, h, t, :])
                        ins.then_inc(fill(*key), 1)

                    if front:
                        maxima_transposed(j, 0, f)
                    if tail:
                        transposes(j - 1, 3, f)
                    if front:
                        scores(j, 0, f, [0, 1, 2, 3])
                    if back:
                        transposes(i, 2, b)
                    if tail:
                        gate(j - 1, f)
                    if front:
                        scores(j, 0, f, [4])
                    if back:
                        queries(i, 1, b)
                    if front:
                        outputs(j, 0, f, 0)
                    if back:
                        scores_for_maxima(i, 1, b, range(5))
                    if front:
                        outputs(j, 0, f, 1)
                    if back:
                        maxima_transposed(i, 1, b)
                    if front:
                        values(j, 1, f)
                        heads_transposed(j, 0, f)
                    if back:
                        scores(i, 1, b, [0, 1])
                    if front:
                        projection(j, 0, f)
                    if back:
                        scores(i, 1, b, [2, 3, 4])
                    if ahead:
                        keys(i + 1, b)
                    if back:
                        outputs(i, 1, b, 0)
                    if front:
                        transposes(j, 1, f)
                    if ahead:
                        transposes(i + 1, 0, b)
                    if back:
                        outputs(i, 1, b, 1)
                    if front:
                        up(j, f, [0])
                    if back:
                        heads_transposed(i, 1, b)
                    if front:
                        up(j, f, [1, 2])
                    if ahead:
                        queries(i + 1, 0, b)
                    if front:
                        up(j, f, [3])
                    if back:
                        projection(i, 1, b)
                    if ahead:
                        scores_for_maxima(i + 1, 0, b, [0, 1, 2, 3])
                        values(i + 1, 0, b)
                        scores_for_maxima(i + 1, 0, b, [4])
                    if front:
                        down(j, f)

                schedule(pe, half)


def routing(nc, ten, ps, const, dram):
    with ExitStack() as ctx:
        def sb(name, shape, dt=F32):
            return ctx.enter_context(nc.sbuf_tensor(name, shape, dt))

        def sem(name):
            return ctx.enter_context(nc.semaphore(name))

        tiles = 2 * B
        full = [P, tiles, E]
        g = ten["gates"]
        key, rank, left, first_two = (sb(n, full) for n in ("key", "rank", "left", "first_two"))
        routes = sb("routes", [P, 2, B, E])
        top, best = sb("top", [P, tiles]), sb("best", [P, tiles])
        total, inv_total = sb("total", [P, 2, E]), sb("inv_total", [P, 2, E])
        rows = [sb(f"rows{h}", [P, S]) for h in range(2)]
        eight = [sb(f"eight{h}", [P, 8]) for h in range(2)]
        mark = {}
        ranked, dve, act, turned = sem("ranked"), sem("route_dve"), sem("route_act"), sem("routes_turned")
        w1_raw, w2_raw, b2_raw = sb("w1_raw", [P, DT, E * SUB]), sb("w2_raw", [P, HT1, D]), sb("b2_raw", [E, D])
        w1, w2, b2, pick, spread = (ten[n] for n in ("w1", "w2", "b2", "pick", "spread"))
        loaded, tables_made = sem("e_loaded"), sem("e_tables_made")
        halves = P * SUB // 2

        def wide(t):
            return t[:].unsqueeze(2).to_broadcast(full)

        with nc.Block() as block:
            @block.gpsimd
            def _(pool):
                pool.iota(rank[:], pattern=[[0, tiles], [-1, E]], base=E, channel_multiplier=0,
                          allow_small_or_imprecise_dtypes=True).then_inc(ranked, 1)
                pool.memset(pick[:], 1.0).then_inc(tables_made, 1)
                pool.wait_ge(tables_made, 1)
                pool.affine_select(out=pick[:], in_=pick[:], compare_op=ALU.is_equal, fill=0.0, base=0,
                                   pattern=[[-1, 2 * P]], channel_multiplier=1).then_inc(tables_made, 1)
                pool.wait_ge(tables_made, 2)
                pool.tensor_copy(spread[:, halves:].rearrange("p (r k) -> p r k", k=SUB),
                                 pick[:, P // 2:P].unsqueeze(2).to_broadcast([P, P // 2, SUB])).then_inc(tables_made, 1)
                for n, (weight, src) in enumerate(((w1, w1_raw), (w2, w2_raw), (b2, b2_raw))):
                    pool.wait_ge(act, n + 4)
                    pool.tensor_tensor(weight[:, 1], src[:], weight[:, 0].bitcast(F32), ALU.subtract)

            @block.sync
            def _(sp):
                sp.dma_start(w1_raw[:], dram["W1"].rearrange("(t p) n -> p t n", p=P)).then_inc(loaded, 16)
                sp.dma_start(w2_raw[:], dram["W2"].rearrange("(t p) n -> p t n", p=P)).then_inc(loaded, 16)
                sp.dma_start(ten["b1"][:], dram["b1"]).then_inc(loaded, 16)
                sp.dma_start(b2_raw[:], dram["b2"]).then_inc(loaded, 16)

            @block.scalar
            def _(sc):
                sc.wait_ge(dve, 2)
                sc.activation(g[:], g[:], ACT.Exp).then_inc(act, 1)
                sc.wait_ge(loaded, 64)
                sc.activation(w2_raw[:], w2_raw[:], ACT.Copy, scale=const["gain"][:, 3:4]).then_inc(act, 1)
                sc.activation(b2_raw[:], b2_raw[:], ACT.Copy, scale=const["gain"][0:E, 3:4]).then_inc(act, 1)
                sc.copy(w1[:, 0], w1_raw[:]).then_inc(act, 1)
                sc.wait_ge(act, 3)
                sc.copy(w2[:, 0], w2_raw[:]).then_inc(act, 1)
                sc.copy(b2[:, 0], b2_raw[:]).then_inc(act, 1)
                sc.wait_ge(tables_made, 2)
                sc.copy(spread[:, 0:halves].rearrange("p (r k) -> p r k", k=SUB),
                        pick[:, 0:P // 2].unsqueeze(2).to_broadcast([P, P // 2, SUB])).then_inc(tables_made, 1)

            @block.vector
            def _(v):
                n = [0]

                def step(ins):
                    n[0] += 1
                    ins.then_inc(dve, 1)
                    v.wait_ge(dve, n[0])

                step(v.tensor_reduce(top[:], g[:], AX.X, ALU.max))
                step(v.tensor_tensor(g[:], g[:], wide(top), ALU.subtract))
                v.wait_ge(act, 1)
                step(v.tensor_reduce(top[:], g[:], AX.X, ALU.add))
                step(v.reciprocal(best[:], top[:]))
                step(v.tensor_tensor(g[:], g[:], wide(best), ALU.mult))
                v.wait_ge(ranked, 1)
                for pick in range(2):
                    src = g if pick == 0 else left
                    step(v.tensor_reduce(top[:], src[:], AX.X, ALU.max))
                    step(v.tensor_tensor(key[:], src[:], wide(top), ALU.is_equal))
                    step(v.tensor_tensor(key[:], key[:], rank[:], ALU.mult))
                    step(v.tensor_reduce(best[:], key[:], AX.X, ALU.max))
                    step(v.tensor_tensor(key[:], key[:], wide(best), ALU.is_equal))
                    if pick == 0:
                        step(v.tensor_copy(first_two[:], key[:]))
                        step(v.scalar_tensor_tensor(left[:].rearrange("p t e -> p (t e)"), key[:].rearrange("p t e -> p (t e)"), -4.0,
                                                    g[:].rearrange("p t e -> p (t e)"), ALU.mult, ALU.add))
                    else:
                        step(v.tensor_tensor(first_two[:], first_two[:], key[:], ALU.add))
                step(v.tensor_tensor(g[:], g[:], first_two[:], ALU.mult))
                step(v.tensor_reduce(total[:], g[:].rearrange("p (b q) e -> p q e b", q=2), AX.X, ALU.add))
                step(v.tensor_scalar(total[:], total[:], 1e-6, None, ALU.add))
                step(v.reciprocal(inv_total[:], total[:]))
                step(v.tensor_scalar(inv_total[:], inv_total[:], CAPACITY, None, ALU.mult))
                for q in range(2):
                    v.tensor_tensor(routes[:, q], g[:].rearrange("p (b q) e -> p q b e", q=2)[:, q],
                                    inv_total[:, q, :].unsqueeze(1).to_broadcast([P, B, E]), ALU.mult).then_inc(dve, 1)
                n[0] += 2
                mark["routed"] = n[0]
                v.wait_ge(turned, 1)
                for h in range(2):
                    step(v.tensor_copy(rows[h][:], ps[h][:, 0:S]))
                for r in range(CHOSEN // 8):
                    for h in range(2):
                        v.max(eight[h][:], rows[h][:]).then_inc(dve, 1)
                    for h in range(2):
                        n[0] += 1
                        v.wait_ge(dve, n[0] + h)
                        v.match_replace(rows[h][:], eight[h][:], rows[h][:], -1.0).then_inc(dve, 1)
                    n[0] += 2
                    v.wait_ge(dve, n[0])
                for h in range(2):
                    step(v.tensor_scalar(ten["chosen"][:, h, :], rows[h][:], 0.0, None, ALU.is_lt))

            @block.tensor
            def _(pe):
                pe.wait_ge(dve, mark["routed"])
                for h in range(2):
                    for q in range(2):
                        src = routes[:, q, h * 16:(h + 1) * 16, :].rearrange("p b e -> p (b e)")
                        ins = pe.transpose(ps[h][:, q * P:(q + 1) * P], src, const["ident"][:])
                ins.then_inc(turned, 1)


def experts(nc, ten, ps, const, dram):
    with ExitStack() as ctx:
        def sb(name, shape, dt=F32):
            return ctx.enter_context(nc.sbuf_tensor(name, shape, dt))

        def sem(name):
            return ctx.enter_context(nc.semaphore(name))

        def two(name, shape, dt=F32):
            return [sb(f"{name}_{n}", shape, dt) for n in range(2)]

        w1, w2, b1, b2, pick, spread = (ten[n] for n in ("w1", "w2", "b1", "b2", "pick", "spread"))
        x = [sb(f"x_expert{c}", [P, 2, D]) for c in range(SLOTS)]
        stats, moments, var_eps, rstd = two("e_stats", [P, 2, 6]), two("e_moments", [P, 2, 2]), two("e_var_eps", [P, 2]), two("e_rstd", [P, 2])
        xn, xT_hi, xT_lo = two("e_xn", [P, 2, D]), two("e_xT_hi", [P, DT, S], F32R), two("e_xT_lo", [P, DT, S], F32R)
        gelu, hid = two("gelu", [P, HT1, S]), two("hid", [P, HT1, S])
        hid_hi, hid_lo = two("hid_hi", [P, HT1, S], F32R), two("hid_lo", [P, HT1, S], F32R)
        sel8 = two("sel8", [E, S], F32R)

        per_group = {}

        def loop_sem(name, n):
            per_group[name] = (sem(name), n)
            return per_group[name][0]

        x_loaded, x_stored = ([loop_sem(f"{n}{c}", 16) for c in range(SLOTS)] for n in ("e_x_loaded", "e_x_stored"))
        stats_made, moments_made, var_made, rstd_made, xn_made, xT_hi_made, xT_made = (loop_sem(n, SLOTS) for n in (
            "e_stats_made", "e_moments_made", "e_var_made", "e_rstd_made", "e_xn_made", "e_xT_hi_made", "e_xT_made"))
        sel8_made, x_made = loop_sem("sel8_made", SLOTS), loop_sem("x4_made", SLOTS)
        xT_filled, sel8_filled, down_filled = loop_sem("e_xT_filled", SLOTS), loop_sem("sel8_filled", SLOTS), loop_sem("e_down_filled", SLOTS)
        gelu_made, hid_made, hid_hi_made, hid_split = (loop_sem(n, 2 * SLOTS) for n in ("gelu_made", "hid_made", "hid_hi_made", "hid_split"))
        sel_filled, up_filled = loop_sem("sel_filled", 2 * SLOTS), loop_sem("e_up_filled", 2 * SLOTS)

        sel_bank, up_bank, xT_bank, down_bank = ps[0:2], ps[2:4], ps[4:6], ps[6:8]

        def one(i, c):
            return at(i, SLOTS, c)

        def of_pair(i, c, u):
            return at(i, 2 * SLOTS, 2 * c + u)

        def later(i, c, turns):
            return i + (c + turns) // SLOTS, (c + turns) % SLOTS

        def pair(t, u):
            return t[:, 2 * u:2 * u + 2, :].rearrange("p t s -> p (t s)")

        def flat(t):
            return t[:].rearrange("p t s -> p (t s)")

        def schedule(eng, turn):
            turn(-1, SLOTS - 2, lambda n: n == 2)
            turn(-1, SLOTS - 1, lambda n: n > 0)
            with eng.Fori(0, GROUPS - 1) as i:
                for c in range(SLOTS):
                    turn(i, c, lambda n: True)
            for c in range(SLOTS):
                turn(GROUPS - 1, c, lambda n, c=c: c + n < SLOTS)

        with nc.Block() as block:
            @block.sync
            def _(sp):
                for s, n in per_group.values():
                    sp.sem_inc(s, n)

        with nc.Block() as block:
            @block.sync
            def _(sp):
                def rows(name, i, c):
                    body = 2 * i + c // 2
                    t = dram[name][body] if isinstance(i, int) else dram[name][bass.ds(body, 1)].squeeze(0)
                    return t[:, 2 * (c % 2):2 * (c % 2) + 2, :]

                def load(i, c):
                    sp.dma_start(x[c][:], rows("x3", i, c)).then_inc(x_loaded[c], 16)

                def store(i, c):
                    sp.wait_ge(x_made, one(i, c))
                    sp.dma_start(rows("out", i, c), x[c][:]).then_inc(x_stored[c], 16)

                for c in range(SLOTS):
                    load(0, c)
                with sp.Fori(0, GROUPS - 1) as i:
                    for c in range(SLOTS):
                        store(i, c)
                        sp.wait_ge(x_stored[c], at(i, 16, 15))
                        load(i + 1, c)
                for c in range(SLOTS):
                    store(GROUPS - 1, c)
                for c in range(SLOTS):
                    sp.wait_ge(x_stored[c], 16 * (GROUPS + 1))

            @block.gpsimd
            def _(pool):
                def turn(i, c, has):
                    if has(2):
                        j, d = later(i, c, 2)
                        pool.wait_ge(var_made, one(j, d))
                        pool.tensor_tensor(rstd[d % 2][:], var_eps[d % 2][:], const["minus_half"][:], ALU.pow).then_inc(rstd_made, 1)
                    if has(1):
                        j, d = later(i, c, 1)
                        for u in range(2):
                            pool.wait_ge(hid_hi_made, of_pair(j, d, u))
                            pool.tensor_tensor(pair(hid_lo[d % 2], u), pair(hid[d % 2], u), pair(hid_hi[d % 2], u).bitcast(F32),
                                               ALU.subtract).then_inc(hid_split, 1)

                schedule(pool, turn)

            @block.scalar
            def _(sc):
                def turn(i, c, has):
                    if has(1):
                        j, d = later(i, c, 1)
                        for u in range(2):
                            sc.wait_ge(up_filled, of_pair(j, d, u))
                            for h in range(2):
                                t = 2 * u + h
                                ins = sc.activation(gelu[d % 2][:, t, :], up_bank[u][:, h * S:(h + 1) * S], ACT.Gelu, bias=b1[:, t:t + 1])
                            ins.then_inc(gelu_made, 1)
                        sc.wait_ge(sel8_filled, one(j, d))
                        sc.copy(sel8[d % 2][:], down_bank[d % 2][0:E, 0:S]).then_inc(sel8_made, 1)
                        sc.wait_ge(hid_made, of_pair(j, d, 0))
                        sc.copy(pair(hid_hi[d % 2], 0), pair(hid[d % 2], 0)).then_inc(hid_hi_made, 1)
                    if has(2):
                        k, e = later(i, c, 2)
                        sc.wait_ge(xT_filled, one(k, e))
                        sc.copy(flat(xT_hi[e % 2]), xT_bank[e % 2][:]).then_inc(xT_hi_made, 1)
                    if has(1):
                        sc.wait_ge(hid_made, of_pair(j, d, 1))
                        sc.copy(pair(hid_hi[d % 2], 1), pair(hid[d % 2], 1)).then_inc(hid_hi_made, 1)

                sc.preload_act_table(ACT.Gelu)
                schedule(sc, turn)

            @block.vector
            def _(v):
                def layer_norm(i, c):
                    n = c % 2
                    v.wait_ge(x_loaded[c], at(i, 16, 15))
                    for q in range(2):
                        ins = v.bn_stats(stats[n][:, q, :], x[c][:, q, :])
                    ins.then_inc(stats_made, 1)
                    v.wait_ge(stats_made, one(i, c))
                    v.sem_inc(const["passed"], 1)
                    for q in range(2):
                        ins = v.bn_aggr(moments[n][:, q, :], stats[n][:, q, :])
                    ins.then_inc(moments_made, 1)
                    v.wait_ge(moments_made, one(i, c))
                    v.tensor_scalar(var_eps[n][:], moments[n][:, :, 1], LN_EPS, None, ALU.add).then_inc(var_made, 1)

                def normalise(i, c):
                    n = c % 2
                    v.wait_ge(rstd_made, one(i, c))
                    for q in range(2):
                        ins = v.tensor_scalar(xn[n][:, q, :], x[c][:, q, :], moments[n][:, q, 0:1], rstd[n][:, q:q + 1], ALU.subtract, ALU.mult)
                    ins.then_inc(xn_made, 1)

                def masked(i, c, u):
                    v.wait_ge(gelu_made, of_pair(i, c, u))
                    v.wait_ge(sel_filled, of_pair(i, c, u))
                    v.tensor_tensor(pair(hid[c % 2], u), sel_bank[u][:], pair(gelu[c % 2], u), ALU.mult).then_inc(hid_made, 1)

                def turn(i, c, has):
                    j, d = later(i, c, 1)
                    k, e = later(i, c, 2)
                    if has(2):
                        layer_norm(k, e)
                    if has(1):
                        masked(j, d, 0)
                    if has(2):
                        normalise(k, e)
                    if has(1):
                        masked(j, d, 1)
                    if has(2):
                        v.wait_ge(xT_hi_made, one(k, e))
                        v.tensor_tensor(flat(xT_lo[e % 2]), xT_bank[e % 2][:], flat(xT_hi[e % 2]).bitcast(F32), ALU.subtract).then_inc(xT_made, 1)
                    if has(0):
                        v.wait_ge(down_filled, one(i, c))
                        v.tensor_tensor(flat(x[c]), down_bank[c % 2][:], flat(x[c]), ALU.add).then_inc(x_made, 1)

                schedule(v, turn)

            @block.tensor
            def _(pe):
                def choices(i, c, half):
                    row = 8 * (SLOTS * i + c) - P * half
                    for u in range(2):
                        j, d = later(i, c, -1)
                        pe.wait_ge(hid_made, of_pair(j, d, u))
                        for h in range(2):
                            first = (row + 2 * (2 * u + h)) * SUB
                            ins = pe.matmul(sel_bank[u][:, h * S:(h + 1) * S], spread[:, bass.ds(first, P)], ten["chosen"][:, half, :],
                                            start=True, stop=True)
                        ins.then_inc(sel_filled, 1)

                def choices_of_eight(i, c, half):
                    row = 8 * (SLOTS * i + c) - P * half
                    j, d = later(i, c, -2)
                    pe.wait_ge(x_made, one(j, d))
                    pe.matmul(down_bank[c % 2][:, 0:S], pick[:, bass.ds(row, P)], ten["chosen"][:, half, :],
                              start=True, stop=True).then_inc(sel8_filled, 1)

                def up(i, c):
                    xT = (xT_hi[c % 2], xT_lo[c % 2])
                    pe.wait_ge(xT_made, one(i, c))
                    for u in range(2):
                        j, d = later(i, c, -1)
                        pe.wait_ge(gelu_made, of_pair(j, d, u))
                        for h in range(2):
                            n = 2 * u + h
                            ins = three_products(pe, up_bank[u][:, h * S:(h + 1) * S],
                                                 lambda a, t: w1[:, a, t, n * P:(n + 1) * P], lambda a, t: xT[a][:, t, :])
                        ins.then_inc(up_filled, 1)

                def transposes(i, c):
                    pe.wait_ge(xn_made, one(i, c))
                    for t in range(DT):
                        for q in range(2):
                            ins = pe.transpose(xT_bank[c % 2][:, t * S + q * P:t * S + (q + 1) * P], xn[c % 2][:, q, t * P:(t + 1) * P], const["ident"][:])
                    ins.then_inc(xT_filled, 1)

                def down(i, c, q):
                    hh = (hid_hi[c % 2], hid_lo[c % 2])
                    if q == 0:
                        pe.wait_ge(hid_split, of_pair(i, c, 1))
                        pe.wait_ge(sel8_made, one(i, c))
                    out = down_bank[c % 2][:, q * D:(q + 1) * D]
                    three_products(pe, out, lambda a, t: hh[a][:, t, q * P:(q + 1) * P], lambda a, t: w2[:, a, t, :], parts=HT1, last=False)
                    for a in range(2):
                        ins = pe.matmul(out, sel8[c % 2][:, q * P:(q + 1) * P], b2[:, a, :], start=False, stop=a == 1)
                    return ins

                def turn(i, c, has, half):
                    j, d = later(i, c, 1)
                    k, e = later(i, c, 2)
                    if has(1):
                        choices(j, d, half)
                        up(j, d)
                        choices_of_eight(j, d, half)
                    if has(0):
                        down(i, c, 0)
                    if has(2):
                        transposes(k, e)
                    if has(0):
                        down(i, c, 1).then_inc(down_filled, 1)

                turn(-1, SLOTS - 2, lambda n: n == 2, 0)
                turn(-1, SLOTS - 1, lambda n: n > 0, 0)
                for half in range(2):
                    last = (half + 1) * GROUPS // 2 - 1
                    with pe.Fori(half * GROUPS // 2, last) as i:
                        for c in range(SLOTS):
                            turn(i, c, lambda n: True, half)
                    for c in range(SLOTS):
                        turn(last, c, lambda n, c=c: half == 0 or c + n < SLOTS, half if c + 1 < SLOTS else 1)


def program(nc, dram):
    with ExitStack() as ctx:
        def sb(name, shape, dt=F32):
            return ctx.enter_context(nc.sbuf_tensor(name, shape, dt))

        ps = [ctx.enter_context(nc.psum_tensor(f"bank{b}", [P, 512], F32)) for b in range(8)]
        const = {"ident": sb("ident", [P, P]), "minus_half": sb("minus_half", [P, 2]), "gain": sb("gain", [P, 4]),
                 "passed": ctx.enter_context(nc.semaphore("passed"))}
        ten = {"gates": sb("gates", [P, 2 * B, E]), "chosen": sb("chosen", [P, 2, S], BF16)}
        with ExitStack() as inner:
            def sbi(name, shape, dt=F32):
                return inner.enter_context(nc.sbuf_tensor(name, shape, dt))

            ten["V_blocks"] = [sbi(f"v_blocks{c}", [P, 2, 5 * GH * VC]) for c in range(LANES)]
            w = {f"{m}{layer}": sbi(f"w_{m}{layer}", [P, 2, DT, D], F32R) for layer in range(2) for m in "qkvo"}
            w["fc"] = sbi("w_fc", [P, 2, DT, HID0], F32R)
            w["pj"] = sbi("w_pj", [P, HT0, D], F32R)
            w["gate"] = sbi("w_gate", [P, 2, DT, E], F32R)
            const.update(
                head=sbi("head_mask", [P, GH]), rest=sbi("rest_mask", [P, GH]), bq=sbi("bq", [P, 2, DT]), bk=sbi("bk", [P, 2, DT]),
                bo=sbi("bo", [P, 2, D]), pj_scale=sbi("pj_scale", [P, D]), gate_b=sbi("gate_b", [P, E]),
                onehot=sbi("onehot", [HEADS, HEADS * PAD], F32R))
            prepare(nc, ten, ps, w, const, dram)
            layers(nc, ten, ps, w, const, dram)
        ten.update(w1=sb("w1", [P, 2, DT, E * SUB], F32R), w2=sb("w2", [P, 2, HT1, D], F32R), b1=sb("b1", [P, HT1]), b2=sb("b2", [E, 2, D], F32R),
                   pick=sb("pick", [P, 2 * P], BF16), spread=sb("spread", [P, P * SUB], BF16))
        routing(nc, ten, ps, const, dram)
        experts(nc, ten, ps, const, dram)


def kernel(**inputs):
    import numpy as np
    import concourse.bacc as bacc
    from concourse.bass_utils import run_bass_kernel_spmd as run

    def a(name):
        return np.asarray(inputs[name])

    def padded(t):
        return np.concatenate([t, t[:, :PAD - KEYS]], axis=1)

    def tokens(t):
        return t.reshape(BODIES, LANES, 2, P, D).transpose(0, 3, 1, 2, 4).reshape(BODIES, P, 2 * LANES, D)

    def columns(t):
        return t.reshape(-1, P).T

    mask = padded(a("mask_Bx1x1xS2_if1").reshape(B, KEYS))
    main = np.concatenate([mask[:, 0:MAIN]] * 2, axis=1)
    rest = np.concatenate([mask[:, MAIN:]] * GH, axis=1)
    arrays = {
        "x": tokens(a("x")),
        "ctxT": padded(a("ctx_1024")).reshape(BODIES, LANES, PAD, DT, P).transpose(0, 4, 3, 1, 2),
        "mask_row": mask.reshape(BODIES, LANES, PAD),
        "mask_col": np.stack([main, rest], axis=-1).reshape(BODIES, LANES, P, 2).transpose(0, 2, 1, 3),
        "g_xattn": a("g_xattn"), "g_ffn": a("g_ffn"), "gate": a("L0_ffn_gate").reshape(1),
        "fcT": a("L0_ffn_w_fc").T, "pjT": a("L0_ffn_w_proj").T, "fast_b": a("L0_ffn_fast_b"), "uT": a("L0_ffn_u").T, "v": a("L0_ffn_v"),
        "w_gate": a("L1_ffn_w_gate_w"), "gate_b": a("L1_ffn_w_gate_b"),
        "W1": a("L1_ffn_W1").transpose(1, 0, 2).reshape(D, E * SUB), "b1": columns(a("L1_ffn_b1").reshape(-1)),
        "W2": a("L1_ffn_W2").reshape(E * SUB, D), "b2": a("L1_ffn_b2"),
    }
    for layer in range(2):
        for m in "qkvo":
            arrays[f"L{layer}_W{m}T"] = a(f"L{layer}_xattn_W{m}").T
            bias = a(f"L{layer}_xattn_b{m}")
            arrays[f"L{layer}_b{m}"] = bias if m == "o" else columns(bias)
    nc = bacc.Bacc("TRN2", target_bir_lowering=False, num_devices=1)
    arrays = {f"in_{n}": np.ascontiguousarray(t) for n, t in arrays.items()}
    dram = {n[3:]: nc.dram_tensor(n, t.shape, mybir.dt.from_np(t.dtype), kind="ExternalInput").ap() for n, t in arrays.items()}
    dram["x3"] = nc.dram_tensor("x3_scratch", (BODIES, P, 2 * LANES, D), F32, kind="Internal").ap()
    dram["out"] = nc.dram_tensor("out_0", (BODIES, P, 2 * LANES, D), F32, kind="ExternalOutput").ap()
    program(nc, dram)
    got = run(nc, [arrays], core_ids=[0]).results[0]["out_0"]
    return got.reshape(BODIES, P, LANES, 2, D).transpose(0, 2, 3, 1, 4).reshape(B, S, D)
```
